# Optimizing a Trainium2 kernel written in Bass

```python
import numpy as np
import jax
import jax.numpy as jnp

def _softmax(x, axis=-1):
    return jax.nn.softmax(x, axis=axis)

def _gelu(x):
    return jax.nn.gelu(x, approximate=True)

def _silu(x):
    return jax.nn.silu(x)

def _sigmoid(x):
    return jax.nn.sigmoid(x)

def _layernorm(x, axis=-1, eps=1e-05):
    m = jnp.mean(x, axis=axis, keepdims=True)
    v = jnp.var(x, axis=axis, keepdims=True)
    return (x - m) / jnp.sqrt(v + eps)

def _scatter_add(tgt, idx, src, axis=0):
    return tgt.at[idx].add(src)

def _segment_sum(src, seg, n):
    return jax.ops.segment_sum(src, seg, n)
kernel_name = 'mk_xattn_ffn_d4_seqx_r8_44fffe'

def setup_inputs(seed: int=0):
    np.random.seed(seed)
    _w = jnp.asarray

    def _rec_inputs():
        import jax
        import jax.numpy as jnp
        _rk = jax.random.key(seed)
        x = 7.22e-05 + 1 * jax.random.normal(jax.random.fold_in(_rk, 1), (8, 56, 128), jnp.float32)
        _lenS = 56 - jax.random.randint(jax.random.fold_in(_rk, 7), (8,), 0, max(1, 56 // 4) + 1, jnp.int32)
        _lenS2 = 1500 - jax.random.randint(jax.random.fold_in(_rk, 8), (8,), 0, max(1, 1500 // 4) + 1, jnp.int32)
        _ctx_1024P = jax.random.normal(jax.random.fold_in(_rk, 11), (8, 16, 128), jnp.float32)
        _ctx_1024c = jax.random.dirichlet(jax.random.fold_in(_rk, 511), 0.3 * jnp.ones((16,), jnp.float32), (8, 1500))
        _ctx_1024t = jnp.einsum('bsk,bkd->bsd', _ctx_1024c, _ctx_1024P)
        _ctx_1024t = _ctx_1024t * jax.lax.rsqrt(jnp.mean(jnp.square(_ctx_1024t)) + 1e-12) * 0.953939
        ctx_1024 = 4.13588e-05 + 0.999923 * (_ctx_1024t + 0.3 * jax.random.normal(jax.random.fold_in(_rk, 611), (8, 1500, 128), jnp.float32))
        _validS = jnp.arange(56)[None, :] < _lenS[:, None]
        _validS2 = jnp.arange(1500)[None, :] < _lenS2[:, None]
        _causal = jnp.tril(jnp.ones((56, 56), dtype=bool))
        mask_1x1xSxS2_ik1 = jnp.where(jnp.broadcast_to(_validS2[0:1, None, None, :], (1, 1, 56, 1500)), 1, 0).astype(jnp.int32)
        return (x, ctx_1024, mask_1x1xSxS2_ik1)
    x, ctx_1024, mask_1x1xSxS2_ik1 = _rec_inputs()

    def _L0_xattn_setup():
        import jax, jax.numpy as jnp
        import numpy as np
        B, S, D, H = (4, 256, 128, 16)
        DK = D // H

        def _split_heads(x):
            b, s, _ = x.shape
            return x.reshape(b, s, H, DK).transpose(0, 2, 1, 3)
        key = jax.random.key(seed)
        ks = jax.random.split(key, 8)
        scale = 1.0 / np.sqrt(D)
        return {'q': jax.random.normal(ks[0], (B, S, D), jnp.float32), 'k': jax.random.normal(ks[1], (B, S, D), jnp.float32), 'v': jax.random.normal(ks[2], (B, S, D), jnp.float32), 'Wq': jax.random.normal(ks[3], (D, D), jnp.float32) * scale, 'bq': jnp.zeros((D,), jnp.float32), 'Wk': jax.random.normal(ks[4], (D, D), jnp.float32) * scale, 'bk': jnp.zeros((D,), jnp.float32), 'Wv': jax.random.normal(ks[5], (D, D), jnp.float32) * scale, 'bv': jnp.zeros((D,), jnp.float32), 'Wo': jax.random.normal(ks[6], (D, D), jnp.float32) * scale, 'bo': jnp.zeros((D,), jnp.float32)}
    _L0_xattn_all = _L0_xattn_setup()
    _L0_xattn_in = {k: v for k, v in _L0_xattn_all.items() if k in ('Wq', 'bq', 'Wk', 'bk', 'Wv', 'bv', 'Wo', 'bo')}
    del _L0_xattn_all

    def _L0_ffn_setup():
        import jax, jax.numpy as jnp
        import numpy as np
        from jax import lax
        T, B, I, M, O = (32, 64, 128, 128, 128)

        def _xavier(key, shape):
            fan_out, fan_in = shape
            limit = float(np.sqrt(6.0 / (fan_in + fan_out)))
            return jax.random.uniform(key, shape, jnp.float32, -limit, limit)
        key = jax.random.key(seed)
        ks = jax.random.split(key, 9)
        x = jax.random.normal(ks[0], (T, B, I), jnp.float32)
        return {'x': x, 'wf': _xavier(ks[1], (M, I)), 'uf': _xavier(ks[2], (M, M)), 'bf': jnp.zeros((M,), jnp.float32), 'wi': _xavier(ks[3], (M, I)), 'ui': _xavier(ks[4], (M, M)), 'bi': jnp.zeros((M,), jnp.float32), 'wc': _xavier(ks[5], (M, I)), 'uc': _xavier(ks[6], (M, M)), 'bc': jnp.zeros((M,), jnp.float32), 'wo': _xavier(ks[7], (O, I)), 'uo': _xavier(ks[8], (O, M)), 'bo': jnp.zeros((O,), jnp.float32), 'in_c': jnp.zeros((M,), jnp.float32)}
    _L0_ffn_all = _L0_ffn_setup()
    _L0_ffn_in = {k: v for k, v in _L0_ffn_all.items() if k in ('wf', 'uf', 'bf', 'wi', 'ui', 'bi', 'wc', 'uc', 'bc', 'wo', 'uo', 'bo', 'in_c')}
    del _L0_ffn_all

    def _L1_xattn_setup():
        import jax, jax.numpy as jnp
        import numpy as np
        D_MODEL = 128
        N_HEAD = 16
        D_K = D_MODEL // N_HEAD
        B, S = (2, 256)
        NEG = -1000000000.0
        key = jax.random.key(seed)
        ks = jax.random.split(key, 9)
        inp = {'input_q': jax.random.normal(ks[0], (B, S, D_MODEL), dtype=jnp.float32), 'input_k': jax.random.normal(ks[1], (B, S, D_MODEL), dtype=jnp.float32), 'input_v': jax.random.normal(ks[2], (B, S, D_MODEL), dtype=jnp.float32), 'mask': jax.random.randint(ks[3], (1, 1, S, S), 0, 2, dtype=jnp.int32), 'w_q': jax.random.normal(ks[4], (D_MODEL, D_MODEL), dtype=jnp.float32) / np.sqrt(D_MODEL), 'w_k': jax.random.normal(ks[5], (D_MODEL, D_MODEL), dtype=jnp.float32) / np.sqrt(D_MODEL), 'w_v': jax.random.normal(ks[6], (D_MODEL, D_MODEL), dtype=jnp.float32) / np.sqrt(D_MODEL), 'w_o': jax.random.normal(ks[7], (D_MODEL, D_MODEL), dtype=jnp.float32) / np.sqrt(D_MODEL), 'b_o': jax.random.normal(ks[8], (D_MODEL,), dtype=jnp.float32) * 0.01}
        return inp
    _L1_xattn_all = _L1_xattn_setup()
    _L1_xattn_in = {k: v for k, v in _L1_xattn_all.items() if k in ('w_q', 'w_k', 'w_v', 'w_o', 'b_o')}
    del _L1_xattn_all

    def _L1_ffn_setup():
        import jax, jax.numpy as jnp
        import numpy as np
        D_MODEL = 128
        D_FF = 512
        NUM_EXPERTS = 8
        TOP_K = 2
        key = jax.random.key(seed)
        ks = jax.random.split(key, 8)
        s_in = 1.0 / np.sqrt(D_MODEL)
        s_ff = 1.0 / np.sqrt(D_FF)
        x = jax.random.normal(ks[0], (2, 256, D_MODEL), dtype=jnp.float32)
        Wg = jax.random.uniform(ks[1], (D_MODEL, NUM_EXPERTS), minval=-s_in, maxval=s_in, dtype=jnp.float32)
        bg = jax.random.uniform(ks[2], (NUM_EXPERTS,), minval=-s_in, maxval=s_in, dtype=jnp.float32)
        W1 = jax.random.uniform(ks[3], (NUM_EXPERTS, D_MODEL, D_FF), minval=-s_in, maxval=s_in, dtype=jnp.float32)
        b1 = jax.random.uniform(ks[4], (NUM_EXPERTS, D_FF), minval=-s_in, maxval=s_in, dtype=jnp.float32)
        W2 = jax.random.uniform(ks[5], (NUM_EXPERTS, D_FF, D_MODEL), minval=-s_ff, maxval=s_ff, dtype=jnp.float32)
        b2 = jax.random.uniform(ks[6], (NUM_EXPERTS, D_MODEL), minval=-s_ff, maxval=s_ff, dtype=jnp.float32)
        return {'x': x, 'Wg': Wg, 'bg': bg, 'W1': W1, 'b1': b1, 'W2': W2, 'b2': b2}
    _L1_ffn_all = _L1_ffn_setup()
    _L1_ffn_in = {k: v for k, v in _L1_ffn_all.items() if k in ('Wg', 'bg', 'W1', 'b1', 'W2', 'b2')}
    del _L1_ffn_all

    def _L2_xattn_setup():
        import jax, jax.numpy as jnp
        import numpy as np
        NUM_HEADS = 16
        DIM_HIDDEN = 128
        DIM_ATTN = DIM_HIDDEN // NUM_HEADS
        SCALE = DIM_ATTN ** (-0.5)
        TOP_K = 32

        def _split_heads(x, b, s):
            return x.reshape(b, s, NUM_HEADS, DIM_ATTN).transpose(0, 2, 1, 3)
        rng = jax.random.key(seed)
        k1, k2, k3, k4, k5 = jax.random.split(rng, 5)
        b, sq, sk, d = (2, 256, 256, DIM_HIDDEN)
        lim = 1.0 / np.sqrt(d)
        return {'query': jax.random.normal(k1, (b, sq, d), jnp.float32), 'key': jax.random.normal(k2, (b, sk, d), jnp.float32), 'value': jax.random.normal(k3, (b, sk, d), jnp.float32), 'Wq': jax.random.uniform(k4, (d, d), jnp.float32, -lim, lim), 'Wk': jax.random.uniform(k5, (d, d), jnp.float32, -lim, lim)}
    _L2_xattn_all = _L2_xattn_setup()
    _L2_xattn_in = {k: v for k, v in _L2_xattn_all.items() if k in ('Wq', 'Wk')}
    del _L2_xattn_all

    def _L2_ffn_setup():
        import jax, jax.numpy as jnp
        import numpy as np
        B, L, D, H, E, K = (4, 256, 128, 256, 8, 2)

        def _mlp(x, w1, b1, w2, b2):
            h = jax.nn.gelu(x @ w1 + b1, approximate=True)
            return h @ w2 + b2
        key = jax.random.key(seed)
        ks = jax.random.split(key, 16)
        s = 0.02
        inp = {'x': jax.random.normal(ks[0], (B, L, D), dtype=jnp.float32), 'task_ids': jax.random.randint(ks[1], (B,), 0, 9), 'gw1': jax.random.normal(ks[2], (D, H), dtype=jnp.float32) * s, 'gb1': jnp.zeros((H,), dtype=jnp.float32), 'gw2': jax.random.normal(ks[3], (H, E), dtype=jnp.float32) * s, 'gb2': jnp.zeros((E,), dtype=jnp.float32), 'We1': jax.random.normal(ks[4], (E, D, H), dtype=jnp.float32) * s, 'be1': jnp.zeros((E, H), dtype=jnp.float32), 'We2': jax.random.normal(ks[5], (E, H, D), dtype=jnp.float32) * s, 'be2': jnp.zeros((E, D), dtype=jnp.float32), 'Ws1': jax.random.normal(ks[6], (D, H), dtype=jnp.float32) * s, 'bs1': jnp.zeros((H,), dtype=jnp.float32), 'Ws2': jax.random.normal(ks[7], (H, D), dtype=jnp.float32) * s, 'bs2': jnp.zeros((D,), dtype=jnp.float32)}
        return inp
    _L2_ffn_all = _L2_ffn_setup()
    _L2_ffn_in = {k: v for k, v in _L2_ffn_all.items() if k in ('task_ids', 'gw1', 'gb1', 'gw2', 'gb2', 'We1', 'be1', 'We2', 'be2', 'Ws1', 'bs1', 'Ws2', 'bs2')}
    del _L2_ffn_all

    def _L3_xattn_setup():
        import jax, jax.numpy as jnp
        import numpy as np
        DIM = 128
        HEADS = 16
        DIM_HEAD = 64
        INNER = HEADS * DIM_HEAD
        EPS = 1e-05

        def _layernorm(t, w, b):
            mu = jnp.mean(t, axis=-1, keepdims=True)
            var = jnp.mean(jnp.square(t - mu), axis=-1, keepdims=True)
            return (t - mu) * jax.lax.rsqrt(var + EPS) * w + b
        key = jax.random.key(seed)
        ks = jax.random.split(key, 8)
        b, n, l = (8, 512, 64)
        x = jax.random.normal(ks[0], (b, n, DIM), dtype=jnp.float32)
        latents = jax.random.normal(ks[1], (b, l, DIM), dtype=jnp.float32)
        ln1_w = jnp.ones((DIM,), jnp.float32)
        ln1_b = jnp.zeros((DIM,), jnp.float32)
        ln2_w = jnp.ones((DIM,), jnp.float32)
        ln2_b = jnp.zeros((DIM,), jnp.float32)
        Wq = jax.random.normal(ks[2], (DIM, INNER), dtype=jnp.float32) / np.sqrt(DIM)
        Wkv = jax.random.normal(ks[3], (DIM, 2 * INNER), dtype=jnp.float32) / np.sqrt(DIM)
        Wo = jax.random.normal(ks[4], (INNER, DIM), dtype=jnp.float32) / np.sqrt(INNER)
        return {'x': x, 'latents': latents, 'ln1_w': ln1_w, 'ln1_b': ln1_b, 'ln2_w': ln2_w, 'ln2_b': ln2_b, 'Wq': Wq, 'Wkv': Wkv, 'Wo': Wo}
    _L3_xattn_all = _L3_xattn_setup()
    _L3_xattn_in = {k: v for k, v in _L3_xattn_all.items() if k in ('ln1_w', 'ln1_b', 'ln2_w', 'ln2_b', 'Wq', 'Wkv', 'Wo')}
    del _L3_xattn_all

    def _L3_ffn_setup():
        import jax, jax.numpy as jnp
        import numpy as np
        ALPHA = 1.0
        key = jax.random.key(seed)
        ks = jax.random.split(key, 7)
        B, S, IN, OUT = (8, 1024, 128, 128)
        RANK, DDIM, UDIM = (4, 100, 50)
        return {'hidden_states': jax.random.normal(ks[0], (B, S, IN), dtype=jnp.float32), 'W': jax.random.normal(ks[1], (OUT, IN), dtype=jnp.float32) * 0.02, 'b': jax.random.normal(ks[2], (OUT,), dtype=jnp.float32) * 0.02, 'lora_down': jax.random.normal(ks[3], (RANK, DDIM), dtype=jnp.float32) * 0.1, 'lora_up': jax.random.normal(ks[4], (UDIM, RANK), dtype=jnp.float32) * 0.1, 'down_aux': jax.random.normal(ks[5], (DDIM, IN), dtype=jnp.float32) * 0.03, 'up_aux': jax.random.normal(ks[6], (OUT, UDIM), dtype=jnp.float32) * 0.03}
    _L3_ffn_all = _L3_ffn_setup()
    _L3_ffn_in = {k: v for k, v in _L3_ffn_all.items() if k in ('W', 'b', 'lora_down', 'lora_up', 'down_aux', 'up_aux')}
    del _L3_ffn_all
    return {'x': x, 'ctx_1024': ctx_1024, 'mask_1x1xSxS2_ik1': mask_1x1xSxS2_ik1, 'L0_xattn_Wq': _L0_xattn_in['Wq'], 'L0_xattn_bq': _L0_xattn_in['bq'], 'L0_xattn_Wk': _L0_xattn_in['Wk'], 'L0_xattn_bk': _L0_xattn_in['bk'], 'L0_xattn_Wv': _L0_xattn_in['Wv'], 'L0_xattn_bv': _L0_xattn_in['bv'], 'L0_xattn_Wo': _L0_xattn_in['Wo'], 'L0_xattn_bo': _L0_xattn_in['bo'], 'L0_ffn_wf': _L0_ffn_in['wf'], 'L0_ffn_uf': _L0_ffn_in['uf'], 'L0_ffn_bf': _L0_ffn_in['bf'], 'L0_ffn_wi': _L0_ffn_in['wi'], 'L0_ffn_ui': _L0_ffn_in['ui'], 'L0_ffn_bi': _L0_ffn_in['bi'], 'L0_ffn_wc': _L0_ffn_in['wc'], 'L0_ffn_uc': _L0_ffn_in['uc'], 'L0_ffn_bc': _L0_ffn_in['bc'], 'L0_ffn_wo': _L0_ffn_in['wo'], 'L0_ffn_uo': _L0_ffn_in['uo'], 'L0_ffn_bo': _L0_ffn_in['bo'], 'L0_ffn_in_c': _L0_ffn_in['in_c'], 'L1_xattn_w_q': _L1_xattn_in['w_q'], 'L1_xattn_w_k': _L1_xattn_in['w_k'], 'L1_xattn_w_v': _L1_xattn_in['w_v'], 'L1_xattn_w_o': _L1_xattn_in['w_o'], 'L1_xattn_b_o': _L1_xattn_in['b_o'], 'L1_ffn_Wg': _L1_ffn_in['Wg'], 'L1_ffn_bg': _L1_ffn_in['bg'], 'L1_ffn_W1': _L1_ffn_in['W1'], 'L1_ffn_b1': _L1_ffn_in['b1'], 'L1_ffn_W2': _L1_ffn_in['W2'], 'L1_ffn_b2': _L1_ffn_in['b2'], 'L2_xattn_Wq': _L2_xattn_in['Wq'], 'L2_xattn_Wk': _L2_xattn_in['Wk'], 'L2_ffn_task_ids': _L2_ffn_in['task_ids'], 'L2_ffn_gw1': _L2_ffn_in['gw1'], 'L2_ffn_gb1': _L2_ffn_in['gb1'], 'L2_ffn_gw2': _L2_ffn_in['gw2'], 'L2_ffn_gb2': _L2_ffn_in['gb2'], 'L2_ffn_We1': _L2_ffn_in['We1'], 'L2_ffn_be1': _L2_ffn_in['be1'], 'L2_ffn_We2': _L2_ffn_in['We2'], 'L2_ffn_be2': _L2_ffn_in['be2'], 'L2_ffn_Ws1': _L2_ffn_in['Ws1'], 'L2_ffn_bs1': _L2_ffn_in['bs1'], 'L2_ffn_Ws2': _L2_ffn_in['Ws2'], 'L2_ffn_bs2': _L2_ffn_in['bs2'], 'L3_xattn_ln1_w': _L3_xattn_in['ln1_w'], 'L3_xattn_ln1_b': _L3_xattn_in['ln1_b'], 'L3_xattn_ln2_w': _L3_xattn_in['ln2_w'], 'L3_xattn_ln2_b': _L3_xattn_in['ln2_b'], 'L3_xattn_Wq': _L3_xattn_in['Wq'], 'L3_xattn_Wkv': _L3_xattn_in['Wkv'], 'L3_xattn_Wo': _L3_xattn_in['Wo'], 'L3_ffn_W': _L3_ffn_in['W'], 'L3_ffn_b': _L3_ffn_in['b'], 'L3_ffn_lora_down': _L3_ffn_in['lora_down'], 'L3_ffn_lora_up': _L3_ffn_in['lora_up'], 'L3_ffn_down_aux': _L3_ffn_in['down_aux'], 'L3_ffn_up_aux': _L3_ffn_in['up_aux']}

def reference(x, ctx_1024, mask_1x1xSxS2_ik1, L0_xattn_Wq, L0_xattn_bq, L0_xattn_Wk, L0_xattn_bk, L0_xattn_Wv, L0_xattn_bv, L0_xattn_Wo, L0_xattn_bo, L0_ffn_wf, L0_ffn_uf, L0_ffn_bf, L0_ffn_wi, L0_ffn_ui, L0_ffn_bi, L0_ffn_wc, L0_ffn_uc, L0_ffn_bc, L0_ffn_wo, L0_ffn_uo, L0_ffn_bo, L0_ffn_in_c, L1_xattn_w_q, L1_xattn_w_k, L1_xattn_w_v, L1_xattn_w_o, L1_xattn_b_o, L1_ffn_Wg, L1_ffn_bg, L1_ffn_W1, L1_ffn_b1, L1_ffn_W2, L1_ffn_b2, L2_xattn_Wq, L2_xattn_Wk, L2_ffn_task_ids, L2_ffn_gw1, L2_ffn_gb1, L2_ffn_gw2, L2_ffn_gb2, L2_ffn_We1, L2_ffn_be1, L2_ffn_We2, L2_ffn_be2, L2_ffn_Ws1, L2_ffn_bs1, L2_ffn_Ws2, L2_ffn_bs2, L3_xattn_ln1_w, L3_xattn_ln1_b, L3_xattn_ln2_w, L3_xattn_ln2_b, L3_xattn_Wq, L3_xattn_Wkv, L3_xattn_Wo, L3_ffn_W, L3_ffn_b, L3_ffn_lora_down, L3_ffn_lora_up, L3_ffn_down_aux, L3_ffn_up_aux):
    import jax
    import jax.numpy as jnp

    def _L0_xattn_ref(q, k, v, Wq, bq, Wk, bk, Wv, bv, Wo, bo):
        import jax, jax.numpy as jnp
        import numpy as np
        B, S, D, H = (4, 256, 128, 16)
        DK = D // H

        def _split_heads(x):
            b, s, _ = x.shape
            return x.reshape(b, s, H, DK).transpose(0, 2, 1, 3)
        Q = _split_heads(q @ Wq + bq)
        K = _split_heads(k @ Wk + bk)
        V = _split_heads(v @ Wv + bv)
        scores = jnp.einsum('bhqd,bhkd->bhqk', Q, K)
        weights = jax.nn.softmax(scores, axis=-1)
        x = jnp.einsum('bhqk,bhkd->bhqd', weights, V)
        x = x.transpose(0, 2, 1, 3).reshape(q.shape[0], -1, D)
        return x @ Wo + bo

    def _L0_ffn_ref(x, wf, uf, bf, wi, ui, bi, wc, uc, bc, wo, uo, bo, in_c):
        import jax, jax.numpy as jnp
        import numpy as np
        from jax import lax
        T, B, I, M, O = (32, 64, 128, 128, 128)

        def _xavier(key, shape):
            fan_out, fan_in = shape
            limit = float(np.sqrt(6.0 / (fan_in + fan_out)))
            return jax.random.uniform(key, shape, jnp.float32, -limit, limit)
        batch = x.shape[1]
        c0 = jnp.broadcast_to(in_c, (batch, in_c.shape[0]))

        def step(c, xt):
            ft = jax.nn.sigmoid(xt @ wf.T + c @ uf.T + bf)
            it = jax.nn.sigmoid(xt @ wi.T + c @ ui.T + bi)
            gt = jnp.tanh(xt @ wc.T + c @ uc.T + bc)
            c = ft * c + it * gt
            return (c, None)
        c_final, _ = lax.scan(step, c0, x)
        h = jnp.tanh(jnp.einsum('tbi,oi->tbo', x, wo) + c_final @ uo.T + bo)
        return h

    def _L1_xattn_ref(input_q, input_k, input_v, mask, w_q, w_k, w_v, w_o, b_o):
        import jax, jax.numpy as jnp
        import numpy as np
        D_MODEL = 128
        N_HEAD = 16
        D_K = D_MODEL // N_HEAD
        B, S = (2, 256)
        NEG = -1000000000.0
        b = input_q.shape[0]

        def split_heads(x):
            return x.reshape(b, -1, N_HEAD, D_K).transpose(0, 2, 1, 3)
        q = split_heads(input_q @ w_q)
        k = split_heads(input_k @ w_k)
        v = split_heads(input_v @ w_v)
        scores = jnp.einsum('bhqd,bhkd->bhqk', q, k) / jnp.sqrt(jnp.float32(D_K))
        scores = jnp.where(mask == 0, jnp.float32(NEG), scores)
        attn = jax.nn.softmax(scores, axis=-1)
        per_head = jnp.einsum('bhqk,bhkd->bhqd', attn, v)
        concat = per_head.transpose(0, 2, 1, 3).reshape(b, -1, N_HEAD * D_K)
        return concat @ w_o + b_o

    def _L1_ffn_ref(x, Wg, bg, W1, b1, W2, b2):
        import jax, jax.numpy as jnp
        import numpy as np
        D_MODEL = 128
        D_FF = 512
        NUM_EXPERTS = 8
        TOP_K = 2
        gate_logits = jnp.einsum('bsd,de->bse', x, Wg) + bg
        gate_probs = jax.nn.softmax(gate_logits, axis=-1)
        topk_probs, topk_idx = jax.lax.top_k(gate_probs, TOP_K)
        topk_probs = topk_probs / jnp.sum(topk_probs, axis=-1, keepdims=True)
        onehot = jax.nn.one_hot(topk_idx, NUM_EXPERTS, dtype=x.dtype)
        weights = jnp.einsum('bske,bsk->bse', onehot, topk_probs)
        h = jnp.einsum('bsd,edf->bsef', x, W1) + b1
        h = jax.nn.gelu(h, approximate=False)
        y = jnp.einsum('bsef,efd->bsed', h, W2) + b2
        return jnp.einsum('bsed,bse->bsd', y, weights)

    def _L2_xattn_ref(query, key, value, Wq, Wk):
        import jax, jax.numpy as jnp
        import numpy as np
        NUM_HEADS = 16
        DIM_HIDDEN = 128
        DIM_ATTN = DIM_HIDDEN // NUM_HEADS
        SCALE = DIM_ATTN ** (-0.5)
        TOP_K = 32

        def _split_heads(x, b, s):
            return x.reshape(b, s, NUM_HEADS, DIM_ATTN).transpose(0, 2, 1, 3)
        b, sq, d = query.shape
        sk = key.shape[1]
        q = _split_heads(query @ Wq.T, b, sq)
        k = _split_heads(key @ Wk.T, b, sk)
        v = _split_heads(value, b, sk)
        scores = jnp.einsum('bhqa,bhka->bhqk', q, k) * SCALE
        top_vals = jax.lax.top_k(scores, TOP_K)[0]
        cutoff = top_vals[..., -1:]
        masked = jnp.where(scores >= cutoff, scores, -jnp.inf)
        w = jax.nn.softmax(masked, axis=-1)
        e = jnp.einsum('bhqk,bhka->bhqa', w, v)
        return e.transpose(0, 2, 1, 3).reshape(b, sq, d)

    def _L2_ffn_ref(x, task_ids, gw1, gb1, gw2, gb2, We1, be1, We2, be2, Ws1, bs1, Ws2, bs2):
        import jax, jax.numpy as jnp
        import numpy as np
        B, L, D, H, E, K = (4, 256, 128, 256, 8, 2)

        def _mlp(x, w1, b1, w2, b2):
            h = jax.nn.gelu(x @ w1 + b1, approximate=True)
            return h @ w2 + b2
        bsz, length, d = x.shape
        T = bsz * length
        xf = x.reshape(T, d)
        logits = jax.nn.gelu(xf @ gw1 + gb1, approximate=False) @ gw2 + gb2
        scores = jax.nn.softmax(logits, axis=-1)
        topk_w, topk_idx = jax.lax.top_k(scores, K)
        rows = jnp.arange(T)[:, None]
        gates = jnp.zeros_like(scores).at[rows, topk_idx].set(topk_w)
        out = _mlp(xf, Ws1, bs1, Ws2, bs2)
        for e in range(E):
            out = out + gates[:, e:e + 1] * _mlp(xf, We1[e], be1[e], We2[e], be2[e])
        return out.reshape(bsz, length, d)

    def _L3_xattn_ref(x, latents, ln1_w, ln1_b, ln2_w, ln2_b, Wq, Wkv, Wo):
        import jax, jax.numpy as jnp
        import numpy as np
        DIM = 128
        HEADS = 16
        DIM_HEAD = 64
        INNER = HEADS * DIM_HEAD
        EPS = 1e-05

        def _layernorm(t, w, b):
            mu = jnp.mean(t, axis=-1, keepdims=True)
            var = jnp.mean(jnp.square(t - mu), axis=-1, keepdims=True)
            return (t - mu) * jax.lax.rsqrt(var + EPS) * w + b
        xn = _layernorm(x, ln1_w, ln1_b)
        latn = _layernorm(latents, ln2_w, ln2_b)
        b, l, _ = latn.shape
        q = latn @ Wq
        kv_input = jnp.concatenate([xn, latn], axis=1)
        kv = kv_input @ Wkv
        k, v = jnp.split(kv, 2, axis=-1)

        def heads(t):
            return t.reshape(t.shape[0], t.shape[1], HEADS, DIM_HEAD).transpose(0, 2, 1, 3)
        q, k, v = (heads(q), heads(k), heads(v))
        scale = 1.0 / np.sqrt(np.sqrt(DIM_HEAD))
        weight = jnp.einsum('bhld,bhnd->bhln', q * scale, k * scale)
        weight = jax.nn.softmax(weight.astype(jnp.float32), axis=-1).astype(weight.dtype)
        out = jnp.einsum('bhln,bhnd->bhld', weight, v)
        out = out.transpose(0, 2, 1, 3).reshape(b, l, INNER)
        return out @ Wo

    def _L3_ffn_ref(hidden_states, W, b, lora_down, lora_up, down_aux, up_aux):
        import jax, jax.numpy as jnp
        import numpy as np
        ALPHA = 1.0
        lilora_weight = up_aux @ (lora_up @ (lora_down @ down_aux))
        base = jnp.einsum('bsi,oi->bso', hidden_states, W) + b
        delta = jnp.einsum('bsi,oi->bso', hidden_states, lilora_weight)
        return base + ALPHA * delta
    x = x + _L0_xattn_ref(_layernorm(x, axis=-1), ctx_1024, ctx_1024, L0_xattn_Wq, L0_xattn_bq, L0_xattn_Wk, L0_xattn_bk, L0_xattn_Wv, L0_xattn_bv, L0_xattn_Wo, L0_xattn_bo)
    x = x + _L0_ffn_ref(_layernorm(x, axis=-1), L0_ffn_wf, L0_ffn_uf, L0_ffn_bf, L0_ffn_wi, L0_ffn_ui, L0_ffn_bi, L0_ffn_wc, L0_ffn_uc, L0_ffn_bc, L0_ffn_wo, L0_ffn_uo, L0_ffn_bo, L0_ffn_in_c)
    x = x + _L1_xattn_ref(_layernorm(x, axis=-1), ctx_1024, ctx_1024, mask_1x1xSxS2_ik1, L1_xattn_w_q, L1_xattn_w_k, L1_xattn_w_v, L1_xattn_w_o, L1_xattn_b_o)
    x = x + _L1_ffn_ref(_layernorm(x, axis=-1), L1_ffn_Wg, L1_ffn_bg, L1_ffn_W1, L1_ffn_b1, L1_ffn_W2, L1_ffn_b2)
    x = x + _L2_xattn_ref(_layernorm(x, axis=-1), ctx_1024, ctx_1024, L2_xattn_Wq, L2_xattn_Wk)
    x = x + _L2_ffn_ref(_layernorm(x, axis=-1), L2_ffn_task_ids, L2_ffn_gw1, L2_ffn_gb1, L2_ffn_gw2, L2_ffn_gb2, L2_ffn_We1, L2_ffn_be1, L2_ffn_We2, L2_ffn_be2, L2_ffn_Ws1, L2_ffn_bs1, L2_ffn_Ws2, L2_ffn_bs2)
    x = x + _L3_xattn_ref(ctx_1024, _layernorm(x, axis=-1), L3_xattn_ln1_w, L3_xattn_ln1_b, L3_xattn_ln2_w, L3_xattn_ln2_b, L3_xattn_Wq, L3_xattn_Wkv, L3_xattn_Wo)
    x = x + _L3_ffn_ref(_layernorm(x, axis=-1), L3_ffn_W, L3_ffn_b, L3_ffn_lora_down, L3_ffn_lora_up, L3_ffn_down_aux, L3_ffn_up_aux)
    return x

_drawn_inputs = setup_inputs


def setup_inputs(seed=0):
    import zlib

    import numpy as np

    out = dict(_drawn_inputs(seed))
    spreads = {'L0_xattn_bq': (0.0, 0.1),
     'L0_xattn_bk': (0.0, 2.0),
     'L0_xattn_bv': (0.0, 0.1),
     'L0_xattn_bo': (0.0, 0.1),
     'L0_ffn_bf': (0.0, 0.561),
     'L0_ffn_bi': (0.0, 0.462),
     'L0_ffn_bc': (0.0, 0.1),
     'L0_ffn_bo': (0.0, 0.1),
     'L0_ffn_in_c': (0.0, 0.649),
     'L2_ffn_gb1': (0.0, 0.8),
     'L2_ffn_gb2': (0.0, 0.645),
     'L2_ffn_be1': (0.0, 0.8),
     'L2_ffn_be2': (0.0, 0.756),
     'L2_ffn_bs1': (0.0, 0.8),
     'L2_ffn_bs2': (0.0, 0.1),
     'L3_xattn_ln1_w': (1.0, 0.2),
     'L3_xattn_ln1_b': (0.0, 0.384),
     'L3_xattn_ln2_w': (1.0, 0.6),
     'L3_xattn_ln2_b': (0.0, 0.612)}
    factors = {'L1_xattn_b_o': 4.679,
     'L1_ffn_b1': 4.4,
     'L1_ffn_b2': 3.526,
     'L2_ffn_gw1': 8.0,
     'L2_ffn_gw2': 8.0,
     'L2_ffn_We1': 8.0,
     'L2_ffn_We2': 8.0,
     'L2_ffn_Ws1': 2.804,
     'L3_ffn_b': 43.312,
     'L3_ffn_lora_down': 6.915,
     'L3_ffn_lora_up': 7.961,
     'L3_ffn_down_aux': 6.145,
     'L3_ffn_up_aux': 7.229,
     'L3_ffn_W': 8.0}
    for name, (base, spread) in spreads.items():
        noise = np.random.default_rng([zlib.crc32(name.encode()), seed]).standard_normal(out[name].shape)
        drawn = base * np.exp(spread * noise) if base else spread * noise
        out[name] = jnp.asarray(drawn.astype(out[name].dtype))
    for name, factor in factors.items():
        out[name] = (out[name] * factor).astype(out[name].dtype)
    return out
```

```python
from contextlib import ExitStack

import concourse.bass as bass
from concourse import mybir

F32 = mybir.dt.float32
I32 = mybir.dt.int32
U32 = mybir.dt.uint32
ALU = mybir.AluOpType
ACT = mybir.ActivationFunctionType
X_AX = mybir.AxisListType.X
XY_AX = mybir.AxisListType.XY

NB, NQ, D = 8, 56, 128
T = NB * NQ
NK = 1500
CH, CK = 12, 125
NH, DH = 16, 8
PAIRS = NH // 2
HQ = 64
DH3 = 64
NK3 = NK + NQ
EPS = 1e-5
NEXP = 8
FF1, FF2 = 512, 256
TOPK = 32
NEG = -1.0e9
LOWEST = -3.0e38
SCALES = [1.0, 8.0 ** -0.5, 8.0 ** -0.5, 0.125]
PRIME = 1
GRP = 4


def groups(chunks):
    return [list(range(g, min(g + GRP, chunks))) for g in range(0, chunks, GRP)]


def moe_blocks(which):
    return [(e, k) for e in range(NEXP + which) for k in range(blocks_per(which))]


def blocks_per(which):
    return (FF1, FF2)[which] // 128


def megakernel(nc, A, scratch, out):
    ctx = ExitStack()
    with ctx:
        def sb(name, shape, dt=F32):
            return ctx.enter_context(nc.sbuf_tensor(name, shape, dt))

        sems = {}

        def S(name):
            if name not in sems:
                sems[name] = ctx.enter_context(nc.semaphore(name))
            return sems[name]

        X = sb("X", [NQ, NB, D])
        XN = sb("XN", [NQ, NB, D])
        XN2 = sb("XN2", [NQ, NB, D])
        XNT = sb("XNT", [D, T])
        ident = sb("ident", [128, 128])
        hmask = sb("hmask", [128, NH])
        pmask = sb("pmask", [128, 2])
        sel = sb("sel", [128, NQ])
        ones = sb("ones", [128, 128])
        esel = sb("esel", [NEXP, NEXP, 128])
        iota8 = sb("iota8", [NQ, NEXP])
        epst = sb("epst", [128, 1])
        st = sb("st", [NQ, NB, 6])
        mv = sb("mv", [NQ, NB, 2])
        std = sb("std", [NQ, NB])
        rstd = sb("rstd", [NQ, NB])

        wq = [sb(f"wq{i}", [D, D]) for i in range(2)]
        wk = [sb(f"wk{i}", [D, D]) for i in range(2)]
        wv = [sb(f"wv{i}", [D, D]) for i in range(2)]
        wo = [sb(f"wo{i}", [D, D]) for i in range(2)]
        COLS = ["bq", "bk", "bf", "bi", "bc", "in_c", "w1", "b1", "w2", "b2"]
        col = sb("col", [D, len(COLS)])
        colat = {n: col[:, i:i + 1] for i, n in enumerate(COLS)}
        rows = sb("rows", [1, 5, D])
        rbv, rbo0, rbos, rbo1, rb3 = (rows[:, i, :] for i in range(5))
        grow = sb("grow", [1, 2, NEXP])
        RAW = sb("RAW", [D, 14, D])
        TW = sb("TW", [D, 14, D])
        big = sb("big", [128, 8192])
        w1a = big[:, 0:4096].rearrange("p (e f) -> p e f", e=NEXP)
        w2a = big[:, 4096:8192].rearrange("p (e k d) -> p e k d", e=NEXP, k=4)
        w1b = big[:, 0:2304].rearrange("p (e f) -> p e f", e=9)
        w2b = big[:, 2304:4608].rearrange("p (e k d) -> p e k d", e=9, k=2)
        gw1 = big[:, 4608:4864]
        bcol = sb("bcol", [128, 52])
        b1a = bcol[:, 0:32]
        b1b = bcol[:, 32:50]
        gb1 = bcol[:, 50:52]
        wg1 = sb("wg1", [D, NEXP])
        gw2 = sb("gw2", [128, 2, NEXP])
        b2a = sb("b2a", [NEXP, D])
        b2b = sb("b2b", [NEXP, D])
        bs2 = sb("bs2", [1, D])
        w1B = sb("w1B", [128, D])
        b1B = sb("b1B", [128, D])
        w2B = sb("w2B", [NQ, D])
        b2B = sb("b2B", [NQ, D])
        lo = sb("lo", [128, 512])
        ld_, lu_ = lo[0:4, 0:100], lo[0:50, 100:104]
        ua_, da_ = lo[:, 104:154], lo[0:100, 154:282]
        lot = sb("lot", [128, 1024])
        ldT, luT, uaT = lot[0:100, 0:4], lot[0:4, 4:54], lot[0:50, 128:256]
        t1_, t2_, lwT = lot[0:4, 256:384], lot[0:50, 384:512], lot[:, 512:640]

        NAT = sb("NAT", [CK, CH, D])
        CT = sb("CT", [D, NK])
        KT = sb("KT", [D, NK3])
        V = sb("V", [128, CH + 1, D])
        QT = sb("QT", [D, T])
        QB = sb("QB", [D, NH, HQ])
        P = sb("P", [128, 2, NK3])
        E = sb("E", [128, NK])
        W = sb("W", [128, NK])
        PT = sb("PT", [128, 2, CH + 1, 128])
        MB = W
        MR = CT.bitcast(I32)
        AO = sb("AO", [128, PAIRS, 128])
        AT = sb("AT", [128, PAIRS, 128])
        Z = AO[:, 0, :]
        ZT = AT[:, 0, :]
        cstat = sb("cstat", [CK, CH, 6])
        cmv = sb("cmv", [CK, NB * CH, 2])
        cmvb = sb("cmvb", [CK, CH, 2])
        crs = sb("crs", [CK, NB * CH])
        rm = sb("rm", [128, PAIRS])
        nb = sb("nb", [128, PAIRS])
        den = sb("den", [128, PAIRS])
        rden = sb("rden", [128, PAIRS])
        rdm = sb("rdm", [128, PAIRS, 2])
        m8 = sb("m8", [128, TOPK])
        Q3 = sb("Q3", [D, NH, T])
        G3 = big[:, 0:2048].rearrange("p (h d) -> p h d", h=NH)
        M3 = big[:, 2048:4096].rearrange("p (h d) -> p h d", h=NH)
        W3r = big[:, 4096:8192]
        W3T = Q3[:, :, :].rearrange("p h t -> p (h t)")
        wo3 = sb("wo3", [128, PAIRS, D])
        LT = sb("LT", [D, T])
        LN_ = sb("LN_", [NQ, NB, D])

        H = V[:, :, :].rearrange("p c d -> p (c d)")[:, 0:3 * T].rearrange("p (r t) -> p r t", r=3)
        HG = KT[:, 0:3 * T].rearrange("p (r t) -> p r t", r=3)
        GH = E[:, 0:2 * T].rearrange("p (r t) -> p r t", r=2)
        lg = sb("lg", [NQ, NB, NEXP])
        top = sb("top", [NQ, NB, 8])
        tidx = sb("tidx", [NQ, NB, 8], U32)
        tif = sb("tif", [NQ, NB, 2])
        ex = sb("ex", [NQ, NB, NEXP])
        dl = sb("dl", [NQ, NB, NEXP])
        sm = sb("sm", [NQ, NB])
        wt = sb("wt", [NQ, NB, 2])
        gt = sb("gt", [NQ, NB, NEXP])
        gt2 = sb("gt2", [NQ, NB, NEXP])
        GT = sb("GT", [NEXP, T])
        YT = sb("YT", [D, T])
        cst = sb("cst", [D, 2, NQ])
        gates = sb("gates", [D, 3, NQ])
        gtmp = sb("gtmp", [D, 2, NQ])

        PS = ctx.enter_context(nc.psum_tensor("PS", [128, 4, 512], F32))
        TR = ctx.enter_context(nc.psum_tensor("TR", [128, 2, 512], F32))
        PO = ctx.enter_context(nc.psum_tensor("PO", [128, 512], F32))
        PM = ctx.enter_context(nc.psum_tensor("PM", [128, 512], F32))

        RAWS = ["L0_ffn_wf", "L0_ffn_uf", "L0_ffn_wi", "L0_ffn_ui", "L0_ffn_wc", "L0_ffn_uc",
                "L0_ffn_wo", "L0_ffn_uo", "L2_xattn_Wq", "L2_xattn_Wk", "L3_ffn_W"]
        tw = {n: TW[:, i, :] for i, n in enumerate(RAWS)}
        WQ = [wq[0][:, :], wq[1][:, :], tw["L2_xattn_Wq"]]
        WK = [wk[0][:, :], wk[1][:, :], tw["L2_xattn_Wk"]]

        def row(ap):
            return ap.rearrange("(a n) -> a n", a=1)

        def column(ap):
            return ap.rearrange("(n a) -> n a", a=1)

        def stand(eng, sem, value):
            eng.wait_ge(sem, value)
            eng.sem_inc(S("turns"), 1)

        block = ctx.enter_context(nc.Block())
        IN_ORDER = ["attn0", "scan", "attn1", "moe1", "attn2", "moe2", "attn3", "lora"]

        @block.sync
        def _(sp):
            sp.dma_start(X[:, :, :], A["x"].rearrange("b q d -> q b d")).then_inc(S("x_in"), 16)
            for layer in range(4):
                if layer == 1:
                    sp.wait_ge(S("ct_saved"), 16 * NB + 16)
                    sp.wait_ge(S("tail0"), NB + PRIME)
                    for half in range(2):
                        sp.dma_start(MR[HQ * half:HQ * half + NQ, :],
                                     A["mask_1x1xSxS2_ik1"][0, 0, :, :]).then_inc(S("mask_in"), 16)
                with sp.Fori(0, NB) as b:
                    if layer in (0, 2, 3):
                        if layer == 3:
                            stand(sp, S("v3_ready"), 3 * b + PRIME)
                            stand(sp, S("k_ready3"), b + PRIME)
                        else:
                            stand(sp, S(f"nat_used{layer}"), b + PRIME)
                        if layer:
                            sp.wait_ge(S(f"nat_used{[0, 0, 0, 2][layer]}"), NB + PRIME)
                        sp.dma_start(NAT[:, :, :], A["ctx_1024"][bass.ds(b, 1), :, :].rearrange(
                            "a (p c) d -> p (a c) d", c=CH)).then_inc(S(f"nat_in{layer}"), 16)
                    if layer in (1, 2):
                        sp.wait_ge(S("mask_made"), 1)
                        if layer == 2:
                            sp.wait_ge(S("ct_used1"), NB + PRIME)
                        stand(sp, S(f"ct_used{layer}"), b + PRIME)
                        sp.dma_start(CT[:, :], scratch[bass.ds(b, 1), :, :].rearrange(
                            "a p n -> p (a n)")).then_inc(S(f"ct_in{layer}"), 16)
                    if layer == 0:
                        stand(sp, S("ct_made"), (b + 1) * 3)
                        sp.dma_start(scratch[bass.ds(b, 1), :, :].rearrange("a p n -> p (a n)"),
                                     CT[:, :]).then_inc(S("ct_saved"), 16)
            sp.wait_ge(S("x_final"), 1)
            sp.dma_start(out.rearrange("b q d -> q b d"), X[:, :, :]).then_inc(S("out_saved"), 16)
            sp.wait_ge(S("out_saved"), 16)
            sp.wait_ge(S("ct_saved"), 16 * NB + 16)

        @block.gpsimd
        def _(pool):
            n = [0]

            def link(ins):
                n[0] += 1
                ins.then_inc(S("pool_step"), 1)
                pool.wait_ge(S("pool_step"), n[0])

            for name in (["nat_used0", "nat_used2", "v3_ready", "k_ready3", "ct_used1", "ct_used2", "v_done"]
                         + [f"k_ready{i}" for i in range(3)]
                         + [f"{a}{i}" for a in ("tail", "p_ready", "tr_used") for i in range(4)]):
                pool.sem_inc(S(name), PRIME)
            pool.sem_inc(S("ct_saved"), 16)

            link(pool.memset(ident[:, :], 0.0))
            link(pool.memset(ones[:, :], 1.0))
            link(pool.memset(esel[:, :, :], 0.0))
            link(pool.memset(epst[:, :], EPS))
            link(pool.memset(QB[:, :, :], 0.0))
            link(pool.memset(hmask[:, :], 1.0))
            link(pool.memset(pmask[:, :], 1.0))
            link(pool.affine_select(out=ident[:, :], in_=ident[:, :], compare_op=ALU.not_equal, fill=1.0,
                                    base=0, pattern=[[-1, 128]], channel_multiplier=1))
            link(pool.affine_select(out=esel[:, :, :], in_=esel[:, :, :], compare_op=ALU.not_equal, fill=1.0,
                                    base=0, pattern=[[-1, NEXP], [0, 128]], channel_multiplier=1))
            for m, w, k in ((hmask, DH, NH), (pmask, HQ, 2)):
                link(pool.affine_select(out=m[:, :], in_=m[:, :], compare_op=ALU.is_ge, fill=0.0,
                                        base=0, pattern=[[-w, k]], channel_multiplier=1))
                link(pool.affine_select(out=m[:, :], in_=m[:, :], compare_op=ALU.is_ge, fill=0.0,
                                        base=w - 1, pattern=[[w, k]], channel_multiplier=-1))
            link(pool.iota(iota8[:, :], pattern=[[1, NEXP]], base=0, channel_multiplier=0,
                           allow_small_or_imprecise_dtypes=True))
            pool.tensor_tensor(sel[:, :], ident[:, 0:NQ], ident[:, HQ:HQ + NQ], ALU.add).then_inc(S("const"), 1)

            def load(dst, src, name):
                pool.dma_start(dst, src, allow_slow_non_contiguous=True).then_inc(S(name), 16)

            for i, nme in enumerate(("Wq", "Wk", "Wv", "Wo")):
                load((wq, wk, wv, wo)[i][0][:, :], A[f"L0_xattn_{nme}"], "w_l0")
            load(colat["bq"], column(A["L0_xattn_bq"]), "w_l0")
            load(colat["bk"], column(A["L0_xattn_bk"]), "w_l0")
            load(rbv, row(A["L0_xattn_bv"]), "w_l0")
            load(rbo0, row(A["L0_xattn_bo"]), "w_l0")
            for i, nme in enumerate(RAWS):
                load(RAW[:, i, :], A[nme], "w_raw")
            for a in ("bf", "bi", "bc", "in_c"):
                load(colat[a], column(A[f"L0_ffn_{a}"]), "w_col")
            for a in ("w1", "b1", "w2", "b2"):
                load(colat[a], column(A[f"L3_xattn_ln{a[1]}_{a[0]}"]), "w_col")
            load(rbos, row(A["L0_ffn_bo"]), "w_col")
            load(rbo1, row(A["L1_xattn_b_o"]), "w_col")
            load(rb3, row(A["L3_ffn_b"]), "w_col")
            for i, nme in enumerate(("w_q", "w_k", "w_v", "w_o")):
                load((wq, wk, wv, wo)[i][1][:, :], A[f"L1_xattn_{nme}"], "w_l1")
            load(w1a, A["L1_ffn_W1"].rearrange("e p f -> p e f"), "w_moe1")
            load(w2a, A["L1_ffn_W2"].rearrange("e (k p) d -> p e k d", p=128), "w_moe1")
            load(b1a, A["L1_ffn_b1"].rearrange("e (k p) -> p (e k)", p=128), "w_moe1")
            load(wg1[:, :], A["L1_ffn_Wg"], "w_moe1")
            load(grow[:, 0, :], row(A["L1_ffn_bg"]), "w_moe1")
            load(b2a[:, :], A["L1_ffn_b2"], "w_moe1")
            load(b1b[:, 0:16], A["L2_ffn_be1"].rearrange("e (k p) -> p (e k)", p=128), "w_moe2")
            load(b1b[:, 16:18], A["L2_ffn_bs1"].rearrange("(k p) -> p k", p=128), "w_moe2")
            load(gb1, A["L2_ffn_gb1"].rearrange("(k p) -> p k", p=128), "w_moe2")
            load(gw2[:, :, :], A["L2_ffn_gw2"].rearrange("(k p) e -> p k e", p=128), "w_moe2")
            load(grow[:, 1, :], row(A["L2_ffn_gb2"]), "w_moe2")
            load(b2b[:, :], A["L2_ffn_be2"], "w_moe2")
            load(bs2[:, :], row(A["L2_ffn_bs2"]), "w_moe2")
            load(wo3[:, :, :], A["L3_xattn_Wo"].rearrange("(j p) d -> p j d", p=128), "w_l3s")
            for dst, src, k in ((w1B, "ln1_w", 128), (b1B, "ln1_b", 128), (w2B, "ln2_w", NQ), (b2B, "ln2_b", NQ)):
                load(dst[:, :], A[f"L3_xattn_{src}"].partition_broadcast(k), "w_l3s")
            for dst, src in ((ld_, "lora_down"), (lu_, "lora_up"), (da_, "down_aux"), (ua_, "up_aux")):
                load(dst, A[f"L3_ffn_{src}"], "w_lora")
            pool.wait_ge(S("moe_done"), 1)
            load(w1b[:, 0:8, :], A["L2_ffn_We1"].rearrange("e p f -> p e f"), "w_moe2")
            load(w1b[:, 8, :], A["L2_ffn_Ws1"], "w_moe2")
            load(w2b[:, 0:8, :, :], A["L2_ffn_We2"].rearrange("e (k p) d -> p e k d", p=128), "w_moe2")
            load(w2b[:, 8, :, :], A["L2_ffn_Ws2"].rearrange("(k p) d -> p k d", p=128), "w_moe2")
            load(gw1, A["L2_ffn_gw1"], "w_moe2")
            with pool.Fori(0, NB) as b:
                pool.wait_ge(S("nat_in2"), 16 * (b + 1))
                stand(pool, S("tail2"), b + 0 + PRIME)
                pool.tensor_copy(V[0:CK, 0:CH, :], NAT[:, :, :]).then_inc(S("nat_used2"), 1)
            pool.wait_ge(S("moe_done"), 2)
            load(W3r[:, 0:1024], A["L3_xattn_Wq"], "w_l3")
            load(W3r[:, 1024:3072], A["L3_xattn_Wkv"], "w_l3")
            pool.wait_ge(S("w_l3s"), 16 * 5)
            pool.wait_ge(S("xn_ready"), 8)
            link(pool.tensor_tensor(LN_[:, :, :], XN2[:, :, :],
                                    w2B[:, :].rearrange("p (a d) -> p a d", a=1).to_broadcast([NQ, NB, D]), ALU.mult))
            link(pool.tensor_tensor(LN_[:, :, :], LN_[:, :, :],
                                    b2B[:, :].rearrange("p (a d) -> p a d", a=1).to_broadcast([NQ, NB, D]), ALU.add))
            base = n[0]
            pool.wait_ge(S("lat_t"), 1)
            with pool.Fori(0, NB) as b:
                stand(pool, S("tail3"), b + 0 + PRIME)
                pool.tensor_copy(KT[:, NK:NK3], LT[:, bass.ds(b * NQ, NQ)]).then_inc(S("v3_ready"), 1)
                pool.tensor_copy(V[0:NQ, CH, :], LN_[:, bass.ds(b, 1), :].rearrange("p a d -> p (a d)"))\
                    .then_inc(S("v3_ready"), 1)
                pool.wait_ge(S("cn_ready"), b + 1)
                pool.tensor_tensor(V[0:CK, 0:CH, :], NAT[:, :, :],
                                   w1B[0:CK, :].rearrange("p (a d) -> p a d", a=1).to_broadcast([CK, CH, D]),
                                   ALU.mult).then_inc(S("pool_step"), 1)
                pool.wait_ge(S("pool_step"), b * 1 + base + 1)
                pool.tensor_tensor(V[0:CK, 0:CH, :], V[0:CK, 0:CH, :],
                                   b1B[0:CK, :].rearrange("p (a d) -> p a d", a=1).to_broadcast([CK, CH, D]),
                                   ALU.add).then_inc(S("v3_ready"), 1)

        @block.tensor
        def _(pe):
            def ln_pe(k, src):
                pe.wait_ge(S("xn_ready"), k + 1)
                for b in range(NB):
                    mm = pe.transpose(PM[:, b * NQ:(b + 1) * NQ], src[:, b, :], ident[0:NQ, 0:NQ])
                mm.then_inc(S("xnt_ps"), 1)
                pe.wait_ge(S("xnt_ready"), k + 1)

            def attn_pe(layer):
                chunks = CH + (layer == 3)
                grp = groups(chunks)
                per_b = len(grp) * PAIRS + {0: 6, 1: 3, 2: 0, 3: 5}[layer]
                s_tr, s_ev = S(f"tr_ready{layer}"), S(f"tr_used{layer}")

                def size(c):
                    return CK if c < CH else NQ

                with pe.Fori(0, NB) as b:
                    k = [0]

                    def ring():
                        i = k[0]
                        k[0] += 1
                        stand(pe, s_ev, b * per_b + (i - 1 if i >= 2 else 0) + PRIME)
                        return TR[:, i % 2, :]

                    if layer in (0, 3):
                        if layer == 0:
                            pe.wait_ge(S("nat_in0"), 16 * (b + 1))
                        else:
                            pe.wait_ge(S("cn_ready"), b + 1)
                        for cs in groups(CH):
                            bank = ring()
                            for i, c in enumerate(cs):
                                mm = pe.transpose(bank[:, i * CK:(i + 1) * CK], NAT[:, c, :], ident[0:CK, 0:CK])
                            mm.then_inc(s_tr, 1)
                    if layer < 3:
                        if layer == 0:
                            pe.wait_ge(S("ct_made"), (b + 1) * 3)
                        else:
                            pe.wait_ge(S(f"ct_in{layer}"), 16 * (b + 1))
                        pe.wait_ge(S(f"p_ready{layer}"), b * PAIRS + PRIME)
                        for n in range(3):
                            mm = pe.matmul(PS[:, n, 0:500], WK[layer], CT[:, n * 500:(n + 1) * 500],
                                           start=True, stop=True)
                        mm.then_inc(S(f"k_ps{layer}"), 1)
                    if layer < 2:
                        for cs in groups(CH):
                            bank = ring()
                            for i, c in enumerate(cs):
                                o = bank[0:CK, i * D:(i + 1) * D]
                                mm = pe.matmul(o, CT[:, c * CK:(c + 1) * CK], wv[layer][:, :],
                                               start=True, stop=(layer == 1))
                                if layer == 0:
                                    mm = pe.matmul(o, ones[0:1, 0:CK], rbv, start=False, stop=True)
                            mm.then_inc(s_tr, 1)
                    if layer in (1, 2):
                        pe.matmul(PM[0:1, 0:1], ident[:, 0:1], ident[:, 0:1], start=True, stop=True)\
                          .then_inc(S(f"ct_used{layer}"), 1)

                    def scores(j):
                        pe.wait_ge(S(f"p_ready{layer}"), b * PAIRS + j + PRIME)
                        nb_, w = (3, 500) if layer < 3 else (4, NK3 // 4)
                        for n in range(nb_):
                            mm = pe.matmul(PS[:, n, 0:w], QB[:, 2 * j:2 * j + 2, :], KT[:, n * w:(n + 1) * w],
                                           start=True, stop=True)
                        mm.then_inc(S(f"s_ready{layer}"), 1)

                    def weigh(j):
                        pe.wait_ge(S(f"p_ready{layer}"), b * PAIRS + j + 1 + PRIME)
                        if layer == 3 and j >= 2:
                            pe.wait_ge(S("ao_ready"), b * PAIRS + j - 1)
                        at = []

                        def turn(g):
                            bank = ring()
                            for i, c in enumerate(grp[g]):
                                mm = pe.transpose(bank[0:size(c), i * 128:(i + 1) * 128],
                                                  P[:, j % 2, c * CK:c * CK + size(c)], ident[:, :])
                            mm.then_inc(s_tr, 1)
                            at.append(b * per_b + k[0])

                        def gather(g):
                            pe.wait_ge(s_ev, at[g] + PRIME)
                            for c in grp[g]:
                                if layer < 3:
                                    o, v = PO[:, j * 16:(j + 1) * 16], V[0:size(c), c, 16 * j:16 * j + 16]
                                else:
                                    o, v = (PO, PM)[j % 2][:, 0:128], V[0:size(c), c, :]
                                mm = pe.matmul(o, PT[0:size(c), j % 2, c, :], v, start=(c == 0),
                                               stop=(c == chunks - 1))
                            return mm

                        turn(0)
                        for g in range(1, len(grp)):
                            turn(g)
                            gather(g - 1)
                        gather(len(grp) - 1).then_inc(S(f"pv_ready{layer}"), 1)

                    pe.wait_ge(S(f"k_ready{layer}"), b + 1 + PRIME)
                    pe.wait_ge(S(f"qb_ready{layer}"), b + 1)
                    if layer == 3:
                        pe.wait_ge(S("v3_ready"), (b + 1) * 3 + PRIME)
                    if layer == 2:
                        pe.wait_ge(S("nat_used2"), b + 1 + PRIME)
                    scores(0)
                    for j in range(1, PAIRS):
                        scores(j)
                        weigh(j - 1)
                    weigh(PAIRS - 1)

                    if layer < 2:
                        pe.wait_ge(S(f"z_ready{layer}"), b + 1)
                        pe.transpose(PM[:, 0:128], Z, ident[:, :]).then_inc(S(f"zt_ps{layer}"), 1)
                        pe.wait_ge(S(f"zt_ready{layer}"), b + 1)
                        pe.matmul(PM[0:NQ, 128:256], ZT[:, 0:NQ], wo[layer][:, :], start=True, stop=False)
                        pe.matmul(PM[0:NQ, 128:256], ZT[:, HQ:HQ + NQ], wo[layer][:, :], start=False, stop=False)
                        pe.matmul(PM[0:NQ, 128:256], ones[0:1, 0:NQ], rbo0 if layer == 0 else rbo1,
                                  start=False, stop=True).then_inc(S(f"y_ready{layer}"), 1)
                    elif layer == 2:
                        pe.wait_ge(S(f"z_ready{layer}"), b + 1)
                        pe.matmul(PM[0:NQ, 128:256], sel[:, :], Z, start=True, stop=True)\
                          .then_inc(S(f"y_ready{layer}"), 1)
                    else:
                        pe.wait_ge(S("ao_ready"), (b + 1) * PAIRS)
                        for g in range(2):
                            bank = ring()
                            for i in range(4):
                                mm = pe.transpose(bank[:, i * 128:(i + 1) * 128], AO[:, 4 * g + i, :], ident[:, :])
                            mm.then_inc(s_tr, 1)
                        pe.wait_ge(s_ev, (b + 1) * per_b + PRIME)
                        for h in range(NH):
                            c = (h % 2) * HQ
                            mm = pe.matmul(PM[0:NQ, 128:256], AT[:, h // 2, c:c + NQ], M3[:, h, :],
                                           start=(h == 0), stop=(h == NH - 1))
                        mm.then_inc(S(f"y_ready{layer}"), 1)
                    assert k[0] == per_b
                    pe.wait_ge(S(f"tail{layer}"), b + 1 + PRIME)

            pe.wait_ge(S("const"), 1)
            pe.wait_ge(S("w_raw"), 16 * len(RAWS))
            for i in range(len(RAWS)):
                if i >= 4:
                    pe.wait_ge(S("tw_ready"), i - 3)
                pe.transpose(PS[:, i % 4, 0:128], RAW[:, i, :], ident[:, :]).then_inc(S("tw_ps"), 1)
            pe.wait_ge(S("tw_ready"), len(RAWS))

            def project_q(layer):
                pe.matmul(PM[:, 0:T], WQ[layer], XNT[:, :], start=True, stop=True)\
                  .then_inc(S("q_ps"), 1)
                pe.wait_ge(S("q_ready"), layer + 1)

            pe.wait_ge(S("w_l0"), 16 * 8)
            ln_pe(0, XN)
            project_q(0)
            attn_pe(0)
            ln_pe(1, XN)
            pe.wait_ge(S("w_col"), 16 * 11)
            for t in range(NB):
                pe.wait_ge(S("c_ready"), t + 1)
                for g, n_ in enumerate(("f", "i", "c")):
                    o = PS[:, t % 2, g * NQ:(g + 1) * NQ]
                    pe.matmul(o, tw[f"L0_ffn_w{n_}"], XNT[:, t * NQ:(t + 1) * NQ], start=True, stop=False)
                    mm = pe.matmul(o, tw[f"L0_ffn_u{n_}"], cst[:, t % 2, :], start=False, stop=True)
                mm.then_inc(S("z_gates"), 1)
            pe.wait_ge(S("c_ready"), NB + 1)
            for t in range(NB):
                o = TR[0:NQ, t // 4, (t % 4) * D:(t % 4 + 1) * D]
                pe.matmul(o, XNT[:, t * NQ:(t + 1) * NQ], tw["L0_ffn_wo"], start=True, stop=False)
                pe.matmul(o, cst[:, NB % 2, :], tw["L0_ffn_uo"], start=False, stop=False)
                mm = pe.matmul(o, ones[0:1, 0:NQ], rbos, start=False, stop=True)
            mm.then_inc(S("h_ps"), 1)

            pe.wait_ge(S("w_l1"), 16 * 4)
            ln_pe(2, XN)
            project_q(1)
            attn_pe(1)

            def moe_pe(which):
                blocks = moe_blocks(which)
                w1, w2, b2 = (w1a, w2a, b2a) if which == 0 else (w1b, w2b, b2b)
                if which == 0:
                    pe.wait_ge(S("w_moe1"), 16 * 6)
                    for b in range(NB):
                        o = PO[0:NQ, b * NEXP:(b + 1) * NEXP]
                        pe.matmul(o, XNT[:, b * NQ:(b + 1) * NQ], wg1[:, :], start=True, stop=False)
                        mm = pe.matmul(o, ones[0:1, 0:NQ], grow[:, 0, :], start=False, stop=True)
                else:
                    pe.wait_ge(S("w_moe2"), 16 * 12)
                    for k in range(2):
                        mm = pe.matmul(PS[:, k, 0:T], gw1[:, k * 128:(k + 1) * 128], XNT[:, :],
                                       start=True, stop=True)
                    mm.then_inc(S("gh_ps"), 1)
                    pe.wait_ge(S("gh_ready"), 2)
                    for b in range(NB):
                        o = PO[0:NQ, b * NEXP:(b + 1) * NEXP]
                        for k in range(2):
                            pe.matmul(o, GH[:, k, b * NQ:(b + 1) * NQ], gw2[:, k, :], start=(k == 0), stop=False)
                        mm = pe.matmul(o, ones[0:1, 0:NQ], grow[:, 1, :], start=False, stop=True)
                mm.then_inc(S("lg_ps"), 1)
                pe.wait_ge(S("gate_ready"), which + 1)
                for b in range(NB):
                    mm = pe.transpose(PO[0:NEXP, b * NQ:(b + 1) * NQ], gt[:, b, :], ident[0:NQ, 0:NQ])
                mm.then_inc(S("gt_ps"), 1)
                pe.wait_ge(S("gt_ready"), which + 1)
                done = len(moe_blocks(0)) if which else 0
                edone = NEXP if which else 0
                acc = PM[:, 0:T]
                pe.matmul(acc, b2[:, :], GT[:, :], start=True, stop=False, skip_group_check=True)
                if which:
                    pe.matmul(acc, bs2[:, :], ones[0:1, 0:1].to_broadcast([1, T]), start=False, stop=False,
                              skip_group_check=True)

                def down(i):
                    e, k = blocks[i]
                    pe.wait_ge(S("hg_ready"), done + i + 1)
                    pe.matmul(acc, w2[:, e, k, :], HG[:, i % 3, :], start=False,
                              stop=(i == len(blocks) - 1), skip_group_check=True).then_inc(S("down_ps"), 1)

                for i, (e, k) in enumerate(blocks):
                    if k == 0 and e < NEXP:
                        if e >= 2:
                            pe.wait_ge(S("hg_ready"), done + (e - 1) * blocks_per(which))
                        pe.matmul(TR[:, e % 2, 0:T], esel[:, e, :], GT[:, :], start=True, stop=True)\
                          .then_inc(S("gb_ps"), 1)
                    if i >= 4:
                        pe.wait_ge(S("gelu_ready"), done + i - 3)
                    pe.matmul(PS[:, i % 4, 0:T], w1[:, e, k * 128:(k + 1) * 128], XNT[:, :],
                              start=True, stop=True).then_inc(S("up_ps"), 1)
                    if i >= 3:
                        down(i - 3)
                for i in range(len(blocks) - 3, len(blocks)):
                    down(i)
                pe.wait_ge(S("yt_ready"), which + 1)
                for b in range(NB):
                    mm = pe.transpose(PS[0:NQ, b // 4, (b % 4) * D:(b % 4 + 1) * D], YT[:, b * NQ:(b + 1) * NQ],
                                      ident[:, :])
                mm.then_inc(S("y_nat"), 1)

            ln_pe(3, XN)
            moe_pe(0)
            ln_pe(4, XN)
            project_q(2)
            attn_pe(2)
            ln_pe(5, XN)
            moe_pe(1)
            pe.wait_ge(S("w_l3"), 32)
            pe.wait_ge(S("w_l3s"), 16 * 5)
            for i in range(24):
                if i >= 4:
                    pe.wait_ge(S("w3t_ready"), i - 3)
                else:
                    pe.wait_ge(S("x_upd"), 6)
                pe.transpose(PS[:, i % 4, 0:128], W3r[:, i * 128:(i + 1) * 128], ident[:, :])\
                  .then_inc(S("w3t_ps"), 1)
            pe.wait_ge(S("w3t_ready"), 24)
            for h in range(NH):
                lo_, j = (h % 2) * DH3, h // 2
                if h >= 2:
                    pe.wait_ge(S("gm_ready"), 2 * (h - 1))
                pe.matmul(PS[:, h % 2, 0:D], W3T[lo_:lo_ + DH3, j * 128:(j + 1) * 128],
                          W3T[lo_:lo_ + DH3, 1024 + j * 128:1024 + (j + 1) * 128],
                          start=True, stop=True).then_inc(S("gm_ps"), 1)
                pe.matmul(PS[:, 2 + h % 2, 0:D], W3T[lo_:lo_ + DH3, 2048 + j * 128:2048 + (j + 1) * 128],
                          wo3[lo_:lo_ + DH3, j, :], start=True, stop=True).then_inc(S("gm_ps"), 1)
            pe.wait_ge(S("gm_ready"), 2 * NH)
            ln_pe(6, XN)
            ln_pe(7, XN2)
            pe.wait_ge(S("lat_t"), 1)
            for h in range(NH):
                if h >= 4:
                    pe.wait_ge(S("q3_ready"), h - 3)
                pe.matmul(PS[:, h % 4, 0:T], G3[:, h, :], LT[:, :], start=True, stop=True)\
                  .then_inc(S("q3_ps"), 1)
            pe.wait_ge(S("q3_ready"), NH)
            attn_pe(3)
            pe.wait_ge(S("w_lora"), 64)
            pe.transpose(TR[0:100, 0, 0:4], ld_, ident[0:4, 0:4])
            pe.transpose(TR[0:4, 0, 4:54], lu_, ident[0:50, 0:50])
            pe.transpose(TR[0:50, 0, 128:256], ua_, ident[:, :]).then_inc(S("lora_ps"), 1)
            pe.wait_ge(S("lora_ready"), 3)
            pe.matmul(TR[0:4, 1, 0:128], ldT, da_, start=True, stop=True).then_inc(S("lora_ps"), 1)
            pe.wait_ge(S("lora_ready"), 4)
            pe.matmul(TR[0:50, 1, 128:256], luT, t1_, start=True, stop=True).then_inc(S("lora_ps"), 1)
            pe.wait_ge(S("lora_ready"), 5)
            pe.matmul(TR[:, 1, 256:384], t2_, uaT, start=True, stop=True).then_inc(S("lora_ps"), 1)
            pe.wait_ge(S("lora_ready"), 6)
            ln_pe(8, XN)
            for b in range(NB):
                o = PS[0:NQ, b // 4, (b % 4) * D:(b % 4 + 1) * D]
                x_ = XNT[:, b * NQ:(b + 1) * NQ]
                pe.matmul(o, x_, tw["L3_ffn_W"], start=True, stop=False)
                pe.matmul(o, ones[0:1, 0:NQ], rb3, start=False, stop=False)
                mm = pe.matmul(o, x_, lwT, start=False, stop=True)
            mm.then_inc(S("y_last"), 1)

        @block.scalar
        def _(act):
            def std_act(k):
                act.wait_ge(S("var_ready"), k + 1)
                act.activation(std[:, :], mv[:, :, 1], ACT.Sqrt, bias=epst[0:NQ, :]).then_inc(S("std_ready"), 1)

            def ln_act(k, dst=None, w=1.0, bias=0.0):
                std_act(k)
                act.wait_ge(S("xnt_ps"), k + 1)
                act.activation((XNT if dst is None else dst)[:, :], PM[:, 0:T], ACT.Identity,
                               bias=bias, scale=w).then_inc(S("xnt_ready"), 1)

            def q_act(layer):
                act.wait_ge(S("q_ps"), layer + 1)
                act.activation(QT[:, :], PM[:, 0:T], ACT.Identity,
                               bias=colat["bq"] if layer == 0 else 0.0).then_inc(S("q_ready"), 1)

            def attn_act(layer):
                chunks = CH + (layer == 3)
                grp = groups(chunks)
                per_b = len(grp) * PAIRS + {0: 6, 1: 3, 2: 0, 3: 5}[layer]
                s_tr, s_ev = S(f"tr_ready{layer}"), S(f"tr_used{layer}")
                scale = SCALES[layer]
                with act.Fori(0, NB) as b:
                    k = [0]

                    def bank():
                        k[0] += 1
                        act.wait_ge(s_tr, b * per_b + k[0])
                        return TR[:, (k[0] - 1) % 2, :]

                    if layer == 0:
                        act.wait_ge(S("ct_saved"), 16 * b + 16)
                        act.wait_ge(S("v_done"), b + PRIME)
                        for g in range(3):
                            t_ = bank()
                            act.activation(CT[:, g * 500:(g + 1) * 500], t_[:, 0:500], ACT.Copy)\
                               .then_inc(s_ev, 1)
                            act.wait_ge(s_ev, b * per_b + k[0] + PRIME)
                            act.nop().then_inc(S("ct_made"), 1)
                    if layer == 3:
                        for g in range(3):
                            t_ = bank()
                            act.activation(KT[:, g * 500:(g + 1) * 500], t_[:, 0:500], ACT.Identity,
                                           scale=colat["w1"], bias=colat["b1"]).then_inc(s_ev, 1)
                        act.wait_ge(s_ev, b * per_b + k[0] + PRIME)
                        act.nop().then_inc(S("k_ready3"), 1)
                    if layer < 3:
                        act.wait_ge(S(f"k_ps{layer}"), b + 1)
                        act.activation(KT[:, 0:NK], PS[:, 0:3, 0:500], ACT.Identity,
                                       bias=colat["bk"] if layer == 0 else 0.0).then_inc(S(f"k_ready{layer}"), 1)
                    if layer < 2:
                        for g in range(3):
                            t_ = bank()
                            act.activation(V[0:CK, 4 * g:4 * g + 4, :], t_[0:CK, :], ACT.Copy).then_inc(s_ev, 1)
                        if layer == 0:
                            act.wait_ge(s_ev, b * per_b + k[0] + PRIME)
                            act.nop().then_inc(S("v_done"), 1)

                    def exps(j):
                        act.wait_ge(S(f"max_ready{layer}"), b * PAIRS + j + 1)
                        if layer == 0:
                            act.activation(P[:, j % 2, 0:NK], PS[:, 0:3, 0:500], ACT.Exp, bias=nb[:, j:j + 1],
                                           scale=scale, accum_out=den[:, j:j + 1]).then_inc(S("p_ready0"), 1)
                        elif layer == 1:
                            act.activation(P[:, j % 2, 0:NK], E[:, :], ACT.Exp, bias=nb[:, j:j + 1],
                                           accum_out=den[:, j:j + 1]).then_inc(S("p_ready1"), 1)
                        elif layer == 2:
                            act.activation(E[:, :], PS[:, 0:3, 0:500], ACT.Exp, bias=nb[:, j:j + 1],
                                           scale=scale).then_inc(S("e_ready"), 1)
                        else:
                            act.activation(P[:, j % 2, :], PS[:, 0:4, 0:NK3 // 4], ACT.Exp, bias=nb[:, j:j + 1],
                                           scale=scale, accum_out=den[:, j:j + 1]).then_inc(S("p_ready3"), 1)

                    def copy_out(j, g):
                        t_ = bank()
                        c0, full = grp[g][0], [c for c in grp[g] if c < CH]
                        if full:
                            act.activation(PT[0:CK, j % 2, c0:c0 + len(full), :], t_[0:CK, 0:128 * len(full)],
                                           ACT.Copy).then_inc(s_ev, 1)
                        else:
                            act.activation(PT[0:NQ, j % 2, CH, :], t_[0:NQ, 0:128], ACT.Copy).then_inc(s_ev, 1)

                    def before(j):
                        if j >= 2:
                            act.wait_ge(S(f"pv_ready{layer}"), b * PAIRS + j - 1)

                    exps(0)
                    for j in range(1, PAIRS):
                        before(j - 1)
                        early = 2 if layer != 2 else 3
                        for g in range(early):
                            copy_out(j - 1, g)
                        exps(j)
                        for g in range(early, len(grp)):
                            copy_out(j - 1, g)
                    before(PAIRS - 1)
                    for g in range(len(grp)):
                        copy_out(PAIRS - 1, g)
                    if layer < 2:
                        act.wait_ge(S(f"zt_ps{layer}"), b + 1)
                        act.activation(ZT, PM[:, 0:128], ACT.Copy).then_inc(S(f"zt_ready{layer}"), 1)
                    if layer == 3:
                        for g in range(2):
                            t_ = bank()
                            act.activation(AT[:, 4 * g:4 * g + 4, :], t_[:, :], ACT.Copy).then_inc(s_ev, 1)
                    assert k[0] == per_b
                    act.wait_ge(S(f"tail{layer}"), b + 1 + PRIME)

            for i in range(len(RAWS)):
                act.wait_ge(S("tw_ps"), i + 1)
                act.activation(TW[:, i, :], PS[:, i % 4, 0:128], ACT.Copy).then_inc(S("tw_ready"), 1)
            act.wait_ge(S("w_l0"), 16 * 8)
            ln_act(0)
            q_act(0)
            attn_act(0)
            ln_act(1)
            act.wait_ge(S("w_col"), 16 * 11)
            for t in range(NB):
                act.wait_ge(S("z_gates"), t + 1)
                act.wait_ge(S("c_ready"), t + 1)
                z_ = PS[:, t % 2, :]
                act.activation(gates[:, 0, :], z_[:, 0:NQ], ACT.Sigmoid, bias=colat["bf"]).then_inc(S("g_ready"), 1)
                act.activation(gates[:, 1, :], z_[:, NQ:2 * NQ], ACT.Sigmoid, bias=colat["bi"]).then_inc(S("g_ready"), 1)
                act.activation(gates[:, 2, :], z_[:, 2 * NQ:3 * NQ], ACT.Tanh, bias=colat["bc"]).then_inc(S("g_ready"), 1)
            act.wait_ge(S("h_ps"), 1)
            act.activation(XN[:, :, :], TR[0:NQ, :, :], ACT.Tanh).then_inc(S("h_ready"), 1)
            ln_act(2)
            q_act(1)
            attn_act(1)

            def moe_act(which):
                blocks = moe_blocks(which)
                done = len(moe_blocks(0)) if which else 0
                b1 = b1a if which == 0 else b1b
                func = ACT.Gelu if which == 0 else ACT.Gelu_apprx_tanh
                if which:
                    act.wait_ge(S("gh_ps"), 1)
                    for k in range(2):
                        act.activation(GH[:, k, :], PS[:, k, 0:T], ACT.Gelu, bias=gb1[:, k:k + 1])\
                           .then_inc(S("gh_ready"), 1)
                act.wait_ge(S("dl_ready"), which + 1)
                act.activation(ex[:, :, :], dl[:, :, :], ACT.Exp).then_inc(S("ex_ready"), 1)
                act.wait_ge(S("gt_ps"), which + 1)
                act.activation(GT[:, :], PO[0:NEXP, 0:T], ACT.Copy).then_inc(S("gt_ready"), 1)
                for i, (e, k) in enumerate(blocks):
                    act.wait_ge(S("up_ps"), done + i + 1)
                    if i >= 3:
                        act.wait_ge(S("hg_ready"), done + i - 2)
                    act.activation(H[:, i % 3, :], PS[:, i % 4, 0:T], func,
                                   bias=b1[:, e * blocks_per(which) + k:e * blocks_per(which) + k + 1])\
                       .then_inc(S("gelu_ready"), 1)
                act.wait_ge(S("down_ps"), done + len(blocks))
                act.activation(YT[:, :], PM[:, 0:T], ACT.Copy).then_inc(S("yt_ready"), 1)

            ln_act(3)
            moe_act(0)
            ln_act(4)
            q_act(2)
            attn_act(2)
            ln_act(5)
            moe_act(1)
            for i in range(24):
                act.wait_ge(S("w3t_ps"), i + 1)
                act.activation(W3T[:, i * 128:(i + 1) * 128], PS[:, i % 4, 0:128], ACT.Copy)\
                   .then_inc(S("w3t_ready"), 1)
            for h in range(NH):
                act.wait_ge(S("gm_ps"), 2 * h + 1)
                act.activation(G3[:, h, :], PS[:, h % 2, 0:D], ACT.Copy).then_inc(S("gm_ready"), 1)
                act.wait_ge(S("gm_ps"), 2 * h + 2)
                act.activation(M3[:, h, :], PS[:, 2 + h % 2, 0:D], ACT.Copy).then_inc(S("gm_ready"), 1)
            ln_act(6)
            std_act(7)
            act.wait_ge(S("xnt_ps"), 8)
            act.activation(LT[:, :], PM[:, 0:T], ACT.Identity, bias=colat["b2"], scale=colat["w2"])\
               .then_inc(S("lat_t"), 1)
            act.wait_ge(S("lat_t"), 1)
            act.nop().then_inc(S("xnt_ready"), 1)
            act.wait_ge(S("cmv_ready"), 1)
            act.activation(crs[:, :], cmv[:, :, 1], ACT.Sqrt, bias=epst[0:CK, :]).then_inc(S("cstd_ready"), 1)
            for h in range(NH):
                act.wait_ge(S("q3_ps"), h + 1)
                act.activation(Q3[:, h, :], PS[:, h % 4, 0:T], ACT.Copy).then_inc(S("q3_ready"), 1)
            attn_act(3)
            act.wait_ge(S("lora_ps"), 1)
            act.activation(ldT, TR[0:100, 0, 0:4], ACT.Copy).then_inc(S("lora_ready"), 1)
            act.activation(luT, TR[0:4, 0, 4:54], ACT.Copy).then_inc(S("lora_ready"), 1)
            act.activation(uaT, TR[0:50, 0, 128:256], ACT.Copy).then_inc(S("lora_ready"), 1)
            act.wait_ge(S("lora_ps"), 2)
            act.activation(t1_, TR[0:4, 1, 0:128], ACT.Copy).then_inc(S("lora_ready"), 1)
            act.wait_ge(S("lora_ps"), 3)
            act.activation(t2_, TR[0:50, 1, 128:256], ACT.Copy).then_inc(S("lora_ready"), 1)
            act.wait_ge(S("lora_ps"), 4)
            act.activation(lwT, TR[:, 1, 256:384], ACT.Copy).then_inc(S("lora_ready"), 1)
            ln_act(8)

        @block.vector
        def _(dve):
            n = [0]
            chain = S("dve_step")

            def link(ins):
                n[0] += 1
                ins.then_inc(chain, 1)
                dve.wait_ge(chain, n[0])

            def ln_dve(k, src, dst):
                for b in range(NB):
                    ins = dve.bn_stats(st[:, b, :], src[:, b, :])
                link(ins)
                for b in range(NB):
                    ins = dve.bn_aggr(mv[:, b, :], st[:, b, :])
                ins.then_inc(S("var_ready"), 1)
                dve.wait_ge(S("std_ready"), k + 1)
                link(dve.reciprocal(rstd[:, :], std[:, :]))
                if k:
                    dve.wait_ge(S("xnt_ps"), k)
                for b in range(NB):
                    ins = dve.tensor_scalar(dst[:, b, :], src[:, b, :], mv[:, b, 0:1], rstd[:, b:b + 1],
                                            ALU.subtract, ALU.mult)
                ins.then_inc(S("xn_ready"), 1)

            def attn_dve(layer):
                scale = SCALES[layer]
                base = n[0]
                lk = {0: PAIRS + 1 + 1 + 3, 1: PAIRS + 2, 2: PAIRS * 7 + 2, 3: PAIRS + 1 + PAIRS}[layer]
                with dve.Fori(0, NB) as b:
                    m = [0]

                    def blink(ins):
                        m[0] += 1
                        ins.then_inc(chain, 1)
                        stand(dve, chain, b * lk + (base + m[0]))

                    def bmark(ins):
                        m[0] += 1
                        ins.then_inc(chain, 1)

                    if layer == 0:
                        dve.wait_ge(S("nat_in0"), 16 * (b + 1))
                        for c in range(CH):
                            ins = dve.bn_stats(cstat[:, c, :], NAT[:, c, :])
                        blink(ins)
                        for c in range(CH):
                            ins = dve.bn_aggr(cmvb[:, c, :], cstat[:, c, :])
                        blink(ins)
                        blink(dve.tensor_copy(cmv[:, bass.ds(b * CH, CH), :], cmvb[:, :, :]))
                        dve.wait_ge(S("tr_ready0"), b * 30 + 3)
                        dve.nop().then_inc(S("nat_used0"), 1)
                    if layer == 3:
                        dve.wait_ge(S("nat_in3"), 16 * (b + 1))
                        for c in range(CH):
                            ins = dve.tensor_scalar(
                                NAT[:, c, :], NAT[:, c, :],
                                cmv[:, bass.ds(b * CH + c, 1), 0:1].rearrange("p a s -> p (a s)"),
                                crs[:, bass.ds(b * CH + c, 1)], ALU.subtract, ALU.mult)
                        ins.then_inc(S("cn_ready"), 1)
                        dve.tensor_copy(QB[:, :, 0:NQ], Q3[:, :, bass.ds(b * NQ, NQ)]).then_inc(S("qb_ready3"), 1)
                    else:
                        dve.tensor_tensor(
                            QB[:, :, 0:NQ],
                            QT[:, bass.ds(b * NQ, NQ)].rearrange("p (a q) -> p a q", a=1).to_broadcast([D, NH, NQ]),
                            hmask[:, :].rearrange("p (h a) -> p h a", a=1).to_broadcast([D, NH, NQ]),
                            ALU.mult).then_inc(S(f"qb_ready{layer}"), 1)
                    for j in range(PAIRS):
                        t1 = b * PAIRS + j + 1
                        stand(dve, S(f"s_ready{layer}"), t1)
                        if layer == 1:
                            blink(dve.tensor_tensor_reduce(out=E[:, :], in0=PS[:, 0:3, 0:500], in1=MB[:, :],
                                                           scale=scale, scalar=LOWEST, op0=ALU.add, op1=ALU.max,
                                                           accum_out=rm[:, j:j + 1]))
                            dve.tensor_scalar(nb[:, j:j + 1], rm[:, j:j + 1], -1.0, None, ALU.mult)\
                               .then_inc(S("max_ready1"), 1)
                        elif layer != 2:
                            s_ = PS[:, 0:3, 0:500] if layer == 0 else PS[:, 0:4, 0:NK3 // 4]
                            blink(dve.tensor_reduce(rm[:, j:j + 1], s_, XY_AX, ALU.max))
                            dve.tensor_scalar(nb[:, j:j + 1], rm[:, j:j + 1], -scale, None, ALU.mult)\
                               .then_inc(S(f"max_ready{layer}"), 1)
                        else:
                            s_ = PS[:, 0:3, 0:500]
                            w_ = W[:, :].rearrange("p (a n) -> p a n", a=3)
                            blink(dve.max(m8[:, 0:8], s_))
                            dve.tensor_scalar(nb[:, j:j + 1], m8[:, 0:1], -scale, None, ALU.mult)
                            for r in range(1, TOPK // 8):
                                blink(dve.match_replace(out=w_, in_to_replace=m8[:, 8 * r - 8:8 * r],
                                                        in_values=s_ if r == 1 else w_, imm_value=LOWEST))
                                if r == 1:
                                    dve.sem_inc(S("max_ready2"), 1)
                                blink(dve.max(m8[:, 8 * r:8 * r + 8], w_))
                            dve.wait_ge(S("e_ready"), t1)
                            dve.scalar_tensor_tensor(out=P[:, j % 2, 0:NK], in0=s_, scalar=m8[:, TOPK - 1:TOPK],
                                                     in1=E[:, :].rearrange("p (a n) -> p a n", a=3),
                                                     op0=ALU.is_ge, op1=ALU.mult, accum_out=den[:, j:j + 1])\
                               .then_inc(S("p_ready2"), 1)
                        if layer == 3 and j >= 1:
                            normalise(dve, b, j - 1, blink)
                    if layer == 3:
                        normalise(dve, b, PAIRS - 1, blink)
                    else:
                        dve.wait_ge(S(f"p_ready{layer}"), (b + 1) * PAIRS + PRIME)
                        blink(dve.reciprocal(rden[:, :], den[:, :]))
                        blink(dve.tensor_tensor(
                            rdm[:, :, :], rden[:, :].rearrange("p (j a) -> p j a", a=1).to_broadcast([128, PAIRS, 2]),
                            pmask[:, :].rearrange("p (a h) -> p a h", a=1).to_broadcast([128, PAIRS, 2]), ALU.mult))
                        dve.wait_ge(S(f"pv_ready{layer}"), (b + 1) * PAIRS)
                        dve.tensor_tensor(
                            Z.rearrange("p (h d) -> p h d", d=DH),
                            PO[:, 0:128].rearrange("p (h d) -> p h d", d=DH),
                            rdm[:, :, :].rearrange("p j h -> p (j h)").rearrange("p (h a) -> p h a", a=1)
                            .to_broadcast([128, NH, DH]), ALU.mult).then_inc(S(f"z_ready{layer}"), 1)
                    dve.wait_ge(S(f"y_ready{layer}"), b + 1)
                    xb = X[:, bass.ds(b, 1), :].rearrange("p a d -> p (a d)")
                    dve.tensor_tensor(xb, PM[0:NQ, 128:256], xb, ALU.add).then_inc(S(f"tail{layer}"), 1)
                    while m[0] < lk:
                        bmark(dve.nop())
                    assert m[0] == lk, (m[0], lk)
                n[0] += lk * NB
                dve.wait_ge(S(f"tail{layer}"), NB + PRIME)
                dve.wait_ge(chain, n[0])

            def normalise(dve, b, j, blink):
                dve.wait_ge(S("pv_ready3"), b * PAIRS + j + 1)
                blink(dve.reciprocal(rden[:, j:j + 1], den[:, j:j + 1]))
                dve.tensor_scalar(AO[:, j, :], (PO, PM)[j % 2][:, 0:128], rden[:, j:j + 1], None,
                                  ALU.mult).then_inc(S("ao_ready"), 1)

            dve.wait_ge(S("const"), 1)
            dve.wait_ge(S("x_in"), 16)
            ln_dve(0, X, XN)
            dve.wait_ge(S("q_ready"), 1)
            attn_dve(0)
            ln_dve(1, X, XN)
            dve.wait_ge(S("w_col"), 16 * 11)
            dve.tensor_scalar(cst[:, 0, :], ones[:, 0:NQ], colat["in_c"], None, ALU.mult).then_inc(S("c_ready"), 1)
            dve.wait_ge(S("c_ready"), 1)
            for t in range(NB):
                dve.wait_ge(S("g_ready"), 3 * t + 3)
                dve.tensor_tensor(gtmp[:, 0, :], gates[:, 0, :], cst[:, t % 2, :], ALU.mult)
                link(dve.tensor_tensor(gtmp[:, 1, :], gates[:, 1, :], gates[:, 2, :], ALU.mult))
                dve.tensor_tensor(cst[:, (t + 1) % 2, :], gtmp[:, 0, :], gtmp[:, 1, :], ALU.add)\
                   .then_inc(S("c_ready"), 1)
                dve.wait_ge(S("c_ready"), t + 2)
            dve.wait_ge(S("h_ready"), 1)
            link(dve.tensor_tensor(X[:, :, :], X[:, :, :], XN[:, :, :], ALU.add))
            ln_dve(2, X, XN)
            dve.wait_ge(S("mask_in"), 32)
            link(dve.memset(MB[:, :], 0.0))
            for half in range(2):
                r = slice(HQ * half, HQ * half + NQ)
                ins = dve.tensor_scalar(MB[r, :].rearrange("q (c p) -> q c p", c=CH),
                                        MR[r, :].rearrange("q (p c) -> q c p", c=CH), 0.0, NEG / SCALES[1],
                                        ALU.is_equal, ALU.mult)
            ins.then_inc(S("mask_made"), 1)
            dve.wait_ge(S("mask_made"), 1)
            dve.wait_ge(S("q_ready"), 2)
            attn_dve(1)

            def moe_dve(which):
                blocks = moe_blocks(which)
                done = len(moe_blocks(0)) if which else 0
                dve.wait_ge(S("lg_ps"), which + 1)
                link(dve.tensor_copy(lg[:, :, :], PO[0:NQ, 0:NB * NEXP]))
                for b in range(NB):
                    ins = dve.max(top[:, b, :], lg[:, b, :])
                link(ins)
                for b in range(NB):
                    ins = dve.max_index(tidx[:, b, :], top[:, b, :], lg[:, b, :])
                link(ins)
                link(dve.tensor_copy(tif[:, :, :], tidx[:, :, 0:2]))
                t0 = top[:, :, 0:1].to_broadcast([NQ, NB, NEXP])
                dve.tensor_tensor(dl[:, :, :], top[:, :, :] , t0, ALU.subtract).then_inc(S("dl_ready"), 1)
                dve.wait_ge(S("ex_ready"), which + 1)
                terms = ex[:, :, 0:2] if which == 0 else ex[:, :, :]
                link(dve.tensor_reduce(sm[:, :], terms, X_AX, ALU.add))
                link(dve.reciprocal(sm[:, :], sm[:, :]))
                link(dve.tensor_tensor(wt[:, :, :], ex[:, :, 0:2],
                                       sm[:, :].rearrange("p (b a) -> p b a", a=1).to_broadcast([NQ, NB, 2]), ALU.mult))
                for r, g_ in ((0, gt), (1, gt2)):
                    link(dve.tensor_tensor(g_[:, :, :], iota8[:, :].rearrange("p (a e) -> p a e", a=1).to_broadcast([NQ, NB, NEXP]),
                                           tif[:, :, r:r + 1].to_broadcast([NQ, NB, NEXP]), ALU.is_equal))
                    link(dve.tensor_tensor(g_[:, :, :], g_[:, :, :], wt[:, :, r:r + 1].to_broadcast([NQ, NB, NEXP]), ALU.mult))
                dve.tensor_tensor(gt[:, :, :], gt[:, :, :], gt2[:, :, :], ALU.add).then_inc(S("gate_ready"), 1)
                per = blocks_per(which)
                for i, (e, k) in enumerate(blocks):
                    dve.wait_ge(S("gelu_ready"), done + i + 1)
                    if i >= 3:
                        dve.wait_ge(S("down_ps"), done + i - 2)
                    if e < NEXP:
                        dve.wait_ge(S("gb_ps"), (NEXP if which else 0) + e + 1)
                        dve.tensor_tensor(HG[:, i % 3, :], H[:, i % 3, :], TR[:, e % 2, 0:T], ALU.mult)\
                           .then_inc(S("hg_ready"), 1)
                    else:
                        dve.tensor_copy(HG[:, i % 3, :], H[:, i % 3, :]).then_inc(S("hg_ready"), 1)
                dve.wait_ge(S("y_nat"), which + 1)
                link(dve.tensor_tensor(X[:, :, :], X[:, :, :], PS[0:NQ, 0:2, :].rearrange("p a (b d) -> p (a b) d", d=D),
                                       ALU.add))
                dve.nop().then_inc(S("moe_done"), 1)

            ln_dve(3, X, XN)
            moe_dve(0)
            ln_dve(4, X, XN)
            dve.wait_ge(S("q_ready"), 3)
            attn_dve(2)
            ln_dve(5, X, XN)
            moe_dve(1)
            dve.nop().then_inc(S("x_upd"), 6)
            ln_dve(6, X, XN)
            dve.wait_ge(S("xn_ready"), 7)
            ln_dve(7, XN, XN2)
            dve.nop().then_inc(S("cmv_ready"), 1)
            dve.wait_ge(S("cstd_ready"), 1)
            link(dve.reciprocal(crs[:, :], crs[:, :]))
            dve.wait_ge(S("q3_ready"), NH)
            attn_dve(3)
            ln_dve(8, X, XN)
            dve.wait_ge(S("y_last"), 1)
            dve.tensor_tensor(X[:, :, :], X[:, :, :], PS[0:NQ, 0:2, :].rearrange("p a (b d) -> p (a b) d", d=D),
                              ALU.add).then_inc(S("x_final"), 1)


_INS = None


def kernel(**inputs):
    import numpy as _np
    import concourse.bacc as _bacc
    from concourse import mybir as _mybir
    from concourse.bass_utils import run_bass_kernel_spmd as _run

    nc = _bacc.Bacc("TRN2", target_bir_lowering=False, num_devices=1)
    arrays, args = {}, {}
    for name in inputs:
        a = _np.ascontiguousarray(inputs[name])
        if name == "L2_ffn_task_ids":
            continue
        arrays[f"in_{name}"] = a
        args[name] = nc.dram_tensor(f"in_{name}", a.shape, _mybir.dt.from_np(a.dtype), kind="ExternalInput").ap()
    scratch = nc.dram_tensor("ctx_transposed", (NB, D, NK), F32, kind="Internal").ap()
    out = nc.dram_tensor("out_0", (NB, NQ, D), F32, kind="ExternalOutput").ap()
    megakernel(nc, args, scratch, out)
    r = _run(nc, [arrays], core_ids=[0])
    return r.results[0]["out_0"]
```

```python
from contextlib import ExitStack

import concourse.bass as bass
from concourse import mybir

F32 = mybir.dt.float32
BF16 = mybir.dt.bfloat16
I32 = mybir.dt.int32
U32 = mybir.dt.uint32
ALU = mybir.AluOpType
ACT = mybir.ActivationFunctionType
X_AX = mybir.AxisListType.X
XY_AX = mybir.AxisListType.XY

NB, NQ, D = 8, 56, 128
T = NB * NQ
NK = 1500
CH, CK = 12, 125
NH, DH = 16, 8
PAIRS = NH // 2
HQ = 64
DH3 = 64
NK3 = NK + NQ
EPS = 1e-5
NEXP = 8
FF1, FF2 = 512, 256
TOPK = 32
NEG = -1.0e9
LOWEST = -3.0e38
SCALES = [1.0, 8.0 ** -0.5, 8.0 ** -0.5, 0.125]
PRIME = 1
UNIT = 8 * NQ
PAIR = 2 * NQ
VW = 2 * DH + 1
BELOW = -3.0e38
WEIGHED = 3
PV_PRIME = 2
TR_PRIME = 4
TURNS = 3 * PAIRS
GRP = 4


def plan(layer):
    prep = {0: [("ct", g) for g in range(3)] + [("kt", g) for g in range(3)] + [("v", g) for g in range(4)],
            1: [("kt", g) for g in range(3)] + [("v", g) for g in range(3)],
            3: [("xt", g) for g in range(4)]}[layer]
    chunks = CH + (layer == 3)
    unit = [("s", c) for c in range(chunks)]
    ahead = [("prep", *e) for e in prep] + [("score", *e) for e in unit]
    turn = []
    for slot in range(4):
        turn += [(slot, "score", *e) for e in unit]
        if slot % 2 == 0:
            turn += [(slot, "prep", *e) for e in prep]
    assert len(turn) % 4 == 0
    return prep, chunks, ahead, turn


class Count:

    def __init__(self, base):
        self.base, self.k = base, 0

    def mark(self, ins):
        self.k += 1
        ins.then_inc(self.sem, 1)
        return self.base + self.k


MARKS = {0: 56, 1: 52, 3: 56}


class Ring:

    def __init__(self, base, skip):
        self.base, self.skip, self.k = base, skip % 4, 0

    def next(self):
        self.k += 1
        return (self.skip + self.k - 1) % 4, self.base + self.k


def groups(chunks):
    return [list(range(g, min(g + GRP, chunks))) for g in range(0, chunks, GRP)]


def moe_blocks(which):
    return [(e, k) for e in range(NEXP + which) for k in range(blocks_per(which))]


def blocks_per(which):
    return (FF1, FF2)[which] // 128


def megakernel(nc, A, scratch, out):
    ctx = ExitStack()
    with ctx:
        def sb(name, shape, dt=F32):
            return ctx.enter_context(nc.sbuf_tensor(name, shape, dt))

        sems = {}

        def S(name):
            if name not in sems:
                sems[name] = ctx.enter_context(nc.semaphore(name))
            return sems[name]

        X = sb("X", [NQ, NB, D])
        XN = sb("XN", [NQ, NB, D])
        XNT = sb("XNT", [D, T])
        ident = sb("ident", [128, 128])
        hmask = sb("hmask", [128, NH])
        pmask = sb("pmask", [128, 2])
        sel = sb("sel", [128, NQ])
        ones = sb("ones", [128, 128])
        esel = sb("esel", [NEXP, NEXP, 128])
        iota8 = sb("iota8", [NQ, NEXP])
        epst = sb("epst", [128, 1])
        st = sb("st", [NQ, NB, 6])
        mv = sb("mv", [NQ, NB, 2])
        std = sb("std", [NQ, NB])
        rstd = sb("rstd", [NQ, NB])

        wq = [sb(f"wq{i}", [D, D]) for i in range(2)]
        wk = [sb(f"wk{i}", [D, D]) for i in range(2)]
        wv = [sb(f"wv{i}", [D, D]) for i in range(2)]
        wo = [sb(f"wo{i}", [D, D]) for i in range(2)]
        COLS = ["bq", "bk", "bv", "bf", "bi", "bc", "in_c", "w1", "b1", "w2", "b2"]
        col = sb("col", [D, len(COLS)])
        colat = {n: col[:, i:i + 1] for i, n in enumerate(COLS)}
        rows = sb("rows", [1, 5, D])
        rbv, rbo0, rbos, rbo1, rb3 = (rows[:, i, :] for i in range(5))
        grow = sb("grow", [1, 2, NEXP])
        TW = sb("TW", [D, 11, D])
        SUB = sb("SUB", [128, 3, T])
        YT = SUB[:, 0, :]
        big = sb("big", [128, 9216])
        w1a = big[:, 0:4096].rearrange("p (e f) -> p e f", e=NEXP)
        w2a = big[:, 4096:8192].rearrange("p (e k d) -> p e k d", e=NEXP, k=4)
        w1b = big[:, 0:2304].rearrange("p (e f) -> p e f", e=9)
        w2b = big[:, 2304:4608].rearrange("p (e k d) -> p e k d", e=9, k=2)
        gw1 = big[:, 4608:4864]
        bcol = sb("bcol", [128, 52])
        b1a = bcol[:, 0:32]
        b1b = bcol[:, 32:50]
        gb1 = bcol[:, 50:52]
        wg1 = sb("wg1", [D, NEXP])
        gw2 = sb("gw2", [128, 2, NEXP])
        b2a = sb("b2a", [NEXP, D])
        b2b = sb("b2b", [NEXP, D])
        bs2 = sb("bs2", [1, D])
        w1B = sb("w1B", [128, D])
        b1B = sb("b1B", [128, D])
        w2B = sb("w2B", [NQ, D])
        b2B = sb("b2B", [NQ, D])
        lo = sb("lo", [128, 512])
        ld_, lu_ = lo[0:4, 0:100], lo[0:50, 100:104]
        ua_, da_ = lo[:, 104:154], lo[0:100, 154:282]
        lot = sb("lot", [128, 640])
        ldT, luT, uaT = lot[0:100, 0:4], lot[0:4, 4:54], lot[0:50, 128:256]
        t1_, t2_, lwT = lot[0:4, 256:384], lot[0:50, 384:512], lot[:, 512:640]

        NAT = sb("NAT", [CK, CH, D])
        CT = sb("CT", [D, NK])
        KTT = sb("KTT", [D, 2, NK3])
        KT = KTT[:, 0, :]
        VV = sb("VV", [128, 2, (CH + 1) * PAIRS * VW])
        V = VV[:, 0, 0:(CH + 1) * D].rearrange("p (c d) -> p c d", d=D)
        VP = VV[:, :, 0:CH * PAIRS * VW].rearrange("p b (c j w) -> p b c j w", c=CH, j=PAIRS)
        V3 = VV[:, :, 0:(CH + 1) * D].rearrange("p b (c d) -> p b c d", d=D)
        QT = sb("QT", [D, T])
        QB = sb("QB", [D, NH, HQ])
        QP = sb("QP", [D, 2, NH * NQ])
        ST = sb("ST", [128, 2, (CH + 1) * UNIT])
        SU = ST[:, :, :].rearrange("p u (c n) -> p u c n", n=UNIT)
        flat = ST[:, :, :].rearrange("p u n -> p (u n)")
        RAW = flat[:, 0:11 * D].rearrange("p (n d) -> p n d", d=D)
        P = flat[:, 0:2 * NK].rearrange("p (r n) -> p r n", r=2)
        E = flat[:, 2 * NK:3 * NK]
        SC = flat[:, 3 * NK:5 * NK].rearrange("p (r n) -> p r n", r=2)
        PT = flat[:, 5 * NK:5 * NK + 2 * CH * 128].rearrange("p (r c n) -> p r c n", r=2, c=CH)
        XN2 = flat[0:NQ, 0:NB * D].rearrange("p (b d) -> p b d", d=D)
        MI = flat[0:NQ, 11 * D:11 * D + NK].bitcast(I32)
        MM = sb("MM", [128, NK], BF16)
        I8 = sb("I8", [128, UNIT], BF16)
        ACC = sb("ACC", [CK, 2, 2, UNIT])
        rmx = sb("rmx", [PAIR, 4])
        DG = sb("DG", [PAIR, 4, PAIR])
        SUMS = SUB[0:CK, 0:2, :]
        RB = SUB[:, 2, :]
        O3 = QB[:, :, 0:NQ]
        pm = sb("pm", [PAIR, 2])
        rdu = sb("rdu", [PAIR, 4])
        rdv = sb("rdv", [PAIR, 4, 2])
        ZU = sb("ZU", [PAIR, PAIRS, 2, DH])
        ZS = sb("ZS", [128, 2, 128])
        Z = ZS[:, 0, :]
        ZT = ZS[:, 1, :]
        cstat = sb("cstat", [CK, CH, 6])
        cmv = sb("cmv", [CK, NB * CH, 2])
        cmvb = sb("cmvb", [CK, CH, 2])
        crs = sb("crs", [CK, NB * CH])
        rm = sb("rm", [128, PAIRS])
        nb = sb("nb", [128, PAIRS])
        den = sb("den", [128, PAIRS])
        rden = sb("rden", [128, PAIRS])
        rdm = sb("rdm", [128, PAIRS, 2])
        m8 = sb("m8", [128, TOPK])
        M3 = big[:, 0:2048].rearrange("p (h d) -> p h d", h=NH)
        Q3 = big[:, 2048:9216].rearrange("p (h t) -> p h t", h=NH)
        W3r = flat[:, 1024:4096]
        W3T = flat[:, 4096:7168]
        G3 = flat[:, 7168:9216].rearrange("p (h d) -> p h d", h=NH)
        wo3 = sb("wo3", [128, PAIRS, D])
        LT = sb("LT", [D, T])
        LN_ = sb("LN_", [NQ, NB, D])

        H = VV[:, 0, 0:3 * T].rearrange("p (r t) -> p r t", r=3)
        HG = KTT[:, 0, 0:3 * T].rearrange("p (r t) -> p r t", r=3)
        GH = E[:, 0:2 * T].rearrange("p (r t) -> p r t", r=2)
        lg = sb("lg", [NQ, NB, NEXP])
        top = sb("top", [NQ, NB, 8])
        tidx = sb("tidx", [NQ, NB, 8], U32)
        tif = sb("tif", [NQ, NB, 2])
        ex = sb("ex", [NQ, NB, NEXP])
        dl = sb("dl", [NQ, NB, NEXP])
        sm = sb("sm", [NQ, NB])
        wt = sb("wt", [NQ, NB, 2])
        gt = sb("gt", [NQ, NB, NEXP])
        gt2 = sb("gt2", [NQ, NB, NEXP])
        GT = sb("GT", [NEXP, T])
        cst = sb("cst", [D, 2, NQ])
        gates = sb("gates", [D, 3, NQ])
        gtmp = sb("gtmp", [D, 2, NQ])

        PS = ctx.enter_context(nc.psum_tensor("PS", [128, 4, 512], F32))
        TR = ctx.enter_context(nc.psum_tensor("TR", [128, 2, 512], F32))
        PO = ctx.enter_context(nc.psum_tensor("PO", [128, 512], F32))
        PM = ctx.enter_context(nc.psum_tensor("PM", [128, 512], F32))

        RAWS = ["L0_ffn_wf", "L0_ffn_uf", "L0_ffn_wi", "L0_ffn_ui", "L0_ffn_wc", "L0_ffn_uc",
                "L0_ffn_wo", "L0_ffn_uo", "L2_xattn_Wq", "L2_xattn_Wk", "L3_ffn_W"]
        tw = {n: TW[:, i, :] for i, n in enumerate(RAWS)}
        WQ = [wq[0][:, :], wq[1][:, :], tw["L2_xattn_Wq"]]
        WK = [wk[0][:, :], wk[1][:, :], tw["L2_xattn_Wk"]]

        def row(ap):
            return ap.rearrange("(a n) -> a n", a=1)

        def column(ap):
            return ap.rearrange("(n a) -> n a", a=1)

        def stand(eng, sem, value):
            eng.wait_ge(sem, value)
            eng.sem_inc(S("turns"), 1)

        block = ctx.enter_context(nc.Block())
        IN_ORDER = ["attn0", "scan", "attn1", "moe1", "attn2", "moe2", "attn3", "lora"]

        @block.sync
        def _(sp):
            sp.dma_start(X[:, :, :], A["x"].rearrange("b q d -> q b d")).then_inc(S("x_in"), 16)
            sp.dma_start(MI[:, :], A["mask_1x1xSxS2_ik1"][0, 0, :, :]).then_inc(S("mask_in"), 16)
            for layer in range(4):
                with sp.Fori(0, NB) as b:
                    if layer in (0, 2, 3):
                        if layer == 3:
                            stand(sp, S("v3_ready"), 4 * b + PRIME)
                            stand(sp, S("xt_made"), b + PRIME)
                        else:
                            stand(sp, S(f"nat_used{layer}"), b + PRIME)
                        if layer:
                            sp.wait_ge(S(f"nat_used{[0, 0, 0, 2][layer]}"), NB + PRIME)
                        sp.dma_start(NAT[:, :, :], A["ctx_1024"][bass.ds(b, 1), :, :].rearrange(
                            "a (p c) d -> p (a c) d", c=CH)).then_inc(S(f"nat_in{layer}"), 16)
                    if layer in (1, 2):
                        sp.wait_ge(S("ct_saved"), 16 * NB + 16)
                        sp.wait_ge(S("ct_used0"), NB)
                        if layer == 2:
                            sp.wait_ge(S("ct_used1"), NB + PRIME)
                        stand(sp, S(("", "ct_used1", "k_ps2")[layer]), b + PRIME)
                        sp.dma_start(CT[:, :], scratch[bass.ds(b, 1), :, :].rearrange(
                            "a p n -> p (a n)")).then_inc(S(f"ct_in{layer}"), 16)
                    if layer == 0:
                        stand(sp, S("ct_made"), b + 1)
                        sp.dma_start(scratch[bass.ds(b, 1), :, :].rearrange("a p n -> p (a n)"),
                                     CT[:, :]).then_inc(S("ct_saved"), 16)
            sp.wait_ge(S("x_final"), 1)
            sp.dma_start(out.rearrange("b q d -> q b d"), X[:, :, :]).then_inc(S("out_saved"), 16)
            sp.wait_ge(S("out_saved"), 16)
            sp.wait_ge(S("ct_saved"), 16 * NB + 16)

        @block.gpsimd
        def _(pool):
            n = [0]

            def link(ins):
                n[0] += 1
                ins.then_inc(S("pool_step"), 1)
                pool.wait_ge(S("pool_step"), n[0])

            for name in ("nat_used0", "nat_used2", "v3_ready", "xt_made", "ct_used1", "k_ps2", "scores_out",
                         "tail2", "tr_used2", "tail0", "tail1", "tail3"):
                pool.sem_inc(S(name), PRIME)
            pool.sem_inc(S("ct_saved"), 16)
            pool.sem_inc(S("pv_ready2"), PV_PRIME)
            pool.sem_inc(S("tr_ready2"), TR_PRIME)
            for layer in (0, 1, 3):
                pool.sem_inc(S(f"weighed{layer}"), WEIGHED)

            link(pool.memset(ident[:, :], 0.0))
            link(pool.memset(ones[:, :], 1.0))
            link(pool.memset(esel[:, :, :], 0.0))
            link(pool.memset(epst[:, :], EPS))
            link(pool.memset(QB[:, :, :], 0.0))
            link(pool.memset(hmask[:, :], 1.0))
            link(pool.memset(pmask[:, :], 1.0))
            link(pool.affine_select(out=ident[:, :], in_=ident[:, :], compare_op=ALU.not_equal, fill=1.0,
                                    base=0, pattern=[[-1, 128]], channel_multiplier=1))
            link(pool.affine_select(out=esel[:, :, :], in_=esel[:, :, :], compare_op=ALU.not_equal, fill=1.0,
                                    base=0, pattern=[[-1, NEXP], [0, 128]], channel_multiplier=1))
            link(pool.memset(pm[:, :], 1.0))
            link(pool.memset(VV[:, :, :], 1.0))
            link(pool.memset(I8[:, :], 0.0))
            link(pool.memset(MM[:, :], 0.0))
            i8 = I8[:, :].rearrange("p (h q) -> p h q", q=NQ)
            link(pool.affine_select(out=i8, in_=i8, compare_op=ALU.not_equal, fill=1.0,
                                    base=0, pattern=[[0, 8], [-1, NQ]], channel_multiplier=1))
            for m, w, k in ((hmask, DH, NH), (pmask, HQ, 2), (pm, NQ, 2)):
                link(pool.affine_select(out=m[:, :], in_=m[:, :], compare_op=ALU.is_ge, fill=0.0,
                                        base=0, pattern=[[-w, k]], channel_multiplier=1))
                link(pool.affine_select(out=m[:, :], in_=m[:, :], compare_op=ALU.is_ge, fill=0.0,
                                        base=w - 1, pattern=[[w, k]], channel_multiplier=-1))
            link(pool.iota(iota8[:, :], pattern=[[1, NEXP]], base=0, channel_multiplier=0,
                           allow_small_or_imprecise_dtypes=True))
            pool.tensor_tensor(sel[:, :], ident[:, 0:NQ], ident[:, HQ:HQ + NQ], ALU.add).then_inc(S("const"), 1)

            def load(dst, src, name):
                pool.dma_start(dst, src, allow_slow_non_contiguous=True).then_inc(S(name), 16)

            def queries(layer):
                pool.wait_ge(S("q_ready"), layer + 1)
                with pool.Fori(0, NB // 2) as i:
                    for par in range(2):
                        stand(pool, S(f"weighed{layer}"), 2 * (2 * i + par) - 2 + WEIGHED)
                        pool.tensor_tensor(
                            QP[:, par, :].rearrange("p (h q) -> p h q", q=NQ),
                            QT[:, bass.ds((2 * i + par) * NQ, NQ)].rearrange("p (a q) -> p a q", a=1)
                            .to_broadcast([D, NH, NQ]),
                            hmask[:, :].rearrange("p (h a) -> p h a", a=1).to_broadcast([D, NH, NQ]),
                            ALU.mult).then_inc(S(f"q_made{layer}"), 1)

            for i, nme in enumerate(("Wq", "Wk", "Wv", "Wo")):
                load((wq, wk, wv, wo)[i][0][:, :], A[f"L0_xattn_{nme}"], "w_l0")
            load(colat["bq"], column(A["L0_xattn_bq"]), "w_l0")
            load(colat["bk"], column(A["L0_xattn_bk"]), "w_l0")
            load(colat["bv"], column(A["L0_xattn_bv"]), "w_l0")
            load(rbo0, row(A["L0_xattn_bo"]), "w_l0")
            for i, nme in enumerate(RAWS):
                load(RAW[:, i, :], A[nme], "w_raw")
            for a in ("bf", "bi", "bc", "in_c"):
                load(colat[a], column(A[f"L0_ffn_{a}"]), "w_col")
            for a in ("w1", "b1", "w2", "b2"):
                load(colat[a], column(A[f"L3_xattn_ln{a[1]}_{a[0]}"]), "w_col")
            load(rbos, row(A["L0_ffn_bo"]), "w_col")
            load(rbo1, row(A["L1_xattn_b_o"]), "w_col")
            load(rb3, row(A["L3_ffn_b"]), "w_col")
            queries(0)
            for i, nme in enumerate(("w_q", "w_k", "w_v", "w_o")):
                load((wq, wk, wv, wo)[i][1][:, :], A[f"L1_xattn_{nme}"], "w_l1")
            load(w1a, A["L1_ffn_W1"].rearrange("e p f -> p e f"), "w_moe1")
            load(w2a, A["L1_ffn_W2"].rearrange("e (k p) d -> p e k d", p=128), "w_moe1")
            load(b1a, A["L1_ffn_b1"].rearrange("e (k p) -> p (e k)", p=128), "w_moe1")
            load(wg1[:, :], A["L1_ffn_Wg"], "w_moe1")
            load(grow[:, 0, :], row(A["L1_ffn_bg"]), "w_moe1")
            load(b2a[:, :], A["L1_ffn_b2"], "w_moe1")
            load(b1b[:, 0:16], A["L2_ffn_be1"].rearrange("e (k p) -> p (e k)", p=128), "w_moe2")
            load(b1b[:, 16:18], A["L2_ffn_bs1"].rearrange("(k p) -> p k", p=128), "w_moe2")
            load(gb1, A["L2_ffn_gb1"].rearrange("(k p) -> p k", p=128), "w_moe2")
            load(gw2[:, :, :], A["L2_ffn_gw2"].rearrange("(k p) e -> p k e", p=128), "w_moe2")
            load(grow[:, 1, :], row(A["L2_ffn_gb2"]), "w_moe2")
            load(b2b[:, :], A["L2_ffn_be2"], "w_moe2")
            load(bs2[:, :], row(A["L2_ffn_bs2"]), "w_moe2")
            load(wo3[:, :, :], A["L3_xattn_Wo"].rearrange("(j p) d -> p j d", p=128), "w_l3s")
            for dst, src, k in ((w1B, "ln1_w", 128), (b1B, "ln1_b", 128), (w2B, "ln2_w", NQ), (b2B, "ln2_b", NQ)):
                load(dst[:, :], A[f"L3_xattn_{src}"].partition_broadcast(k), "w_l3s")
            for dst, src in ((ld_, "lora_down"), (lu_, "lora_up"), (da_, "down_aux"), (ua_, "up_aux")):
                load(dst, A[f"L3_ffn_{src}"], "w_lora")
            queries(1)
            pool.wait_ge(S("moe_done"), 1)
            load(w1b[:, 0:8, :], A["L2_ffn_We1"].rearrange("e p f -> p e f"), "w_moe2")
            load(w1b[:, 8, :], A["L2_ffn_Ws1"], "w_moe2")
            load(w2b[:, 0:8, :, :], A["L2_ffn_We2"].rearrange("e (k p) d -> p e k d", p=128), "w_moe2")
            load(w2b[:, 8, :, :], A["L2_ffn_Ws2"].rearrange("(k p) d -> p k d", p=128), "w_moe2")
            load(gw1, A["L2_ffn_gw1"], "w_moe2")
            def operands(b):
                if not isinstance(b, int):
                    stand(pool, S("s_ready2"), PAIRS * b)
                pool.tensor_tensor(
                    QB[:, :, 0:NQ],
                    QT[:, bass.ds(b * NQ, NQ)].rearrange("p (a q) -> p a q", a=1).to_broadcast([D, NH, NQ]),
                    hmask[:, :].rearrange("p (h a) -> p h a", a=1).to_broadcast([D, NH, NQ]),
                    ALU.mult).then_inc(S("qb_ready2"), 1)
                pool.wait_ge(S("nat_in2"), 16 * (b + 1))
                if not isinstance(b, int):
                    stand(pool, S("pv_ready2"), PAIRS * b + PV_PRIME)
                pool.tensor_copy(V[0:CK, 0:CH, :], NAT[:, :, :]).then_inc(S("nat_used2"), 1)

            pool.wait_ge(S("q_ready"), 3)
            operands(0)
            with pool.Fori(1, NB) as b:
                operands(b)
            pool.wait_ge(S("moe_done"), 2)
            load(W3r[:, 0:1024], A["L3_xattn_Wq"], "w_l3")
            load(W3r[:, 1024:3072], A["L3_xattn_Wkv"], "w_l3")
            pool.wait_ge(S("w_l3s"), 16 * 5)
            pool.wait_ge(S("xn_ready"), 8)
            link(pool.tensor_tensor(LN_[:, :, :], XN2[:, :, :],
                                    w2B[:, :].rearrange("p (a d) -> p a d", a=1).to_broadcast([NQ, NB, D]), ALU.mult))
            link(pool.tensor_tensor(LN_[:, :, :], LN_[:, :, :],
                                    b2B[:, :].rearrange("p (a d) -> p a d", a=1).to_broadcast([NQ, NB, D]), ALU.add))
            base = n[0]
            pool.wait_ge(S("lat_t"), 1)
            pool.wait_ge(S("q3_ready"), NH)
            with pool.Fori(0, NB // 2) as i:
                for par in range(2):
                    b = 2 * i + par
                    stand(pool, S("weighed3"), 2 * b - 2 + WEIGHED)
                    pool.tensor_copy(KTT[:, par, NK:NK3], LT[:, bass.ds(b * NQ, NQ)]).then_inc(S("v3_ready"), 1)
                    pool.tensor_copy(V3[0:NQ, par, CH, :], LN_[:, bass.ds(b, 1), :].rearrange("p a d -> p (a d)"))\
                        .then_inc(S("v3_ready"), 1)
                    pool.tensor_copy(QP[:, par, :].rearrange("p (h q) -> p h q", q=NQ),
                                     Q3[:, :, bass.ds(b * NQ, NQ)]).then_inc(S("v3_ready"), 1)
                    pool.wait_ge(S("cn_ready"), b + 1)
                    pool.tensor_tensor(V3[0:CK, par, 0:CH, :], NAT[:, :, :],
                                       w1B[0:CK, :].rearrange("p (a d) -> p a d", a=1).to_broadcast([CK, CH, D]),
                                       ALU.mult).then_inc(S("pool_step"), 1)
                    pool.wait_ge(S("pool_step"), b + base + 1)
                    pool.tensor_tensor(V3[0:CK, par, 0:CH, :], V3[0:CK, par, 0:CH, :],
                                       b1B[0:CK, :].rearrange("p (a d) -> p a d", a=1).to_broadcast([CK, CH, D]),
                                       ALU.add).then_inc(S("v3_ready"), 1)

        @block.tensor
        def _(pe):
            def ln_pe(k, src):
                pe.wait_ge(S("xn_ready"), k + 1)
                for b in range(NB):
                    mm = pe.transpose(PM[:, b * NQ:(b + 1) * NQ], src[:, b, :], ident[0:NQ, 0:NQ])
                mm.then_inc(S("xnt_ps"), 1)
                pe.wait_ge(S("xnt_ready"), k + 1)

            def unit_pe(layer):
                prep, chunks, ahead, turn = plan(layer)
                made, used = S(f"bank_made{layer}"), S(f"bank_used{layer}")

                def size(c):
                    return CK if c < CH else NQ

                def bank(ring):
                    r, n = ring.next()
                    if not (isinstance(n, int) and n <= 4):
                        pe.wait_ge(used, n - 4)
                    return PS[:, r, :]

                def prepare(ring, b):
                    if layer == 0:
                        pe.wait_ge(S("nat_in0"), 16 * (b + 1))
                    elif layer == 1:
                        pe.wait_ge(S("ct_in1"), 16 * (b + 1))
                    else:
                        pe.wait_ge(S("cn_ready"), b + 1)
                    for kind, g in prep:
                        o = bank(ring)
                        if kind == "ct" or kind == "xt":
                            n = 4 if kind == "ct" else 3
                            for i in range(n):
                                mm = pe.transpose(o[:, i * CK:(i + 1) * CK], NAT[:, n * g + i, :], ident[0:CK, 0:CK])
                        elif kind == "kt":
                            if layer == 0 and g == 0:
                                pe.wait_ge(S("ct_made"), b + 1)
                            mm = pe.matmul(o[:, 0:500], WK[layer], CT[:, g * 500:(g + 1) * 500],
                                           start=True, stop=True)
                        else:
                            n = CH // len([e for e in prep if e[0] == "v"])
                            for i in range(n):
                                c = n * g + i
                                mm = pe.matmul(o[0:CK, i * D:(i + 1) * D], CT[:, c * CK:(c + 1) * CK],
                                               wv[layer][:, :], start=True, stop=True)
                        mm.then_inc(made, 1)

                def score(ring, c, par, half):
                    o = bank(ring)[0:size(c), 0:UNIT]
                    if layer == 1:
                        pe.matmul(o, MM[:, c * CK:c * CK + size(c)], I8[:, :], start=True, stop=False)
                    pe.matmul(o, KTT[:, par, c * CK:c * CK + size(c)],
                              QP[:, par, half * UNIT:(half + 1) * UNIT],
                              start=(layer != 1), stop=True).then_inc(made, 1)

                def maxima_turn(u, up):
                    pe.wait_ge(S(f"chunk_max{layer}"), u + 1)
                    for i in range(4):
                        mm = pe.transpose(TR[0:PAIR, 0, i * CK:(i + 1) * CK],
                                          ACC[:, up, 0, i * PAIR:(i + 1) * PAIR], ident[0:CK, 0:CK])
                    mm.then_inc(S(f"max_turned{layer}"), 1)

                def maxima_spread(u):
                    pe.wait_ge(S(f"diag_made{layer}"), u + 1)
                    pe.matmul(TR[0:CK, 1, 0:UNIT], ones[0:PAIR, 0:CK], DG[:, :, :], start=True, stop=True)\
                      .then_inc(S(f"max_spread{layer}"), 1)

                def weigh(u, up, par, half):
                    o = (PO, PM)[up]
                    for p in range(3):
                        pe.wait_ge(S(f"exp_made{layer}"), 3 * u + p + 1)
                        cs = [4 * p, 4 * p + 1, 4 * p + 2, 4 * p + 3] + ([CH] if p == 2 and chunks > CH else [])
                        if layer == 3:
                            for c in cs:
                                mm = pe.matmul(o[:, 0:UNIT], V3[0:size(c), par, c, :], SU[0:size(c), up, c, :],
                                               start=(c == 0), stop=(c == chunks - 1))
                        else:
                            for i in range(4):
                                for c in cs:
                                    mm = pe.matmul(o[0:PAIR, i * VW:(i + 1) * VW],
                                                   SU[0:CK, up, c, i * PAIR:(i + 1) * PAIR],
                                                   VP[0:CK, par, c, 4 * half + i, :],
                                                   start=(c == 0 and i == 0), stop=(c == CH - 1 and i == 3),
                                                   skip_group_check=True)
                    mm.then_inc(S(f"weighed{layer}"), 1)
                    if layer == 3:
                        pe.wait_ge(S("sums_made"), u + 1)
                        pe.matmul(TR[:, 1, 0:UNIT], ones[0:CK, :], SUMS[:, up, :], start=True, stop=True)\
                          .then_inc(S("sums_spread"), 1)

                def project(b):
                    if layer < 3:
                        pe.wait_ge(S(f"z_ready{layer}"), 2 * b + 2)
                        pe.transpose(TR[:, 0, 0:PAIR], ZU[:, :, :, :].rearrange("p j h d -> p (j h d)"),
                                     ident[0:PAIR, 0:PAIR]).then_inc(S(f"zt_ps{layer}"), 1)
                        pe.wait_ge(S(f"zt_ready{layer}"), b + 1)
                        y = TR[0:NQ, 0, 128:256]
                        pe.matmul(y, ZT[:, 0:NQ], wo[layer][:, :], start=True, stop=False)
                        pe.matmul(y, ZT[:, NQ:PAIR], wo[layer][:, :], start=False, stop=False)
                        pe.matmul(y, ones[0:1, 0:NQ], rbv if layer == 0 else rbo1,
                                  start=False, stop=True).then_inc(S(f"y_ready{layer}"), 1)
                    else:
                        pe.wait_ge(S("o3_ready"), 2 * b + 2)
                        for h in range(NH):
                            mm = pe.matmul(TR[0:NQ, 0, 128:256], O3[:, h, :], M3[:, h, :],
                                           start=(h == 0), stop=(h == NH - 1))
                        mm.then_inc(S(f"y_ready{layer}"), 1)

                def first_scores_wait(ring_end, b):
                    pe.wait_ge(used, ring_end)
                    if layer == 3:
                        pe.wait_ge(S("v3_ready"), 4 * b + 3 + PRIME)
                    else:
                        pe.wait_ge(S(f"q_made{layer}"), b + 1)

                def slot(ring, i, s):
                    u, b = 4 * i + s, 2 * i + s // 2
                    half = up = s % 2
                    final = isinstance(b, int) and b == NB - 1
                    pe.wait_ge(S(f"tail{layer}"), b + PRIME)
                    if final and half:
                        maxima_turn(u, up)
                        maxima_spread(u)
                    else:
                        if half:
                            first_scores_wait(ring.base + ring.k, b + 1)
                        for c in range(chunks):
                            score(ring, c, (s // 2 + half) % 2, 1 - half)
                            if c == 1:
                                maxima_turn(u, up)
                            if c == 5:
                                maxima_spread(u)
                    if not half and not final:
                        prepare(ring, b + 1)
                    if layer == 3:
                        pe.wait_ge(S("v3_ready"), 4 * b + 4 + PRIME)
                    weigh(u, up, s // 2, half)
                    if half:
                        project(b)

                ring = Ring(0, 0)
                prepare(ring, 0)
                first_scores_wait(ring.k, 0)
                for c in range(chunks):
                    score(ring, c, 0, 0)
                n0 = ring.k
                with pe.Fori(0, NB // 2 - 1) as i:
                    ring = Ring(i * len(turn) + n0, n0)
                    for s in range(4):
                        slot(ring, i, s)
                    assert ring.k == len(turn)
                ring = Ring((NB // 2 - 1) * len(turn) + n0, n0)
                for s in range(4):
                    slot(ring, NB // 2 - 1, s)
                pe.wait_ge(S(f"tail{layer}"), NB + PRIME)

            def top_pe():
                def keys(b):
                    pe.wait_ge(S("ct_in2"), 16 * (b + 1))
                    pe.wait_ge(S("scores_out"), PAIRS * b + PRIME)
                    for n in range(3):
                        mm = pe.matmul(PS[:, n, 0:500], WK[2], CT[:, n * 500:(n + 1) * 500],
                                       start=True, stop=True)
                    mm.then_inc(S("k_ps2"), 1)

                def scores(b, j):
                    if j == 0:
                        pe.wait_ge(S("qb_ready2"), b + 1)
                        pe.wait_ge(S("k_ready2"), b + 1)
                    else:
                        pe.wait_ge(S("scores_out"), PAIRS * b + j + PRIME)
                    for n in range(3):
                        mm = pe.matmul(PS[:, n, 0:500], QB[:, 2 * j:2 * j + 2, :], KT[:, n * 500:(n + 1) * 500],
                                       start=True, stop=True)
                    mm.then_inc(S("s_ready2"), 1)

                def turn_batch(b, last):
                    k, at = [0], []

                    def turn(j, cs):
                        i = k[0]
                        k[0] += 1
                        stand(pe, S("tr_used2"), b * TURNS + (i - 1 if i >= 2 else 0) + PRIME)
                        for n, c in enumerate(cs):
                            mm = pe.transpose(TR[0:CK, i % 2, n * 128:(n + 1) * 128],
                                              P[:, j % 2, c * CK:(c + 1) * CK], ident[:, :])
                        mm.then_inc(S("tr_ready2"), 1)
                        at.append(k[0])

                    def gather(j, g):
                        pe.wait_ge(S("tr_used2"), b * TURNS + at[3 * j + g] + PRIME)
                        for c in groups(CH)[g]:
                            mm = pe.matmul(PO[:, j * 16:(j + 1) * 16], PT[0:CK, j % 2, c, :],
                                           V[0:CK, c, 16 * j:16 * j + 16], start=(c == 0), stop=(c == CH - 1))
                        return mm

                    for j in range(PAIRS):
                        if j < PAIRS - 1:
                            scores(b, j + 1)
                        elif not last:
                            scores(b + 1, 0)
                        if j == PAIRS - 2 and not last:
                            keys(b + 1)
                        if j == 0:
                            pe.wait_ge(S("nat_used2"), b + 1 + PRIME)
                        pe.wait_ge(S("p_ready2"), b * PAIRS + j + 1)
                        turn(j, groups(CH)[0])
                        for g in range(1, 3):
                            turn(j, groups(CH)[g])
                            gather(j, g - 1)
                        gather(j, 2).then_inc(S("pv_ready2"), 1)
                    assert k[0] == TURNS
                    pe.wait_ge(S("z_ready2"), b + 1)
                    pe.wait_ge(S("tail2"), b + PRIME)
                    pe.matmul(PM[0:NQ, 128:256], sel[:, :], Z, start=True, stop=True)\
                      .then_inc(S("y_ready2"), 1)

                keys(0)
                scores(0, 0)
                with pe.Fori(0, NB - 1) as b:
                    turn_batch(b, False)
                turn_batch(NB - 1, True)
                pe.wait_ge(S("tail2"), NB + PRIME)

            pe.wait_ge(S("const"), 1)
            pe.wait_ge(S("w_raw"), 16 * len(RAWS))
            for i in range(len(RAWS)):
                if i >= 4:
                    pe.wait_ge(S("tw_ready"), i - 3)
                pe.transpose(PS[:, i % 4, 0:128], RAW[:, i, :], ident[:, :]).then_inc(S("tw_ps"), 1)
            pe.wait_ge(S("tw_ready"), len(RAWS))

            def project_q(layer):
                pe.matmul(PM[:, 0:T], WQ[layer], XNT[:, :], start=True, stop=True)\
                  .then_inc(S("q_ps"), 1)
                pe.wait_ge(S("q_ready"), layer + 1)

            pe.wait_ge(S("w_l0"), 16 * 8)
            pe.matmul(PO[0:1, 0:D], colat["bv"], wo[0][:, :], start=True, stop=False)
            pe.matmul(PO[0:1, 0:D], ones[0:1, 0:1], rbo0, start=False, stop=True).then_inc(S("bvo_ps"), 1)
            pe.wait_ge(S("bvo_made"), 1)
            ln_pe(0, XN)
            project_q(0)
            unit_pe(0)
            ln_pe(1, XN)
            pe.wait_ge(S("w_col"), 16 * 11)
            for t in range(NB):
                pe.wait_ge(S("c_ready"), t + 1)
                for g, n_ in enumerate(("f", "i", "c")):
                    o = PS[:, t % 2, g * NQ:(g + 1) * NQ]
                    pe.matmul(o, tw[f"L0_ffn_w{n_}"], XNT[:, t * NQ:(t + 1) * NQ], start=True, stop=False)
                    mm = pe.matmul(o, tw[f"L0_ffn_u{n_}"], cst[:, t % 2, :], start=False, stop=True)
                mm.then_inc(S("z_gates"), 1)
            pe.wait_ge(S("c_ready"), NB + 1)
            for t in range(NB):
                o = TR[0:NQ, t // 4, (t % 4) * D:(t % 4 + 1) * D]
                pe.matmul(o, XNT[:, t * NQ:(t + 1) * NQ], tw["L0_ffn_wo"], start=True, stop=False)
                pe.matmul(o, cst[:, NB % 2, :], tw["L0_ffn_uo"], start=False, stop=False)
                mm = pe.matmul(o, ones[0:1, 0:NQ], rbos, start=False, stop=True)
            mm.then_inc(S("h_ps"), 1)

            pe.wait_ge(S("w_l1"), 16 * 4)
            ln_pe(2, XN)
            project_q(1)
            pe.wait_ge(S("mask_made"), 1)
            unit_pe(1)

            def moe_pe(which):
                blocks = moe_blocks(which)
                w1, w2, b2 = (w1a, w2a, b2a) if which == 0 else (w1b, w2b, b2b)
                if which == 0:
                    pe.wait_ge(S("w_moe1"), 16 * 6)
                    for b in range(NB):
                        o = PO[0:NQ, b * NEXP:(b + 1) * NEXP]
                        pe.matmul(o, XNT[:, b * NQ:(b + 1) * NQ], wg1[:, :], start=True, stop=False)
                        mm = pe.matmul(o, ones[0:1, 0:NQ], grow[:, 0, :], start=False, stop=True)
                else:
                    pe.wait_ge(S("w_moe2"), 16 * 12)
                    for k in range(2):
                        mm = pe.matmul(PS[:, k, 0:T], gw1[:, k * 128:(k + 1) * 128], XNT[:, :],
                                       start=True, stop=True)
                    mm.then_inc(S("gh_ps"), 1)
                    pe.wait_ge(S("gh_ready"), 2)
                    for b in range(NB):
                        o = PO[0:NQ, b * NEXP:(b + 1) * NEXP]
                        for k in range(2):
                            pe.matmul(o, GH[:, k, b * NQ:(b + 1) * NQ], gw2[:, k, :], start=(k == 0), stop=False)
                        mm = pe.matmul(o, ones[0:1, 0:NQ], grow[:, 1, :], start=False, stop=True)
                mm.then_inc(S("lg_ps"), 1)
                pe.wait_ge(S("gate_ready"), which + 1)
                for b in range(NB):
                    mm = pe.transpose(PO[0:NEXP, b * NQ:(b + 1) * NQ], gt[:, b, :], ident[0:NQ, 0:NQ])
                mm.then_inc(S("gt_ps"), 1)
                pe.wait_ge(S("gt_ready"), which + 1)
                done = len(moe_blocks(0)) if which else 0
                edone = NEXP if which else 0
                acc = PM[:, 0:T]
                pe.matmul(acc, b2[:, :], GT[:, :], start=True, stop=False, skip_group_check=True)
                if which:
                    pe.matmul(acc, bs2[:, :], ones[0:1, 0:1].to_broadcast([1, T]), start=False, stop=False,
                              skip_group_check=True)

                def down(i):
                    e, k = blocks[i]
                    pe.wait_ge(S("hg_ready"), done + i + 1)
                    pe.matmul(acc, w2[:, e, k, :], HG[:, i % 3, :], start=False,
                              stop=(i == len(blocks) - 1), skip_group_check=True).then_inc(S("down_ps"), 1)

                for i, (e, k) in enumerate(blocks):
                    if k == 0 and e < NEXP:
                        if e >= 2:
                            pe.wait_ge(S("hg_ready"), done + (e - 1) * blocks_per(which))
                        pe.matmul(TR[:, e % 2, 0:T], esel[:, e, :], GT[:, :], start=True, stop=True)\
                          .then_inc(S("gb_ps"), 1)
                    if i >= 4:
                        pe.wait_ge(S("gelu_ready"), done + i - 3)
                    pe.matmul(PS[:, i % 4, 0:T], w1[:, e, k * 128:(k + 1) * 128], XNT[:, :],
                              start=True, stop=True).then_inc(S("up_ps"), 1)
                    if i >= 3:
                        down(i - 3)
                for i in range(len(blocks) - 3, len(blocks)):
                    down(i)
                pe.wait_ge(S("yt_ready"), which + 1)
                for b in range(NB):
                    mm = pe.transpose(PS[0:NQ, b // 4, (b % 4) * D:(b % 4 + 1) * D], YT[:, b * NQ:(b + 1) * NQ],
                                      ident[:, :])
                mm.then_inc(S("y_nat"), 1)

            ln_pe(3, XN)
            moe_pe(0)
            ln_pe(4, XN)
            project_q(2)
            top_pe()
            ln_pe(5, XN)
            moe_pe(1)
            pe.wait_ge(S("w_l3"), 32)
            pe.wait_ge(S("w_l3s"), 16 * 5)
            for i in range(24):
                if i >= 4:
                    pe.wait_ge(S("w3t_ready"), i - 3)
                else:
                    pe.wait_ge(S("x_upd"), 6)
                pe.transpose(PS[:, i % 4, 0:128], W3r[:, i * 128:(i + 1) * 128], ident[:, :])\
                  .then_inc(S("w3t_ps"), 1)
            pe.wait_ge(S("w3t_ready"), 24)
            for h in range(NH):
                lo_, j = (h % 2) * DH3, h // 2
                if h >= 2:
                    pe.wait_ge(S("gm_ready"), 2 * (h - 1))
                pe.matmul(PS[:, h % 2, 0:D], W3T[lo_:lo_ + DH3, j * 128:(j + 1) * 128],
                          W3T[lo_:lo_ + DH3, 1024 + j * 128:1024 + (j + 1) * 128],
                          start=True, stop=True).then_inc(S("gm_ps"), 1)
                pe.matmul(PS[:, 2 + h % 2, 0:D], W3T[lo_:lo_ + DH3, 2048 + j * 128:2048 + (j + 1) * 128],
                          wo3[lo_:lo_ + DH3, j, :], start=True, stop=True).then_inc(S("gm_ps"), 1)
            pe.wait_ge(S("gm_ready"), 2 * NH)
            ln_pe(6, XN)
            ln_pe(7, XN2)
            pe.wait_ge(S("lat_t"), 1)
            for h in range(NH):
                if h >= 4:
                    pe.wait_ge(S("q3_ready"), h - 3)
                pe.matmul(PS[:, h % 4, 0:T], G3[:, h, :], LT[:, :], start=True, stop=True)\
                  .then_inc(S("q3_ps"), 1)
            pe.wait_ge(S("q3_ready"), NH)
            unit_pe(3)
            pe.wait_ge(S("w_lora"), 64)
            pe.transpose(TR[0:100, 0, 0:4], ld_, ident[0:4, 0:4])
            pe.transpose(TR[0:4, 0, 4:54], lu_, ident[0:50, 0:50])
            pe.transpose(TR[0:50, 0, 128:256], ua_, ident[:, :]).then_inc(S("lora_ps"), 1)
            pe.wait_ge(S("lora_ready"), 3)
            pe.matmul(TR[0:4, 1, 0:128], ldT, da_, start=True, stop=True).then_inc(S("lora_ps"), 1)
            pe.wait_ge(S("lora_ready"), 4)
            pe.matmul(TR[0:50, 1, 128:256], luT, t1_, start=True, stop=True).then_inc(S("lora_ps"), 1)
            pe.wait_ge(S("lora_ready"), 5)
            pe.matmul(TR[:, 1, 256:384], t2_, uaT, start=True, stop=True).then_inc(S("lora_ps"), 1)
            pe.wait_ge(S("lora_ready"), 6)
            ln_pe(8, XN)
            for b in range(NB):
                o = PS[0:NQ, b // 4, (b % 4) * D:(b % 4 + 1) * D]
                x_ = XNT[:, b * NQ:(b + 1) * NQ]
                pe.matmul(o, x_, tw["L3_ffn_W"], start=True, stop=False)
                pe.matmul(o, ones[0:1, 0:NQ], rb3, start=False, stop=False)
                mm = pe.matmul(o, x_, lwT, start=False, stop=True)
            mm.then_inc(S("y_last"), 1)

        @block.scalar
        def _(act):
            def std_act(k):
                act.wait_ge(S("var_ready"), k + 1)
                act.activation(std[:, :], mv[:, :, 1], ACT.Sqrt, bias=epst[0:NQ, :]).then_inc(S("std_ready"), 1)

            def ln_act(k, dst=None, w=1.0, bias=0.0):
                std_act(k)
                act.wait_ge(S("xnt_ps"), k + 1)
                act.activation((XNT if dst is None else dst)[:, :], PM[:, 0:T], ACT.Identity,
                               bias=bias, scale=w).then_inc(S("xnt_ready"), 1)

            def q_act(layer):
                act.wait_ge(S("q_ps"), layer + 1)
                act.activation(QT[:, :], PM[:, 0:T], ACT.Identity,
                               bias=colat["bq"] if layer == 0 else 0.0).then_inc(S("q_ready"), 1)

            def unit_act(layer):
                prep, chunks, ahead, turn = plan(layer)
                made, used = S(f"bank_made{layer}"), S(f"bank_used{layer}")

                def size(c):
                    return CK if c < CH else NQ

                def bank(ring):
                    r, n = ring.next()
                    act.wait_ge(made, n)
                    return PS[:, r, :]

                def prepare(ring, b, par):
                    for kind, g in prep:
                        if kind == "ct" and g == 0:
                            act.wait_ge(S("ct_saved"), 16 * b + 16)
                        o = bank(ring)
                        if kind == "ct":
                            act.activation(CT[:, g * 500:(g + 1) * 500], o[:, 0:500], ACT.Copy).then_inc(used, 1)
                        elif kind == "xt":
                            act.activation(KTT[:, par, g * 375:(g + 1) * 375], o[:, 0:375], ACT.Identity,
                                           scale=colat["w1"], bias=colat["b1"]).then_inc(used, 1)
                        elif kind == "kt":
                            act.activation(KTT[:, par, g * 500:(g + 1) * 500], o[:, 0:500], ACT.Identity,
                                           bias=colat["bk"] if layer == 0 else 0.0).then_inc(used, 1)
                        else:
                            n = CH // len([e for e in prep if e[0] == "v"])
                            act.activation(VP[0:CK, par, n * g:n * g + n, :, 0:2 * DH],
                                           o[0:CK, 0:n * D].rearrange("p (c j w) -> p c j w", c=n, w=2 * DH),
                                           ACT.Copy).then_inc(used, 1)
                        if (kind, g) in (("ct", 2), ("xt", 3)):
                            act.wait_ge(used, ring.base + ring.k)
                            act.nop().then_inc(S(f"{kind}_made"), 1)
                    if layer < 2:
                        act.wait_ge(used, ring.base + ring.k)
                        act.nop().then_inc(S(f"ct_used{layer}"), 1)

                def copy_out(ring, c, vp):
                    o = bank(ring)
                    act.activation(SU[0:size(c), vp, c, :], o[0:size(c), 0:UNIT], ACT.Copy).then_inc(used, 1)

                def exps(u, up, p):
                    act.wait_ge(S(f"shifted{layer}"), 3 * u + p + 1)
                    w = SU[0:CK, up, 4 * p:4 * p + 4, :]
                    ins = act.activation(w, w, ACT.Exp, scale=SCALES[layer])
                    if p == 2 and chunks > CH:
                        w = SU[0:NQ, up, CH, :]
                        ins = act.activation(w, w, ACT.Exp, scale=SCALES[layer])
                    ins.then_inc(S(f"exp_made{layer}"), 1)

                def slot(ring, i, s):
                    u, b = 4 * i + s, 2 * i + s // 2
                    half = up = s % 2
                    final = isinstance(b, int) and b == NB - 1
                    if final and half:
                        for p in range(3):
                            exps(u, up, p)
                    else:
                        for c in range(chunks):
                            copy_out(ring, c, 1 - up)
                            if c == 7:
                                exps(u, up, 0)
                            if c == 9:
                                exps(u, up, 1)
                        exps(u, up, 2)
                    if not half and not final:
                        prepare(ring, b + 1, (s // 2 + 1) % 2)
                    if half and layer < 3:
                        act.wait_ge(S(f"zt_ps{layer}"), b + 1)
                        act.activation(ZT[:, 0:PAIR], TR[:, 0, 0:PAIR], ACT.Copy).then_inc(S(f"zt_ready{layer}"), 1)

                ring = Ring(0, 0)
                prepare(ring, 0, 0)
                for c in range(chunks):
                    copy_out(ring, c, 0)
                n0 = ring.k
                with act.Fori(0, NB // 2 - 1) as i:
                    ring = Ring(i * len(turn) + n0, n0)
                    for s in range(4):
                        slot(ring, i, s)
                ring = Ring((NB // 2 - 1) * len(turn) + n0, n0)
                for s in range(4):
                    slot(ring, NB // 2 - 1, s)

            def top_act():
                def keys_out(b):
                    act.wait_ge(S("k_ps2"), b + 1 + PRIME)
                    act.activation(KT[:, 0:NK], PS[:, 0:3, 0:500], ACT.Copy).then_inc(S("k_ready2"), 1)

                def scores_out(b, j):
                    act.wait_ge(S("s_ready2"), PAIRS * b + j + 1)
                    act.activation(SC[:, j % 2, :], PS[:, 0:3, 0:500], ACT.Copy).then_inc(S("scores_out"), 1)

                def turn_batch(b, last):
                    for j in range(PAIRS):
                        act.wait_ge(S("max_ready2"), b * PAIRS + j + 1)
                        act.activation(E[:, :], SC[:, j % 2, :], ACT.Exp, bias=nb[:, j:j + 1],
                                       scale=SCALES[2]).then_inc(S("e_ready"), 1)
                        if j < PAIRS - 1:
                            scores_out(b, j + 1)
                        elif not last:
                            scores_out(b + 1, 0)
                        if j == PAIRS - 2 and not last:
                            keys_out(b + 1)
                        act.wait_ge(S("pv_ready2"), b * PAIRS + j - 1 + PV_PRIME)
                        for g in range(3):
                            k = 3 * j + g
                            act.wait_ge(S("tr_ready2"), b * TURNS + k + 1 + TR_PRIME)
                            act.activation(PT[0:CK, j % 2, 4 * g:4 * g + 4, :], TR[0:CK, k % 2, 0:4 * 128],
                                           ACT.Copy).then_inc(S("tr_used2"), 1)

                keys_out(0)
                scores_out(0, 0)
                with act.Fori(0, NB - 1) as b:
                    turn_batch(b, False)
                turn_batch(NB - 1, True)

            for i in range(len(RAWS)):
                act.wait_ge(S("tw_ps"), i + 1)
                act.activation(TW[:, i, :], PS[:, i % 4, 0:128], ACT.Copy).then_inc(S("tw_ready"), 1)
            act.wait_ge(S("w_l0"), 16 * 8)
            act.wait_ge(S("bvo_ps"), 1)
            act.activation(rbv, PO[0:1, 0:D], ACT.Copy).then_inc(S("bvo_made"), 1)
            ln_act(0)
            q_act(0)
            unit_act(0)
            ln_act(1)
            act.wait_ge(S("w_col"), 16 * 11)
            for t in range(NB):
                act.wait_ge(S("z_gates"), t + 1)
                act.wait_ge(S("c_ready"), t + 1)
                z_ = PS[:, t % 2, :]
                act.activation(gates[:, 0, :], z_[:, 0:NQ], ACT.Sigmoid, bias=colat["bf"]).then_inc(S("g_ready"), 1)
                act.activation(gates[:, 1, :], z_[:, NQ:2 * NQ], ACT.Sigmoid, bias=colat["bi"]).then_inc(S("g_ready"), 1)
                act.activation(gates[:, 2, :], z_[:, 2 * NQ:3 * NQ], ACT.Tanh, bias=colat["bc"]).then_inc(S("g_ready"), 1)
            act.wait_ge(S("h_ps"), 1)
            act.activation(XN[:, :, :], TR[0:NQ, :, :], ACT.Tanh).then_inc(S("h_ready"), 1)
            ln_act(2)
            q_act(1)
            unit_act(1)

            def moe_act(which):
                blocks = moe_blocks(which)
                done = len(moe_blocks(0)) if which else 0
                b1 = b1a if which == 0 else b1b
                func = ACT.Gelu if which == 0 else ACT.Gelu_apprx_tanh
                if which:
                    act.wait_ge(S("gh_ps"), 1)
                    for k in range(2):
                        act.activation(GH[:, k, :], PS[:, k, 0:T], ACT.Gelu, bias=gb1[:, k:k + 1])\
                           .then_inc(S("gh_ready"), 1)
                act.wait_ge(S("dl_ready"), which + 1)
                act.activation(ex[:, :, :], dl[:, :, :], ACT.Exp).then_inc(S("ex_ready"), 1)
                act.wait_ge(S("gt_ps"), which + 1)
                act.activation(GT[:, :], PO[0:NEXP, 0:T], ACT.Copy).then_inc(S("gt_ready"), 1)
                for i, (e, k) in enumerate(blocks):
                    act.wait_ge(S("up_ps"), done + i + 1)
                    if i >= 3:
                        act.wait_ge(S("hg_ready"), done + i - 2)
                    act.activation(H[:, i % 3, :], PS[:, i % 4, 0:T], func,
                                   bias=b1[:, e * blocks_per(which) + k:e * blocks_per(which) + k + 1])\
                       .then_inc(S("gelu_ready"), 1)
                act.wait_ge(S("down_ps"), done + len(blocks))
                act.activation(YT[:, :], PM[:, 0:T], ACT.Copy).then_inc(S("yt_ready"), 1)

            ln_act(3)
            moe_act(0)
            ln_act(4)
            q_act(2)
            top_act()
            ln_act(5)
            moe_act(1)
            for i in range(24):
                act.wait_ge(S("w3t_ps"), i + 1)
                act.activation(W3T[:, i * 128:(i + 1) * 128], PS[:, i % 4, 0:128], ACT.Copy)\
                   .then_inc(S("w3t_ready"), 1)
            for h in range(NH):
                act.wait_ge(S("gm_ps"), 2 * h + 1)
                act.activation(G3[:, h, :], PS[:, h % 2, 0:D], ACT.Copy).then_inc(S("gm_ready"), 1)
                act.wait_ge(S("gm_ps"), 2 * h + 2)
                act.activation(M3[:, h, :], PS[:, 2 + h % 2, 0:D], ACT.Copy).then_inc(S("gm_ready"), 1)
            ln_act(6)
            std_act(7)
            act.wait_ge(S("xnt_ps"), 8)
            act.activation(LT[:, :], PM[:, 0:T], ACT.Identity, bias=colat["b2"], scale=colat["w2"])\
               .then_inc(S("lat_t"), 1)
            act.wait_ge(S("lat_t"), 1)
            act.nop().then_inc(S("xnt_ready"), 1)
            act.wait_ge(S("cmv_ready"), 1)
            act.activation(crs[:, :], cmv[:, :, 1], ACT.Sqrt, bias=epst[0:CK, :]).then_inc(S("cstd_ready"), 1)
            for h in range(NH):
                act.wait_ge(S("q3_ps"), h + 1)
                act.activation(Q3[:, h, :], PS[:, h % 4, 0:T], ACT.Copy).then_inc(S("q3_ready"), 1)
            unit_act(3)
            act.wait_ge(S("lora_ps"), 1)
            act.activation(ldT, TR[0:100, 0, 0:4], ACT.Copy).then_inc(S("lora_ready"), 1)
            act.activation(luT, TR[0:4, 0, 4:54], ACT.Copy).then_inc(S("lora_ready"), 1)
            act.activation(uaT, TR[0:50, 0, 128:256], ACT.Copy).then_inc(S("lora_ready"), 1)
            act.wait_ge(S("lora_ps"), 2)
            act.activation(t1_, TR[0:4, 1, 0:128], ACT.Copy).then_inc(S("lora_ready"), 1)
            act.wait_ge(S("lora_ps"), 3)
            act.activation(t2_, TR[0:50, 1, 128:256], ACT.Copy).then_inc(S("lora_ready"), 1)
            act.wait_ge(S("lora_ps"), 4)
            act.activation(lwT, TR[:, 1, 256:384], ACT.Copy).then_inc(S("lora_ready"), 1)
            ln_act(8)

        @block.vector
        def _(dve):
            n = [0]
            chain = Count.sem = S("dve_step")

            def link(ins):
                n[0] += 1
                ins.then_inc(chain, 1)
                dve.wait_ge(chain, n[0])

            def ln_dve(k, src, dst):
                for b in range(NB):
                    ins = dve.bn_stats(st[:, b, :], src[:, b, :])
                link(ins)
                for b in range(NB):
                    ins = dve.bn_aggr(mv[:, b, :], st[:, b, :])
                ins.then_inc(S("var_ready"), 1)
                dve.wait_ge(S("std_ready"), k + 1)
                link(dve.reciprocal(rstd[:, :], std[:, :]))
                if k:
                    dve.wait_ge(S("xnt_ps"), k)
                for b in range(NB):
                    ins = dve.tensor_scalar(dst[:, b, :], src[:, b, :], mv[:, b, 0:1], rstd[:, b:b + 1],
                                            ALU.subtract, ALU.mult)
                ins.then_inc(S("xn_ready"), 1)

            def unit_dve(layer):
                prep, chunks, ahead, turn = plan(layer)
                used = S(f"bank_used{layer}")

                def batch_in(cnt, i, b):
                    if layer == 0:
                        dve.wait_ge(S("nat_in0"), 16 * (b + 1))
                        for c in range(CH):
                            ins = dve.bn_stats(cstat[:, c, :], NAT[:, c, :])
                        stand(dve, chain, cnt.mark(ins))
                        for c in range(CH):
                            ins = dve.bn_aggr(cmvb[:, c, :], cstat[:, c, :])
                        dve.wait_ge(chain, cnt.mark(ins))
                        dve.tensor_copy(cmv[:, bass.ds(b * CH, CH), :], cmvb[:, :, :]).then_inc(S("nat_used0"), 1)
                    if layer == 3:
                        dve.wait_ge(S("nat_in3"), 16 * (b + 1))
                        for c in range(CH):
                            ins = dve.tensor_scalar(
                                NAT[:, c, :], NAT[:, c, :],
                                cmv[:, bass.ds(b * CH + c, 1), 0:1].rearrange("p a s -> p (a s)"),
                                crs[:, bass.ds(b * CH + c, 1)], ALU.subtract, ALU.mult)
                        ins.then_inc(S("cn_ready"), 1)

                def size(c):
                    return CK if c < CH else NQ

                def chunk_max(cnt, ring, c, vp, last):
                    _, n = ring.next()
                    if c in (0, 2):
                        return
                    dve.wait_ge(used, n)
                    k = size(c)
                    if c in (1, 3):
                        a = c // 2
                        last[a] = cnt.mark(dve.tensor_tensor(ACC[:, vp, a, :], SU[0:CK, vp, c - 1, :],
                                                             SU[0:CK, vp, c, :], ALU.max))
                        return
                    a = c % 2
                    dve.wait_ge(chain, last[a])
                    last[a] = cnt.mark(dve.tensor_tensor(ACC[0:k, vp, a, :], ACC[0:k, vp, a, :],
                                                         SU[0:k, vp, c, :], ALU.max))

                def join_max(vp, last):
                    dve.wait_ge(chain, last[0])
                    dve.wait_ge(chain, last[1])
                    dve.tensor_tensor(ACC[:, vp, 0, :], ACC[:, vp, 0, :], ACC[:, vp, 1, :], ALU.max)\
                       .then_inc(S(f"chunk_max{layer}"), 1)

                def column_max(cnt, u):
                    dve.wait_ge(S(f"max_turned{layer}"), u + 1)
                    dve.wait_ge(chain, cnt.mark(dve.tensor_reduce(
                        rmx[:, :], TR[0:PAIR, 0, 0:4 * CK].rearrange("p (j k) -> p j k", j=4), X_AX, ALU.max)))
                    dve.tensor_tensor(DG[:, :, :],
                                      ident[0:PAIR, 0:PAIR].rearrange("p (a n) -> p a n", a=1)
                                      .to_broadcast([PAIR, 4, PAIR]),
                                      rmx[:, :].rearrange("p (j a) -> p j a", a=1).to_broadcast([PAIR, 4, PAIR]),
                                      ALU.mult).then_inc(S(f"diag_made{layer}"), 1)

                def shift(u, up, p):
                    if p == 0:
                        dve.wait_ge(S(f"max_spread{layer}"), u + 1)
                    w = SU[0:CK, up, 4 * p:4 * p + 4, :]
                    ins = dve.tensor_tensor(w, w, TR[0:CK, 1, 0:UNIT].rearrange("p (a n) -> p a n", a=1)
                                            .to_broadcast([CK, 4, UNIT]), ALU.subtract)
                    if p == 2 and chunks > CH:
                        w = SU[0:NQ, up, CH, :]
                        ins = dve.tensor_tensor(w, w, TR[0:NQ, 1, 0:UNIT], ALU.subtract)
                    ins.then_inc(S(f"shifted{layer}"), 1)

                def output(cnt, u, up, half):
                    o = (PO, PM)[up]
                    if layer == 3:
                        dve.wait_ge(S("exp_made3"), 3 * u + 3)
                        dve.wait_ge(chain, cnt.mark(dve.tensor_reduce(
                            SUMS[:, up, :], SU[0:CK, up, 0:CH, :].rearrange("p c n -> p n c"), X_AX, ALU.add)))
                        dve.tensor_tensor(SUMS[0:NQ, up, :], SUMS[0:NQ, up, :], SU[0:NQ, up, CH, :], ALU.add)\
                           .then_inc(S("sums_made"), 1)
                        dve.wait_ge(S("sums_spread"), u + 1)
                        dve.wait_ge(chain, cnt.mark(dve.reciprocal(RB[:, :], TR[:, 1, 0:UNIT])))
                        dve.wait_ge(S("weighed3"), u + 1 + WEIGHED)
                        dve.tensor_tensor(O3[:, 8 * half:8 * half + 8, :],
                                          o[:, 0:UNIT].rearrange("p (h q) -> p h q", q=NQ),
                                          RB[:, :].rearrange("p (h q) -> p h q", q=NQ), ALU.mult)\
                           .then_inc(S("o3_ready"), 1)
                        return
                    dve.wait_ge(S(f"weighed{layer}"), u + 1 + WEIGHED)
                    ov = o[0:PAIR, 0:4 * VW].rearrange("p (j w) -> p j w", w=VW)
                    dve.wait_ge(chain, cnt.mark(dve.reciprocal(
                        rdu[:, :].rearrange("p (j a) -> p j a", a=1), ov[:, :, VW - 1:VW])))
                    dve.wait_ge(chain, cnt.mark(dve.tensor_tensor(
                        rdv[:, :, :], rdu[:, :].rearrange("p (j a) -> p j a", a=1).to_broadcast([PAIR, 4, 2]),
                        pm[:, :].rearrange("p (a h) -> p a h", a=1).to_broadcast([PAIR, 4, 2]), ALU.mult)))
                    dve.tensor_tensor(ZU[:, 4 * half:4 * half + 4, :, :],
                                      ov[:, :, 0:2 * DH].rearrange("p j (h d) -> p j h d", d=DH),
                                      rdv[:, :, :].rearrange("p j (h a) -> p j h a", a=1)
                                      .to_broadcast([PAIR, 4, 2, DH]), ALU.mult).then_inc(S(f"z_ready{layer}"), 1)

                def slot(cnt, ring, i, s):
                    u, b = 4 * i + s, 2 * i + s // 2
                    half = up = s % 2
                    final = isinstance(b, int) and b == NB - 1
                    if final and half:
                        column_max(cnt, u)
                        for p in range(3):
                            shift(u, up, p)
                    else:
                        last = {}
                        for c in range(chunks):
                            chunk_max(cnt, ring, c, 1 - up, last)
                            if c == 1:
                                column_max(cnt, u)
                                if not half and not final:
                                    batch_in(cnt, i, b + 1)
                            if c in (6, 8, 10):
                                shift(u, up, c // 2 - 3)
                        join_max(1 - up, last)
                    if not half and not final:
                        ring.k += len(prep)
                    output(cnt, u, up, half)
                    if half:
                        dve.wait_ge(S(f"y_ready{layer}"), b + 1)
                        xb = X[:, bass.ds(b, 1), :].rearrange("p a d -> p (a d)")
                        dve.tensor_tensor(xb, TR[0:NQ, 0, 128:256], xb, ALU.add).then_inc(S(f"tail{layer}"), 1)

                cnt, ring = Count(n[0]), Ring(len(prep), 0)
                batch_in(cnt, 0, 0)
                last = {}
                for c in range(chunks):
                    chunk_max(cnt, ring, c, 0, last)
                join_max(0, last)
                base, n0 = n[0] + cnt.k, len(prep) + chunks
                marks = MARKS[layer]
                with dve.Fori(0, NB // 2 - 1) as i:
                    cnt, ring = Count(i * marks + base), Ring(i * len(turn) + n0, 0)
                    for s in range(4):
                        slot(cnt, ring, i, s)
                    assert cnt.k == marks, (layer, cnt.k)
                last_turn = NB // 2 - 1
                cnt, ring = Count(last_turn * marks + base), Ring(last_turn * len(turn) + n0, 0)
                for s in range(4):
                    slot(cnt, ring, last_turn, s)
                n[0] = last_turn * marks + base + cnt.k
                dve.wait_ge(S(f"tail{layer}"), NB + PRIME)
                dve.wait_ge(chain, n[0])

            def top_dve():
                marks = 7 * PAIRS + 2

                def tile(b, j, base, tail):
                    k = [0]
                    sc, w = SC[:, j % 2, :], P[:, j % 2, 0:NK]

                    def link2(ins, between=None):
                        k[0] += 1
                        mine = k[0]
                        ins.then_inc(chain, 1)
                        if between is not None and tail is not None:
                            between()
                        stand(dve, chain, base + mine)

                    def sums():
                        dve.wait_ge(S("p_ready2"), PAIRS * (tail + 1))
                        k[0] += 1
                        dve.reciprocal(rden[:, :], den[:, :]).then_inc(chain, 1)

                    def spread():
                        dve.wait_ge(chain, base + 2)
                        k[0] += 1
                        dve.tensor_tensor(
                            rdm[:, :, :], rden[:, :].rearrange("p (j a) -> p j a", a=1).to_broadcast([128, PAIRS, 2]),
                            pmask[:, :].rearrange("p (a h) -> p a h", a=1).to_broadcast([128, PAIRS, 2]),
                            ALU.mult).then_inc(chain, 1)

                    def outputs():
                        dve.wait_ge(chain, base + 4)
                        output(tail)

                    between = [spread, outputs, lambda: add(tail)]
                    stand(dve, S("scores_out"), PAIRS * b + j + 1 + PRIME)
                    link2(dve.max(m8[:, 0:8], sc), sums)
                    dve.tensor_scalar(nb[:, j:j + 1], m8[:, 0:1], -SCALES[2], None, ALU.mult)\
                       .then_inc(S("max_ready2"), 1)
                    stand(dve, S("tr_ready2"), 3 * (PAIRS * b + j - 1) + TR_PRIME)
                    for r in range(1, TOPK // 8):
                        link2(dve.match_replace(out=w, in_to_replace=m8[:, 8 * r - 8:8 * r],
                                                in_values=sc if r == 1 else w, imm_value=LOWEST), between[r - 1])
                        link2(dve.max(m8[:, 8 * r:8 * r + 8], w))
                    dve.wait_ge(S("e_ready"), PAIRS * b + j + 1)
                    dve.scalar_tensor_tensor(out=w, in0=sc, scalar=m8[:, TOPK - 1:TOPK], in1=E[:, :],
                                             op0=ALU.is_ge, op1=ALU.mult, accum_out=den[:, j:j + 1])\
                       .then_inc(S("p_ready2"), 1)
                    return k[0]

                def output(b):
                    dve.wait_ge(S("pv_ready2"), (b + 1) * PAIRS + PV_PRIME)
                    dve.tensor_tensor(
                        Z.rearrange("p (h d) -> p h d", d=DH),
                        PO[:, 0:128].rearrange("p (h d) -> p h d", d=DH),
                        rdm[:, :, :].rearrange("p j h -> p (j h)").rearrange("p (h a) -> p h a", a=1)
                        .to_broadcast([128, NH, DH]), ALU.mult).then_inc(S("z_ready2"), 1)

                def add(b):
                    dve.wait_ge(S("y_ready2"), b + 1)
                    xb = X[:, bass.ds(b, 1), :].rearrange("p a d -> p (a d)")
                    dve.tensor_tensor(xb, PM[0:NQ, 128:256], xb, ALU.add).then_inc(S("tail2"), 1)

                n[0] += tile(0, 0, n[0], None)
                base = n[0]
                with dve.Fori(0, NB - 1) as b:
                    k = 0
                    for j in range(1, PAIRS):
                        k += tile(b, j, b * marks + (base + k), None)
                    k += tile(b + 1, 0, b * marks + (base + k), b)
                    assert k == marks
                n[0] += (NB - 1) * marks
                for j in range(1, PAIRS):
                    n[0] += tile(NB - 1, j, n[0], None)
                dve.wait_ge(S("p_ready2"), PAIRS * NB)
                link(dve.reciprocal(rden[:, :], den[:, :]))
                link(dve.tensor_tensor(
                    rdm[:, :, :], rden[:, :].rearrange("p (j a) -> p j a", a=1).to_broadcast([128, PAIRS, 2]),
                    pmask[:, :].rearrange("p (a h) -> p a h", a=1).to_broadcast([128, PAIRS, 2]), ALU.mult))
                output(NB - 1)
                add(NB - 1)
                dve.wait_ge(S("tail2"), NB + PRIME)

            dve.wait_ge(S("const"), 1)
            dve.wait_ge(S("mask_in"), 16)
            dve.tensor_scalar(MM[0:NQ, :].rearrange("q (c p) -> q c p", c=CH),
                              MI[:, :].rearrange("q (p c) -> q c p", c=CH), 0.0, BELOW,
                              ALU.is_equal, ALU.mult).then_inc(S("mask_made"), 1)
            dve.wait_ge(S("mask_made"), 1)
            dve.wait_ge(S("x_in"), 16)
            ln_dve(0, X, XN)
            dve.wait_ge(S("q_ready"), 1)
            unit_dve(0)
            ln_dve(1, X, XN)
            dve.wait_ge(S("w_col"), 16 * 11)
            dve.tensor_scalar(cst[:, 0, :], ones[:, 0:NQ], colat["in_c"], None, ALU.mult).then_inc(S("c_ready"), 1)
            dve.wait_ge(S("c_ready"), 1)
            for t in range(NB):
                dve.wait_ge(S("g_ready"), 3 * t + 3)
                dve.tensor_tensor(gtmp[:, 0, :], gates[:, 0, :], cst[:, t % 2, :], ALU.mult)
                link(dve.tensor_tensor(gtmp[:, 1, :], gates[:, 1, :], gates[:, 2, :], ALU.mult))
                dve.tensor_tensor(cst[:, (t + 1) % 2, :], gtmp[:, 0, :], gtmp[:, 1, :], ALU.add)\
                   .then_inc(S("c_ready"), 1)
                dve.wait_ge(S("c_ready"), t + 2)
            dve.wait_ge(S("h_ready"), 1)
            link(dve.tensor_tensor(X[:, :, :], X[:, :, :], XN[:, :, :], ALU.add))
            ln_dve(2, X, XN)
            dve.wait_ge(S("q_ready"), 2)
            unit_dve(1)

            def moe_dve(which):
                blocks = moe_blocks(which)
                done = len(moe_blocks(0)) if which else 0
                dve.wait_ge(S("lg_ps"), which + 1)
                link(dve.tensor_copy(lg[:, :, :], PO[0:NQ, 0:NB * NEXP]))
                for b in range(NB):
                    ins = dve.max(top[:, b, :], lg[:, b, :])
                link(ins)
                for b in range(NB):
                    ins = dve.max_index(tidx[:, b, :], top[:, b, :], lg[:, b, :])
                link(ins)
                link(dve.tensor_copy(tif[:, :, :], tidx[:, :, 0:2]))
                t0 = top[:, :, 0:1].to_broadcast([NQ, NB, NEXP])
                dve.tensor_tensor(dl[:, :, :], top[:, :, :] , t0, ALU.subtract).then_inc(S("dl_ready"), 1)
                dve.wait_ge(S("ex_ready"), which + 1)
                terms = ex[:, :, 0:2] if which == 0 else ex[:, :, :]
                link(dve.tensor_reduce(sm[:, :], terms, X_AX, ALU.add))
                link(dve.reciprocal(sm[:, :], sm[:, :]))
                link(dve.tensor_tensor(wt[:, :, :], ex[:, :, 0:2],
                                       sm[:, :].rearrange("p (b a) -> p b a", a=1).to_broadcast([NQ, NB, 2]), ALU.mult))
                for r, g_ in ((0, gt), (1, gt2)):
                    link(dve.tensor_tensor(g_[:, :, :], iota8[:, :].rearrange("p (a e) -> p a e", a=1).to_broadcast([NQ, NB, NEXP]),
                                           tif[:, :, r:r + 1].to_broadcast([NQ, NB, NEXP]), ALU.is_equal))
                    link(dve.tensor_tensor(g_[:, :, :], g_[:, :, :], wt[:, :, r:r + 1].to_broadcast([NQ, NB, NEXP]), ALU.mult))
                dve.tensor_tensor(gt[:, :, :], gt[:, :, :], gt2[:, :, :], ALU.add).then_inc(S("gate_ready"), 1)
                per = blocks_per(which)
                for i, (e, k) in enumerate(blocks):
                    dve.wait_ge(S("gelu_ready"), done + i + 1)
                    if i >= 3:
                        dve.wait_ge(S("down_ps"), done + i - 2)
                    if e < NEXP:
                        dve.wait_ge(S("gb_ps"), (NEXP if which else 0) + e + 1)
                        dve.tensor_tensor(HG[:, i % 3, :], H[:, i % 3, :], TR[:, e % 2, 0:T], ALU.mult)\
                           .then_inc(S("hg_ready"), 1)
                    else:
                        dve.tensor_copy(HG[:, i % 3, :], H[:, i % 3, :]).then_inc(S("hg_ready"), 1)
                dve.wait_ge(S("y_nat"), which + 1)
                link(dve.tensor_tensor(X[:, :, :], X[:, :, :], PS[0:NQ, 0:2, :].rearrange("p a (b d) -> p (a b) d", d=D),
                                       ALU.add))
                dve.nop().then_inc(S("moe_done"), 1)

            ln_dve(3, X, XN)
            moe_dve(0)
            ln_dve(4, X, XN)
            dve.wait_ge(S("q_ready"), 3)
            top_dve()
            ln_dve(5, X, XN)
            moe_dve(1)
            dve.nop().then_inc(S("x_upd"), 6)
            ln_dve(6, X, XN)
            dve.wait_ge(S("xn_ready"), 7)
            ln_dve(7, XN, XN2)
            dve.nop().then_inc(S("cmv_ready"), 1)
            dve.wait_ge(S("cstd_ready"), 1)
            link(dve.reciprocal(crs[:, :], crs[:, :]))
            dve.wait_ge(S("q3_ready"), NH)
            unit_dve(3)
            ln_dve(8, X, XN)
            dve.wait_ge(S("y_last"), 1)
            dve.tensor_tensor(X[:, :, :], X[:, :, :], PS[0:NQ, 0:2, :].rearrange("p a (b d) -> p (a b) d", d=D),
                              ALU.add).then_inc(S("x_final"), 1)


_INS = None


def kernel(**inputs):
    import numpy as _np
    import concourse.bacc as _bacc
    from concourse import mybir as _mybir
    from concourse.bass_utils import run_bass_kernel_spmd as _run

    nc = _bacc.Bacc("TRN2", target_bir_lowering=False, num_devices=1)
    arrays, args = {}, {}
    for name in inputs:
        a = _np.ascontiguousarray(inputs[name])
        if name == "L2_ffn_task_ids":
            continue
        arrays[f"in_{name}"] = a
        args[name] = nc.dram_tensor(f"in_{name}", a.shape, _mybir.dt.from_np(a.dtype), kind="ExternalInput").ap()
    scratch = nc.dram_tensor("ctx_transposed", (NB, D, NK), F32, kind="Internal").ap()
    out = nc.dram_tensor("out_0", (NB, NQ, D), F32, kind="ExternalOutput").ap()
    megakernel(nc, args, scratch, out)
    r = _run(nc, [arrays], core_ids=[0])
    return r.results[0]["out_0"]
```

```python
from contextlib import ExitStack

import concourse.bass as bass
from concourse import mybir

F32 = mybir.dt.float32
BF16 = mybir.dt.bfloat16
I32 = mybir.dt.int32
U32 = mybir.dt.uint32
ALU = mybir.AluOpType
ACT = mybir.ActivationFunctionType
X_AX = mybir.AxisListType.X

NB, NQ, D = 8, 56, 128
T = NB * NQ
NK = 1500
CH, CK = 12, 125
NH, DH = 16, 8
PAIRS = NH // 2
HQ = 64
DH3 = 64
NK3 = NK + NQ
EPS = 1e-5
NEXP = 8
FF1, FF2 = 512, 256
TOPK = 32
LOWEST = -3.0e38
SCALES = [1.0, 8.0 ** -0.5, 8.0 ** -0.5, 0.125]
PRIME = 1
UNIT = 8 * NQ
PAIR = 2 * NQ
VW = 1 + 2 * DH
BELOW = -3.0e38
WEIGHED = 4
PV_PRIME = 2
TR_PRIME = 4
TURNS = 3 * PAIRS
GRP = 4


def plan(layer):
    early = [("ct", g) for g in range(3)] if layer == 0 else []
    late = [("xt", g) for g in range(4)] if layer == 3 else [("kt", g) for g in range(3)]
    values = [("v", g) for g in range({0: 4, 1: 3, 3: 0}[layer])]
    return (early, late, values), CH + (layer == 3)


UNITS = 2 * NB


def per_turn(layer):
    (early, late, values), chunks = plan(layer)
    n = 4 * chunks + 2 * len(early + late + values)
    assert n % 4 == 0
    return n


def ahead(layer):
    (early, late, values), chunks = plan(layer)
    return len(early + late + values) + chunks + 2 * chunks + len(early + late + values)


class Count:

    def __init__(self, sem, base):
        self.sem, self.base, self.k = sem, base, 0

    def mark(self, ins):
        self.k += 1
        ins.then_inc(self.sem, 1)
        return self.base + self.k


MARKS = {0: 56, 1: 52, 3: 52}


class Ring:

    def __init__(self, base, skip):
        self.base, self.skip, self.k = base, skip % 4, 0

    def next(self):
        self.k += 1
        return (self.skip + self.k - 1) % 4, self.base + self.k


def groups(chunks):
    return [list(range(g, min(g + GRP, chunks))) for g in range(0, chunks, GRP)]


def moe_blocks(which):
    return [(e, k) for e in range(NEXP + which) for k in range(blocks_per(which))]


def blocks_per(which):
    return (FF1, FF2)[which] // 128


def megakernel(nc, A, scratch, out):
    ctx = ExitStack()
    with ctx:
        def sb(name, shape, dt=F32):
            return ctx.enter_context(nc.sbuf_tensor(name, shape, dt))

        sems = {}

        def S(name):
            if name not in sems:
                sems[name] = ctx.enter_context(nc.semaphore(name))
            return sems[name]

        X = sb("X", [NQ, NB, D])
        XN = sb("XN", [NQ, NB, D])
        XNT = sb("XNT", [D, T])
        ident = sb("ident", [128, 128])
        hmask = sb("hmask", [128, NH])
        pmask = sb("pmask", [128, 2])
        sel = sb("sel", [128, NQ])
        ones = sb("ones", [128, 128])
        esel = sb("esel", [NEXP, NEXP, 128])
        iota8 = sb("iota8", [NQ, NEXP])
        epst = sb("epst", [128, 1])
        st = sb("st", [NQ, NB, 6])
        mv = sb("mv", [NQ, NB, 2])
        std = sb("std", [NQ, NB])
        rstd = sb("rstd", [NQ, NB])

        wq = [sb(f"wq{i}", [D, D]) for i in range(2)]
        wk = [sb(f"wk{i}", [D, D]) for i in range(2)]
        wv = [sb(f"wv{i}", [D, D]) for i in range(2)]
        wo = [sb(f"wo{i}", [D, D]) for i in range(2)]
        COLS = ["bq", "bk", "bv", "bf", "bi", "bc", "in_c", "w1", "b1", "w2", "b2"]
        col = sb("col", [D, len(COLS)])
        colat = {n: col[:, i:i + 1] for i, n in enumerate(COLS)}
        rows = sb("rows", [1, 5, D])
        rbv, rbo0, rbos, rbo1, rb3 = (rows[:, i, :] for i in range(5))
        grow = sb("grow", [1, 2, NEXP])
        TW = sb("TW", [D, 11, D])
        SUB = sb("SUB", [128, 3, T])
        YT = SUB[:, 0, :]
        big = sb("big", [128, 9216])
        w1a = big[:, 0:4096].rearrange("p (e f) -> p e f", e=NEXP)
        w2a = big[:, 4096:8192].rearrange("p (e k d) -> p e k d", e=NEXP, k=4)
        w1b = big[:, 0:2304].rearrange("p (e f) -> p e f", e=9)
        w2b = big[:, 2304:4608].rearrange("p (e k d) -> p e k d", e=9, k=2)
        gw1 = big[:, 4608:4864]
        bcol = sb("bcol", [128, 52])
        b1a = bcol[:, 0:32]
        b1b = bcol[:, 32:50]
        gb1 = bcol[:, 50:52]
        wg1 = sb("wg1", [D, NEXP])
        gw2 = sb("gw2", [128, 2, NEXP])
        b2a = sb("b2a", [NEXP, D])
        b2b = sb("b2b", [NEXP, D])
        bs2 = sb("bs2", [1, D])
        w1B = sb("w1B", [128, D])
        b1B = sb("b1B", [128, D])
        w2B = sb("w2B", [NQ, D])
        b2B = sb("b2B", [NQ, D])
        lo = sb("lo", [128, 512])
        ld_, lu_ = lo[0:4, 0:100], lo[0:50, 100:104]
        ua_, da_ = lo[:, 104:154], lo[0:100, 154:282]
        lot = sb("lot", [128, 640])
        ldT, luT, uaT = lot[0:100, 0:4], lot[0:4, 4:54], lot[0:50, 128:256]
        t1_, t2_, lwT = lot[0:4, 256:384], lot[0:50, 384:512], lot[:, 512:640]

        NAT = sb("NAT", [CK, CH, D])
        CT = sb("CT", [D, NK])
        KTT = sb("KTT", [D, 2, NK3])
        KT = KTT[:, 0, :]
        VV = sb("VV", [128, 2, (CH + 1) * PAIRS * VW])
        VP = VV[:, :, 0:CH * PAIRS * VW].rearrange("p b (c j w) -> p b c j w", c=CH, j=PAIRS)
        V3 = VV[:, :, 0:(CH + 1) * D].rearrange("p b (c d) -> p b c d", d=D)
        QT = sb("QT", [D, T])
        QB = sb("QB", [D, NH, HQ])
        QP = sb("QP", [D, 2, NH * NQ])
        ST = sb("ST", [128, 2, (CH + 1) * UNIT])
        SU = ST[:, :, :].rearrange("p u (c n) -> p u c n", n=UNIT)
        flat = ST[:, :, :].rearrange("p u n -> p (u n)")
        RAW = flat[:, 0:11 * D].rearrange("p (n d) -> p n d", d=D)
        P = flat[:, 0:2 * NK].rearrange("p (r n) -> p r n", r=2)
        E = flat[:, 2 * NK:3 * NK]
        SC = flat[:, 3 * NK:5 * NK].rearrange("p (r n) -> p r n", r=2)
        PT = flat[:, 5 * NK:5 * NK + 2 * CH * 128].rearrange("p (r c n) -> p r c n", r=2, c=CH)
        XN2 = flat[0:NQ, 0:NB * D].rearrange("p (b d) -> p b d", d=D)
        MI = flat[0:NQ, 11 * D:11 * D + NK].bitcast(I32)
        MM = sb("MM", [128, NK], BF16)
        I8 = sb("I8", [128, UNIT], BF16)
        ACC = sb("ACC", [CK, 2, 2, UNIT])
        rmx = sb("rmx", [PAIR, 4])
        DG = sb("DG", [PAIR, 4, PAIR])
        PSUMS = SUB[0:CK, 0:2, :]
        SUMS = SUB[0:CK, 2, :]
        RB = XNT[:, :]
        O3 = QB[:, :, 0:NQ]
        pm = sb("pm", [PAIR, 2])
        rdu = sb("rdu", [PAIR, 4])
        rdv = sb("rdv", [PAIR, 4, 2])
        ZU = sb("ZU", [PAIR, PAIRS, 2, DH])
        ZS = sb("ZS", [128, 2, 128])
        Z = ZS[:, 0, :]
        ZT = ZS[:, 1, :]
        cstat = sb("cstat", [CK, CH, 6])
        cmv = sb("cmv", [CK, NB * CH, 2])
        cmvb = sb("cmvb", [CK, CH, 2])
        crs = sb("crs", [CK, NB * CH])
        nb = sb("nb", [128, PAIRS])
        rden = sb("rden", [128, PAIRS])
        rdm = sb("rdm", [128, PAIRS, 2])
        m8 = sb("m8", [128, TOPK + 1 + TOPK // 2])
        least = sb("least", [128, 1 + TOPK // 2])
        limit = sb("limit", [128, 2])
        W = VV[:, 1, 0:NK]
        OR = sb("OR", [128, PAIRS * VW])
        M3 = big[:, 0:2048].rearrange("p (h d) -> p h d", h=NH)
        Q3 = big[:, 2048:9216].rearrange("p (h t) -> p h t", h=NH)
        W3r = flat[:, 1024:4096]
        W3T = flat[:, 4096:7168]
        G3 = flat[:, 7168:9216].rearrange("p (h d) -> p h d", h=NH)
        wo3 = sb("wo3", [128, PAIRS, D])
        LT = sb("LT", [D, T])
        LN_ = sb("LN_", [NQ, NB, D])

        H = VV[:, 0, 0:3 * T].rearrange("p (r t) -> p r t", r=3)
        HG = KTT[:, 0, 0:3 * T].rearrange("p (r t) -> p r t", r=3)
        GH = E[:, 0:2 * T].rearrange("p (r t) -> p r t", r=2)
        lg = sb("lg", [NQ, NB, NEXP])
        top = sb("top", [NQ, NB, 8])
        tidx = sb("tidx", [NQ, NB, 8], U32)
        tif = sb("tif", [NQ, NB, 2])
        ex = sb("ex", [NQ, NB, NEXP])
        dl = sb("dl", [NQ, NB, NEXP])
        sm = sb("sm", [NQ, NB])
        wt = sb("wt", [NQ, NB, 2])
        gt = sb("gt", [NQ, NB, NEXP])
        gt2 = sb("gt2", [NQ, NB, NEXP])
        GT = sb("GT", [NEXP, T])
        OU = LT[0:VW, :]
        cst = sb("cst", [D, 2, NQ])
        gates = sb("gates", [D, 3, NQ])
        gtmp = sb("gtmp", [D, 2, NQ])

        PS = ctx.enter_context(nc.psum_tensor("PS", [128, 4, 512], F32))
        TR = ctx.enter_context(nc.psum_tensor("TR", [128, 2, 512], F32))
        PO = ctx.enter_context(nc.psum_tensor("PO", [128, 512], F32))
        PM = ctx.enter_context(nc.psum_tensor("PM", [128, 512], F32))

        RAWS = ["L0_ffn_wf", "L0_ffn_uf", "L0_ffn_wi", "L0_ffn_ui", "L0_ffn_wc", "L0_ffn_uc",
                "L0_ffn_wo", "L0_ffn_uo", "L2_xattn_Wq", "L2_xattn_Wk", "L3_ffn_W"]
        tw = {n: TW[:, i, :] for i, n in enumerate(RAWS)}
        WQ = [wq[0][:, :], wq[1][:, :], tw["L2_xattn_Wq"]]
        WK = [wk[0][:, :], wk[1][:, :], tw["L2_xattn_Wk"]]

        def row(ap):
            return ap.rearrange("(a n) -> a n", a=1)

        def column(ap):
            return ap.rearrange("(n a) -> n a", a=1)

        def stand(eng, sem, value):
            eng.wait_ge(sem, value)
            eng.sem_inc(S("turns"), 1)

        block = ctx.enter_context(nc.Block())

        @block.sync
        def _(sp):
            sp.dma_start(X[:, :, :], A["x"].rearrange("b q d -> q b d")).then_inc(S("x_in"), 16)
            sp.dma_start(MI[:, :], A["mask_1x1xSxS2_ik1"][0, 0, :, :]).then_inc(S("mask_in"), 16)
            for i, name in enumerate(RAWS):
                sp.dma_start(RAW[:, i, :], A[name]).then_inc(S("w_raw"), 16)
            for dst, name in ((wq, "Wq"), (wk, "Wk"), (wv, "Wv"), (wo, "Wo")):
                sp.dma_start(dst[0][:, :], A[f"L0_xattn_{name}"]).then_inc(S("w_l0_matrices"), 16)
            for layer in range(4):
                with sp.Fori(0, NB) as b:
                    if layer in (0, 2, 3):
                        if layer == 3:
                            stand(sp, S("v3_ready"), 4 * b + PRIME)
                            stand(sp, S("xt_made"), b + PRIME)
                        else:
                            stand(sp, S(f"nat_used{layer}"), b + PRIME)
                        if layer:
                            sp.wait_ge(S(f"nat_used{[0, 0, 0, 2][layer]}"), NB + PRIME)
                        sp.dma_start(NAT[:, :, :], A["ctx_1024"][bass.ds(b, 1), :, :].rearrange(
                            "a (p c) d -> p (a c) d", c=CH)).then_inc(S(f"nat_in{layer}"), 16)
                    if layer in (1, 2):
                        sp.wait_ge(S("ct_saved"), 16 * NB + 16)
                        sp.wait_ge(S("ct_used0"), NB)
                        if layer == 2:
                            sp.wait_ge(S("ct_used1"), NB + PRIME)
                        stand(sp, S(("", "ct_used1", "k_ps2")[layer]), b + PRIME)
                        sp.dma_start(CT[:, :], scratch[bass.ds(b, 1), :, :].rearrange(
                            "a p n -> p (a n)")).then_inc(S(f"ct_in{layer}"), 16)
                    if layer == 0:
                        stand(sp, S("ct_made"), b + 1)
                        sp.dma_start(scratch[bass.ds(b, 1), :, :].rearrange("a p n -> p (a n)"),
                                     CT[:, :]).then_inc(S("ct_saved"), 16)
            sp.wait_ge(S("x_final"), 1)
            sp.dma_start(out.rearrange("b q d -> q b d"), X[:, :, :]).then_inc(S("out_saved"), 16)
            sp.wait_ge(S("out_saved"), 16)
            sp.wait_ge(S("ct_saved"), 16 * NB + 16)

        @block.gpsimd
        def _(pool):
            n = [0]

            def link(ins):
                n[0] += 1
                ins.then_inc(S("pool_step"), 1)
                pool.wait_ge(S("pool_step"), n[0])

            for name in ("nat_used0", "nat_used2", "v3_ready", "xt_made", "ct_used1", "k_ps2", "scores_out",
                         "tail2", "tr_used2", "p_ready2", "tail0", "tail1", "tail3"):
                pool.sem_inc(S(name), PRIME)
            pool.sem_inc(S("ct_saved"), 16)
            pool.sem_inc(S("pv_ready2"), PV_PRIME)
            pool.sem_inc(S("tr_ready2"), TR_PRIME)
            for layer in (0, 1, 3):
                pool.sem_inc(S(f"weighed{layer}"), WEIGHED)
                pool.sem_inc(S(f"out_made{layer}"), PRIME)
            pool.sem_inc(S("sums_turned3"), PRIME)

            link(pool.memset(ident[:, :], 0.0))
            link(pool.memset(ones[:, :], 1.0))
            link(pool.memset(epst[:, :], EPS))
            link(pool.memset(hmask[:, :], 1.0))
            link(pool.memset(pmask[:, :], 1.0))
            link(pool.affine_select(out=ident[:, :], in_=ident[:, :], compare_op=ALU.not_equal, fill=1.0,
                                    base=0, pattern=[[-1, 128]], channel_multiplier=1))
            link(pool.memset(pm[:, :], 1.0))
            link(pool.memset(VP[:, :, :, :, 0:1], 1.0))
            link(pool.memset(I8[:, :], 0.0))
            link(pool.memset(MM[:, :], 0.0))
            i8 = I8[:, :].rearrange("p (h q) -> p h q", q=NQ)
            link(pool.affine_select(out=i8, in_=i8, compare_op=ALU.not_equal, fill=1.0,
                                    base=0, pattern=[[0, 8], [-1, NQ]], channel_multiplier=1))
            for m, w, k in ((hmask, DH, NH), (pmask, HQ, 2), (pm, NQ, 2)):
                link(pool.affine_select(out=m[:, :], in_=m[:, :], compare_op=ALU.is_ge, fill=0.0,
                                        base=0, pattern=[[-w, k]], channel_multiplier=1))
                link(pool.affine_select(out=m[:, :], in_=m[:, :], compare_op=ALU.is_ge, fill=0.0,
                                        base=w - 1, pattern=[[w, k]], channel_multiplier=-1))
            pool.tensor_tensor(sel[:, :], ident[:, 0:NQ], ident[:, HQ:HQ + NQ], ALU.add).then_inc(S("const"), 1)

            def load(dst, src, name):
                pool.dma_start(dst, src, allow_slow_non_contiguous=True).then_inc(S(name), 16)

            def queries(layer):
                pool.wait_ge(S("q_ready"), layer + 1)
                with pool.Fori(0, NB // 2) as i:
                    for par in range(2):
                        stand(pool, S(f"weighed{layer}"), 2 * (2 * i + par) - 3 + WEIGHED)
                        pool.tensor_tensor(
                            QP[:, par, :].rearrange("p (h q) -> p h q", q=NQ),
                            QT[:, bass.ds((2 * i + par) * NQ, NQ)].rearrange("p (a q) -> p a q", a=1)
                            .to_broadcast([D, NH, NQ]),
                            hmask[:, :].rearrange("p (h a) -> p h a", a=1).to_broadcast([D, NH, NQ]),
                            ALU.mult).then_inc(S(f"q_made{layer}"), 1)

            load(colat["bq"], column(A["L0_xattn_bq"]), "w_l0")
            load(colat["bk"], column(A["L0_xattn_bk"]), "w_l0")
            load(colat["bv"], column(A["L0_xattn_bv"]), "w_l0")
            load(rbo0, row(A["L0_xattn_bo"]), "w_l0")
            for a in ("bf", "bi", "bc", "in_c"):
                load(colat[a], column(A[f"L0_ffn_{a}"]), "w_col")
            for a in ("w1", "b1", "w2", "b2"):
                load(colat[a], column(A[f"L3_xattn_ln{a[1]}_{a[0]}"]), "w_col")
            load(rbos, row(A["L0_ffn_bo"]), "w_col")
            load(rbo1, row(A["L1_xattn_b_o"]), "w_col")
            load(rb3, row(A["L3_ffn_b"]), "w_col")
            queries(0)
            link(pool.memset(QB[:, :, :], 0.0))
            link(pool.memset(m8[:, TOPK:TOPK + 1], -LOWEST))
            link(pool.memset(esel[:, :, :], 0.0))
            link(pool.affine_select(out=esel[:, :, :], in_=esel[:, :, :], compare_op=ALU.not_equal, fill=1.0,
                                    base=0, pattern=[[-1, NEXP], [0, 128]], channel_multiplier=1))
            pool.iota(iota8[:, :], pattern=[[1, NEXP]], base=0, channel_multiplier=0,
                      allow_small_or_imprecise_dtypes=True).then_inc(S("const_late"), 1)
            for i, nme in enumerate(("w_q", "w_k", "w_v", "w_o")):
                load((wq, wk, wv, wo)[i][1][:, :], A[f"L1_xattn_{nme}"], "w_l1")
            load(w1a, A["L1_ffn_W1"].rearrange("e p f -> p e f"), "w_moe1")
            load(w2a, A["L1_ffn_W2"].rearrange("e (k p) d -> p e k d", p=128), "w_moe1")
            load(b1a, A["L1_ffn_b1"].rearrange("e (k p) -> p (e k)", p=128), "w_moe1")
            load(wg1[:, :], A["L1_ffn_Wg"], "w_moe1")
            load(grow[:, 0, :], row(A["L1_ffn_bg"]), "w_moe1")
            load(b2a[:, :], A["L1_ffn_b2"], "w_moe1")
            load(b1b[:, 0:16], A["L2_ffn_be1"].rearrange("e (k p) -> p (e k)", p=128), "w_moe2")
            load(b1b[:, 16:18], A["L2_ffn_bs1"].rearrange("(k p) -> p k", p=128), "w_moe2")
            load(gb1, A["L2_ffn_gb1"].rearrange("(k p) -> p k", p=128), "w_moe2")
            load(gw2[:, :, :], A["L2_ffn_gw2"].rearrange("(k p) e -> p k e", p=128), "w_moe2")
            load(grow[:, 1, :], row(A["L2_ffn_gb2"]), "w_moe2")
            load(b2b[:, :], A["L2_ffn_be2"], "w_moe2")
            load(bs2[:, :], row(A["L2_ffn_bs2"]), "w_moe2")
            load(wo3[:, :, :], A["L3_xattn_Wo"].rearrange("(j p) d -> p j d", p=128), "w_l3s")
            for dst, src, k in ((w1B, "ln1_w", 128), (b1B, "ln1_b", 128), (w2B, "ln2_w", NQ), (b2B, "ln2_b", NQ)):
                load(dst[:, :], A[f"L3_xattn_{src}"].partition_broadcast(k), "w_l3s")
            for dst, src in ((ld_, "lora_down"), (lu_, "lora_up"), (da_, "down_aux"), (ua_, "up_aux")):
                load(dst, A[f"L3_ffn_{src}"], "w_lora")
            queries(1)
            pool.wait_ge(S("moe_done"), 1)
            load(w1b[:, 0:8, :], A["L2_ffn_We1"].rearrange("e p f -> p e f"), "w_moe2")
            load(w1b[:, 8, :], A["L2_ffn_Ws1"], "w_moe2")
            load(w2b[:, 0:8, :, :], A["L2_ffn_We2"].rearrange("e (k p) d -> p e k d", p=128), "w_moe2")
            load(w2b[:, 8, :, :], A["L2_ffn_Ws2"].rearrange("(k p) d -> p k d", p=128), "w_moe2")
            load(gw1, A["L2_ffn_gw1"], "w_moe2")

            def top_queries(b):
                if not isinstance(b, int):
                    stand(pool, S("s_ready2"), PAIRS * b)
                pool.tensor_tensor(
                    QB[:, :, 0:NQ],
                    QT[:, bass.ds(b * NQ, NQ)].rearrange("p (a q) -> p a q", a=1).to_broadcast([D, NH, NQ]),
                    hmask[:, :].rearrange("p (h a) -> p h a", a=1).to_broadcast([D, NH, NQ]),
                    ALU.mult).then_inc(S("qb_ready2"), 1)

            def weights(b, j):
                stand(pool, S("tr_ready2"), 3 * (b * PAIRS + j - 1) + TR_PRIME)
                stand(pool, S("cut_ready"), b * PAIRS + j + 1)
                pool.tensor_scalar(P[:, j % 2, :], SC[:, j % 2, :], limit[:, j % 2:j % 2 + 1], None,
                                   ALU.is_ge).then_inc(S("reached"), 1)
                stand(pool, S("reached"), b * PAIRS + j + 1)
                stand(pool, S("e_ready"), b * PAIRS + j + 1)
                pool.tensor_tensor(P[:, j % 2, :], P[:, j % 2, :], E[:, :], ALU.mult).then_inc(S("p_ready2"), 1)

            pool.wait_ge(S("q_ready"), 3)
            top_queries(0)
            pool.memset(VP[:, 0, :, :, 0:1], 1.0).then_inc(S("ones_made"), 1)
            for j in range(PAIRS - 2):
                weights(0, j)
            with pool.Fori(1, NB) as b:
                top_queries(b)
                weights(b - 1, PAIRS - 2)
                weights(b - 1, PAIRS - 1)
                for j in range(PAIRS - 2):
                    weights(b, j)
            weights(NB - 1, PAIRS - 2)
            weights(NB - 1, PAIRS - 1)
            pool.wait_ge(S("moe_done"), 2)
            load(W3r[:, 0:1024], A["L3_xattn_Wq"], "w_l3")
            load(W3r[:, 1024:3072], A["L3_xattn_Wkv"], "w_l3")
            pool.wait_ge(S("w_l3s"), 16 * 5)
            pool.wait_ge(S("xn_ready"), 8)
            link(pool.tensor_tensor(LN_[:, :, :], XN2[:, :, :],
                                    w2B[:, :].rearrange("p (a d) -> p a d", a=1).to_broadcast([NQ, NB, D]), ALU.mult))
            link(pool.tensor_tensor(LN_[:, :, :], LN_[:, :, :],
                                    b2B[:, :].rearrange("p (a d) -> p a d", a=1).to_broadcast([NQ, NB, D]), ALU.add))
            base = n[0]
            pool.wait_ge(S("lat_t"), 1)
            pool.wait_ge(S("q3_ready"), NH)

            def keys_queries(b, par):
                if not isinstance(b, int):
                    stand(pool, S("weighed3"), 2 * b - 3 + WEIGHED)
                pool.tensor_copy(KTT[:, par, NK:NK3], LT[:, bass.ds(b * NQ, NQ)]).then_inc(S("v3_ready"), 1)
                pool.tensor_copy(QP[:, par, :].rearrange("p (h q) -> p h q", q=NQ),
                                 Q3[:, :, bass.ds(b * NQ, NQ)]).then_inc(S("v3_ready"), 1)

            def values3(b, par, step):
                if not isinstance(b, int):
                    stand(pool, S("weighed3"), 2 * b - 2 + WEIGHED)
                pool.tensor_copy(V3[0:NQ, par, CH, :], LN_[:, bass.ds(b, 1), :].rearrange("p a d -> p (a d)"))\
                    .then_inc(S("v3_ready"), 1)
                pool.wait_ge(S("cn_ready"), b + 1)
                pool.tensor_tensor(V3[0:CK, par, 0:CH, :], NAT[:, :, :],
                                   w1B[0:CK, :].rearrange("p (a d) -> p a d", a=1).to_broadcast([CK, CH, D]),
                                   ALU.mult).then_inc(S("pool_step"), 1)
                pool.wait_ge(S("pool_step"), step + 1)
                pool.tensor_tensor(V3[0:CK, par, 0:CH, :], V3[0:CK, par, 0:CH, :],
                                   b1B[0:CK, :].rearrange("p (a d) -> p a d", a=1).to_broadcast([CK, CH, D]),
                                   ALU.add).then_inc(S("v3_ready"), 1)
                return step + 1

            def sums3(u, up, step):
                pool.wait_ge(S("exp_made3"), 3 * u + 1)
                pool.tensor_tensor(PSUMS[:, :, :], SU[0:CK, up, 0:2, :], SU[0:CK, up, 2:4, :], ALU.add)\
                    .then_inc(S("pool_step"), 1)
                for k, c in enumerate((4, 6, 8, 10)):
                    if c in (4, 8):
                        pool.wait_ge(S("exp_made3"), 3 * u + c // 4 + 1)
                    pool.wait_ge(S("pool_step"), step + k + 1)
                    pool.tensor_tensor(PSUMS[:, :, :], PSUMS[:, :, :], SU[0:CK, up, c:c + 2, :], ALU.add)\
                        .then_inc(S("pool_step"), 1)
                pool.wait_ge(S("pool_step"), step + 5)
                pool.wait_ge(S("sums_turned3"), u + PRIME)
                pool.tensor_tensor(SUMS[:, :], PSUMS[:, 0, :], PSUMS[:, 1, :], ALU.add).then_inc(S("pool_step"), 1)
                pool.wait_ge(S("pool_step"), step + 6)
                pool.tensor_tensor(SUMS[0:NQ, :], SUMS[0:NQ, :], SU[0:NQ, up, CH, :], ALU.add)\
                    .then_inc(S("sums_made3"), 1)
                return step + 6

            def batch3(b, par, step):
                keys_queries(b, par)
                step = sums3(2 * b - 2, 0, step)
                step = values3(b, par, step)
                return sums3(2 * b - 1, 1, step)

            keys_queries(0, 0)
            base = batch3(1, 1, values3(0, 0, base))
            per = 2 * (6 + 1 + 6)
            with pool.Fori(1, NB // 2) as i:
                step = i * per + (base - per)
                for par in range(2):
                    step = batch3(2 * i + par, par, step)
            base += (NB // 2 - 1) * per
            sums3(UNITS - 1, 1, sums3(UNITS - 2, 0, base))

        @block.tensor
        def _(pe):
            def ln_pe(k, src):
                pe.wait_ge(S("xn_ready"), k + 1)
                for b in range(NB):
                    mm = pe.transpose(PM[:, b * NQ:(b + 1) * NQ], src[:, b, :], ident[0:NQ, 0:NQ])
                mm.then_inc(S("xnt_ps"), 1)
                pe.wait_ge(S("xnt_ready"), k + 1)

            def unit_pe(layer):
                (early, late, values), chunks = plan(layer)
                made, used = S(f"bank_made{layer}"), S(f"bank_used{layer}")
                out_made = S(f"out_made{layer}")

                def size(c):
                    return CK if c < CH else NQ

                def bank(ring):
                    r, n = ring.next()
                    if not (isinstance(n, int) and n <= 4):
                        pe.wait_ge(used, n - 4)
                    return PS[:, r, :]

                def prepare(ring, b, what):
                    for kind, g in what:
                        o = bank(ring)
                        if (kind, g) == ("ct", 0):
                            pe.wait_ge(S("nat_in0"), 16 * (b + 1))
                        elif (kind, g) == ("kt", 0) and layer == 1:
                            pe.wait_ge(S("ct_in1"), 16 * (b + 1))
                        elif (kind, g) == ("xt", 0):
                            pe.wait_ge(S("cn_ready"), b + 1)
                        if kind == "ct" or kind == "xt":
                            n = 4 if kind == "ct" else 3
                            for i in range(n):
                                mm = pe.transpose(o[:, i * CK:(i + 1) * CK], NAT[:, n * g + i, :], ident[0:CK, 0:CK])
                        elif kind == "kt":
                            if layer == 0 and g == 0:
                                pe.wait_ge(S("ct_made"), b + 1)
                            mm = pe.matmul(o[:, 0:500], WK[layer], CT[:, g * 500:(g + 1) * 500],
                                           start=True, stop=True)
                        else:
                            n = CH // len(values)
                            for i in range(n):
                                c = n * g + i
                                mm = pe.matmul(o[0:CK, i * D:(i + 1) * D], CT[:, c * CK:(c + 1) * CK],
                                               wv[layer][:, :], start=True, stop=True)
                        mm.then_inc(made, 1)

                def score(ring, c, par, half):
                    o = bank(ring)[0:size(c), 0:UNIT]
                    if layer == 1:
                        pe.matmul(o, MM[:, c * CK:c * CK + size(c)], I8[:, :], start=True, stop=False)
                    pe.matmul(o, KTT[:, par, c * CK:c * CK + size(c)],
                              QP[:, par, half * UNIT:(half + 1) * UNIT],
                              start=(layer != 1), stop=True).then_inc(made, 1)

                def maxima_turn(u, up):
                    pe.wait_ge(S(f"chunk_max{layer}"), u + 1)
                    for i in range(4):
                        mm = pe.transpose(TR[0:PAIR, 0, i * CK:(i + 1) * CK],
                                          ACC[:, up, 0, i * PAIR:(i + 1) * PAIR], ident[0:CK, 0:CK])
                    mm.then_inc(S(f"max_turned{layer}"), 1)

                def maxima_spread(u):
                    pe.wait_ge(S(f"diag_made{layer}"), u + 1)
                    pe.matmul(TR[0:CK, 1, 0:UNIT], ones[0:PAIR, 0:CK], DG[:, :, :], start=True, stop=True)\
                      .then_inc(S(f"max_spread{layer}"), 1)

                def weigh(u, b, up, par, p):
                    o = (PO, PM)[up]
                    if layer == 3 and p == 0:
                        pe.wait_ge(S("v3_ready"), 4 * b + 4 + PRIME)
                    pe.wait_ge(S(f"exp_made{layer}"), 3 * u + p + 1)
                    cs = [4 * p, 4 * p + 1, 4 * p + 2, 4 * p + 3] + ([CH] if p == 2 and chunks > CH else [])
                    if layer == 3:
                        for c in cs:
                            mm = pe.matmul(o[:, 0:UNIT], V3[0:size(c), par, c, :], SU[0:size(c), up, c, :],
                                           start=(c == 0), stop=(c == chunks - 1))
                    else:
                        for i in range(4):
                            for c in cs:
                                mm = pe.matmul(o[0:VW, i * PAIR:(i + 1) * PAIR],
                                               VP[0:CK, par, c, 4 * up + i, :],
                                               SU[0:CK, up, c, i * PAIR:(i + 1) * PAIR],
                                               start=(c == 0 and i == 0), stop=(c == CH - 1 and i == 3),
                                               skip_group_check=True)
                    if p == 2:
                        mm.then_inc(S(f"weighed{layer}"), 1)

                def sums_turn(u, up):
                    if layer == 3:
                        pe.wait_ge(S("sums_made3"), u + 1)
                        for i in range(4):
                            mm = pe.matmul(TR[0:PAIR, 0, i:i + 1], SUMS[:, i * PAIR:(i + 1) * PAIR], ones[0:CK, 0:1],
                                           start=True, stop=True)
                    else:
                        stand(pe, S(f"raw_out{layer}"), u + 1)
                        for i in range(4):
                            mm = pe.transpose(TR[0:PAIR, 0, i * VW:(i + 1) * VW], OU[:, i * PAIR:(i + 1) * PAIR],
                                              ident[0:VW, 0:VW])
                    mm.then_inc(S(f"sums_turned{layer}"), 1)

                def sums_spread(u):
                    pe.wait_ge(S("sums_diag"), u + 1)
                    pe.matmul(TR[:, 0, 0:UNIT], ones[0:PAIR, :], DG[:, :, :], start=True, stop=True)\
                      .then_inc(S("sums_spread3"), 1)

                def project_turn(b):
                    pe.wait_ge(out_made, 2 * b + 2 + PRIME)
                    if layer < 3:
                        pe.transpose(TR[:, 0, 0:PAIR], ZU[:, :, :, :].rearrange("p j h d -> p (j h d)"),
                                     ident[0:PAIR, 0:PAIR]).then_inc(S(f"zt_ps{layer}"), 1)

                def project(b):
                    y = TR[0:NQ, 0, 128:256]
                    if layer < 3:
                        pe.wait_ge(S(f"zt_ready{layer}"), b + 1)
                        pe.matmul(y, ZT[:, 0:NQ], wo[layer][:, :], start=True, stop=False)
                        pe.matmul(y, ZT[:, NQ:PAIR], wo[layer][:, :], start=False, stop=False)
                        pe.matmul(y, ones[0:1, 0:NQ], rbv if layer == 0 else rbo1,
                                  start=False, stop=True).then_inc(S(f"y_ready{layer}"), 1)
                    else:
                        for h in range(NH):
                            mm = pe.matmul(y, O3[:, h, :], M3[:, h, :], start=(h == 0), stop=(h == NH - 1))
                        mm.then_inc(S(f"y_ready{layer}"), 1)

                def first_scores_wait(done, b):
                    pe.wait_ge(used, done)
                    if layer == 3:
                        pe.wait_ge(S("v3_ready"), 4 * b + 2 + PRIME)
                    else:
                        pe.wait_ge(S(f"q_made{layer}"), b + 1)

                def slot(ring, i, s):
                    u, b, bn, bp = 4 * i + s, 2 * i + s // 2, 2 * i + (s + 1) // 2, 2 * i + (s - 1) // 2
                    first, last = isinstance(u, int) and u == 0, isinstance(u, int) and u == UNITS - 1
                    drain = isinstance(u, int) and u == UNITS
                    complete = s % 2 == 1 and not (isinstance(u, int) and u < 3)

                    def part(p):
                        if not first:
                            weigh(u - 1, bp, (s - 1) % 2, ((s - 1) // 2) % 2, p)

                    def scores(c):
                        if not (last or drain):
                            score(ring, c, ((s + 1) // 2) % 2, (s + 1) % 2)

                    part(0)
                    if not drain:
                        if not first:
                            pe.wait_ge(out_made, u - 1 + PRIME)
                        maxima_turn(u, s % 2)
                        if s % 2 and not last:
                            first_scores_wait(ring.base + ring.k, bn)
                        scores(0)
                        scores(1)
                        maxima_spread(u)
                        scores(2)
                        scores(3)
                        if complete:
                            project_turn(b - 1)
                    if layer == 3 and not first:
                        if drain:
                            pe.wait_ge(out_made, u - 1 + PRIME)
                        sums_turn(u - 1, (s - 1) % 2)
                    part(1)
                    if layer == 3 and not first:
                        sums_spread(u - 1)
                    scores(4)
                    scores(5)
                    if not drain and complete:
                        if layer == 3:
                            pe.wait_ge(S("rb_out"), u)
                        project(b - 1)
                    scores(6)
                    scores(7)
                    prep = not (last or drain) and not (isinstance(b, int) and b == NB - 1)
                    if prep and s % 2 == 0:
                        prepare(ring, b + 1, early)
                    part(2)
                    scores(8)
                    scores(9)
                    if not first and layer < 3:
                        if not drain and complete:
                            pe.wait_ge(S(f"tail{layer}"), b + PRIME)
                        if drain:
                            pe.wait_ge(out_made, u - 1 + PRIME)
                        sums_turn(u - 1, (s - 1) % 2)
                    for c in range(10, chunks):
                        scores(c)
                    if prep:
                        prepare(ring, b + 1, late if s % 2 == 0 else values)
                    if drain:
                        project_turn(NB - 1)
                        project(NB - 1)

                ring = Ring(0, 0)
                prepare(ring, 0, early + late)
                prepare(ring, 0, values)
                first_scores_wait(ring.k, 0)
                for c in range(chunks):
                    score(ring, c, 0, 0)
                slot(ring, 0, 0)
                slot(ring, 0, 1)
                n0, turn = ring.k, per_turn(layer)
                assert n0 == ahead(layer)
                with pe.Fori(0, NB // 2 - 1) as i:
                    ring = Ring(i * turn + n0, n0)
                    for s in range(2, 6):
                        slot(ring, i, s)
                    assert ring.k == turn
                ring = Ring((NB // 2 - 1) * turn + n0, n0)
                for s in range(2, 5):
                    slot(ring, NB // 2 - 1, s)
                pe.wait_ge(S(f"tail{layer}"), NB + PRIME)

            def top_pe():
                def keys(b):
                    pe.wait_ge(S("ct_in2"), 16 * (b + 1))
                    pe.wait_ge(S("scores_out"), PAIRS * b + PRIME)
                    for n in range(3):
                        mm = pe.matmul(PS[:, n, 0:500], WK[2], CT[:, n * 500:(n + 1) * 500],
                                       start=True, stop=True)
                    mm.then_inc(S("k_ps2"), 1)

                def scores(b, j):
                    if j == 0:
                        pe.wait_ge(S("qb_ready2"), b + 1)
                        pe.wait_ge(S("k_ready2"), b + 1)
                    else:
                        pe.wait_ge(S("scores_out"), PAIRS * b + j + PRIME)
                    for n in range(3):
                        mm = pe.matmul(PS[:, n, 0:500], QB[:, 2 * j:2 * j + 2, :], KT[:, n * 500:(n + 1) * 500],
                                       start=True, stop=True)
                    mm.then_inc(S("s_ready2"), 1)

                def weigh(b, j):
                    def turn(g):
                        i = 3 * j + g
                        stand(pe, S("tr_used2"), b * TURNS + (i - 1 if i >= 2 else 0) + PRIME)
                        for n, c in enumerate(groups(CH)[g]):
                            mm = pe.transpose(TR[0:CK, i % 2, n * 128:(n + 1) * 128],
                                              P[:, j % 2, c * CK:(c + 1) * CK], ident[:, :])
                        mm.then_inc(S("tr_ready2"), 1)

                    def gather(g):
                        pe.wait_ge(S("tr_used2"), b * TURNS + 3 * j + g + 1 + PRIME)
                        for c in groups(CH)[g]:
                            mm = pe.matmul(PO[:, j * VW:(j + 1) * VW], PT[0:CK, j % 2, c, :],
                                           VP[0:CK, 0, c, j, :], start=(c == 0), stop=(c == CH - 1))
                        return mm

                    if j == 0:
                        pe.wait_ge(S("nat_used2"), b + 1 + PRIME)
                        if not isinstance(b, int) or b:
                            pe.wait_ge(S("raw_out2"), b)
                    pe.wait_ge(S("p_ready2"), b * PAIRS + j + 1 + PRIME)
                    turn(0)
                    for g in range(1, 3):
                        turn(g)
                        gather(g - 1)
                    gather(2).then_inc(S("pv_ready2"), 1)

                def add_heads(b):
                    pe.wait_ge(S("z_ready2"), b + 1)
                    pe.matmul(PM[0:NQ, 128:256], sel[:, :], Z, start=True, stop=True)\
                      .then_inc(S("y_ready2"), 1)

                def step(b, j, output_of=None):
                    last = isinstance(b, int) and b == NB - 1
                    if j + 2 < PAIRS:
                        scores(b, j + 2)
                    elif not last:
                        scores(b + 1, j + 2 - PAIRS)
                    if output_of is not None:
                        add_heads(output_of)
                    weigh(b, j)
                    if j == PAIRS - 3 and not last:
                        keys(b + 1)

                keys(0)
                scores(0, 0)
                scores(0, 1)
                step(0, 0)
                step(0, 1)
                with pe.Fori(0, NB - 1) as b:
                    for j in range(2, PAIRS):
                        step(b, j)
                    step(b + 1, 0)
                    step(b + 1, 1, output_of=b)
                for j in range(2, PAIRS):
                    step(NB - 1, j)
                add_heads(NB - 1)
                pe.wait_ge(S("tail2"), NB + PRIME)

            pe.wait_ge(S("const"), 1)
            pe.wait_ge(S("w_raw"), 16 * len(RAWS))
            for i in range(len(RAWS)):
                if i >= 4:
                    pe.wait_ge(S("tw_ready"), i - 3)
                pe.transpose(PS[:, i % 4, 0:128], RAW[:, i, :], ident[:, :]).then_inc(S("tw_ps"), 1)
            pe.wait_ge(S("tw_ready"), len(RAWS))

            def project_q(layer):
                pe.matmul(PM[:, 0:T], WQ[layer], XNT[:, :], start=True, stop=True)\
                  .then_inc(S("q_ps"), 1)
                pe.wait_ge(S("q_ready"), layer + 1)

            pe.wait_ge(S("w_l0_matrices"), 16 * 4)
            pe.wait_ge(S("w_l0"), 16 * 4)
            pe.matmul(PO[0:1, 0:D], colat["bv"], wo[0][:, :], start=True, stop=False)
            pe.matmul(PO[0:1, 0:D], ones[0:1, 0:1], rbo0, start=False, stop=True).then_inc(S("bvo_ps"), 1)
            pe.wait_ge(S("bvo_made"), 1)
            ln_pe(0, XN)
            project_q(0)
            unit_pe(0)
            ln_pe(1, XN)
            pe.wait_ge(S("w_col"), 16 * 11)
            for t in range(NB):
                pe.wait_ge(S("c_ready"), t + 1)
                for g, n_ in enumerate(("f", "i", "c")):
                    o = PS[:, t % 2, g * NQ:(g + 1) * NQ]
                    pe.matmul(o, tw[f"L0_ffn_w{n_}"], XNT[:, t * NQ:(t + 1) * NQ], start=True, stop=False)
                    mm = pe.matmul(o, tw[f"L0_ffn_u{n_}"], cst[:, t % 2, :], start=False, stop=True)
                mm.then_inc(S("z_gates"), 1)
            pe.wait_ge(S("c_ready"), NB + 1)
            for t in range(NB):
                o = TR[0:NQ, t // 4, (t % 4) * D:(t % 4 + 1) * D]
                pe.matmul(o, XNT[:, t * NQ:(t + 1) * NQ], tw["L0_ffn_wo"], start=True, stop=False)
                pe.matmul(o, cst[:, NB % 2, :], tw["L0_ffn_uo"], start=False, stop=False)
                mm = pe.matmul(o, ones[0:1, 0:NQ], rbos, start=False, stop=True)
            mm.then_inc(S("h_ps"), 1)

            pe.wait_ge(S("w_l1"), 16 * 4)
            ln_pe(2, XN)
            project_q(1)
            pe.wait_ge(S("mask_made"), 1)
            unit_pe(1)

            def moe_pe(which):
                pe.wait_ge(S("const_late"), 1)
                blocks = moe_blocks(which)
                w1, w2, b2 = (w1a, w2a, b2a) if which == 0 else (w1b, w2b, b2b)
                if which == 0:
                    pe.wait_ge(S("w_moe1"), 16 * 6)
                    for b in range(NB):
                        o = PO[0:NQ, b * NEXP:(b + 1) * NEXP]
                        pe.matmul(o, XNT[:, b * NQ:(b + 1) * NQ], wg1[:, :], start=True, stop=False)
                        mm = pe.matmul(o, ones[0:1, 0:NQ], grow[:, 0, :], start=False, stop=True)
                else:
                    pe.wait_ge(S("w_moe2"), 16 * 12)
                    for k in range(2):
                        mm = pe.matmul(PS[:, k, 0:T], gw1[:, k * 128:(k + 1) * 128], XNT[:, :],
                                       start=True, stop=True)
                    mm.then_inc(S("gh_ps"), 1)
                    pe.wait_ge(S("gh_ready"), 2)
                    for b in range(NB):
                        o = PO[0:NQ, b * NEXP:(b + 1) * NEXP]
                        for k in range(2):
                            pe.matmul(o, GH[:, k, b * NQ:(b + 1) * NQ], gw2[:, k, :], start=(k == 0), stop=False)
                        mm = pe.matmul(o, ones[0:1, 0:NQ], grow[:, 1, :], start=False, stop=True)
                mm.then_inc(S("lg_ps"), 1)
                pe.wait_ge(S("gate_ready"), which + 1)
                for b in range(NB):
                    mm = pe.transpose(PO[0:NEXP, b * NQ:(b + 1) * NQ], gt[:, b, :], ident[0:NQ, 0:NQ])
                mm.then_inc(S("gt_ps"), 1)
                pe.wait_ge(S("gt_ready"), which + 1)
                done = len(moe_blocks(0)) if which else 0
                acc = PM[:, 0:T]
                pe.matmul(acc, b2[:, :], GT[:, :], start=True, stop=False, skip_group_check=True)
                if which:
                    pe.matmul(acc, bs2[:, :], ones[0:1, 0:1].to_broadcast([1, T]), start=False, stop=False,
                              skip_group_check=True)

                def down(i):
                    e, k = blocks[i]
                    pe.wait_ge(S("hg_ready"), done + i + 1)
                    pe.matmul(acc, w2[:, e, k, :], HG[:, i % 3, :], start=False,
                              stop=(i == len(blocks) - 1), skip_group_check=True).then_inc(S("down_ps"), 1)

                for i, (e, k) in enumerate(blocks):
                    if k == 0 and e < NEXP:
                        if e >= 2:
                            pe.wait_ge(S("hg_ready"), done + (e - 1) * blocks_per(which))
                        pe.matmul(TR[:, e % 2, 0:T], esel[:, e, :], GT[:, :], start=True, stop=True)\
                          .then_inc(S("gb_ps"), 1)
                    if i >= 4:
                        pe.wait_ge(S("gelu_ready"), done + i - 3)
                    pe.matmul(PS[:, i % 4, 0:T], w1[:, e, k * 128:(k + 1) * 128], XNT[:, :],
                              start=True, stop=True).then_inc(S("up_ps"), 1)
                    if i >= 3:
                        down(i - 3)
                for i in range(len(blocks) - 3, len(blocks)):
                    down(i)
                pe.wait_ge(S("yt_ready"), which + 1)
                for b in range(NB):
                    mm = pe.transpose(PS[0:NQ, b // 4, (b % 4) * D:(b % 4 + 1) * D], YT[:, b * NQ:(b + 1) * NQ],
                                      ident[:, :])
                mm.then_inc(S("y_nat"), 1)

            ln_pe(3, XN)
            moe_pe(0)
            ln_pe(4, XN)
            project_q(2)
            top_pe()
            ln_pe(5, XN)
            moe_pe(1)
            pe.wait_ge(S("w_l3"), 32)
            pe.wait_ge(S("w_l3s"), 16 * 5)
            for i in range(24):
                if i >= 4:
                    pe.wait_ge(S("w3t_ready"), i - 3)
                else:
                    pe.wait_ge(S("moe_done"), 2)
                pe.transpose(PS[:, i % 4, 0:128], W3r[:, i * 128:(i + 1) * 128], ident[:, :])\
                  .then_inc(S("w3t_ps"), 1)
            pe.wait_ge(S("w3t_ready"), 24)
            for h in range(NH):
                lo_, j = (h % 2) * DH3, h // 2
                if h >= 2:
                    pe.wait_ge(S("gm_ready"), 2 * (h - 1))
                pe.matmul(PS[:, h % 2, 0:D], W3T[lo_:lo_ + DH3, j * 128:(j + 1) * 128],
                          W3T[lo_:lo_ + DH3, 1024 + j * 128:1024 + (j + 1) * 128],
                          start=True, stop=True).then_inc(S("gm_ps"), 1)
                pe.matmul(PS[:, 2 + h % 2, 0:D], W3T[lo_:lo_ + DH3, 2048 + j * 128:2048 + (j + 1) * 128],
                          wo3[lo_:lo_ + DH3, j, :], start=True, stop=True).then_inc(S("gm_ps"), 1)
            pe.wait_ge(S("gm_ready"), 2 * NH)
            ln_pe(6, XN)
            ln_pe(7, XN2)
            pe.wait_ge(S("lat_t"), 1)
            for h in range(NH):
                if h >= 4:
                    pe.wait_ge(S("q3_ready"), h - 3)
                pe.matmul(PS[:, h % 4, 0:T], G3[:, h, :], LT[:, :], start=True, stop=True)\
                  .then_inc(S("q3_ps"), 1)
            pe.wait_ge(S("q3_ready"), NH)
            unit_pe(3)
            pe.wait_ge(S("w_lora"), 64)
            pe.transpose(TR[0:100, 0, 0:4], ld_, ident[0:4, 0:4])
            pe.transpose(TR[0:4, 0, 4:54], lu_, ident[0:50, 0:50])
            pe.transpose(TR[0:50, 0, 128:256], ua_, ident[:, :]).then_inc(S("lora_ps"), 1)
            pe.wait_ge(S("lora_ready"), 3)
            pe.matmul(TR[0:4, 1, 0:128], ldT, da_, start=True, stop=True).then_inc(S("lora_ps"), 1)
            pe.wait_ge(S("lora_ready"), 4)
            pe.matmul(TR[0:50, 1, 128:256], luT, t1_, start=True, stop=True).then_inc(S("lora_ps"), 1)
            pe.wait_ge(S("lora_ready"), 5)
            pe.matmul(TR[:, 1, 256:384], t2_, uaT, start=True, stop=True).then_inc(S("lora_ps"), 1)
            pe.wait_ge(S("lora_ready"), 6)
            ln_pe(8, XN)
            for b in range(NB):
                o = PS[0:NQ, b // 4, (b % 4) * D:(b % 4 + 1) * D]
                x_ = XNT[:, b * NQ:(b + 1) * NQ]
                pe.matmul(o, x_, tw["L3_ffn_W"], start=True, stop=False)
                pe.matmul(o, ones[0:1, 0:NQ], rb3, start=False, stop=False)
                mm = pe.matmul(o, x_, lwT, start=False, stop=True)
            mm.then_inc(S("y_last"), 1)

        @block.scalar
        def _(act):
            def std_act(k):
                act.wait_ge(S("var_ready"), k + 1)
                act.activation(std[:, :], mv[:, :, 1], ACT.Sqrt, bias=epst[0:NQ, :]).then_inc(S("std_ready"), 1)

            def ln_act(k, dst=None, w=1.0, bias=0.0):
                std_act(k)
                act.wait_ge(S("xnt_ps"), k + 1)
                act.activation((XNT if dst is None else dst)[:, :], PM[:, 0:T], ACT.Identity,
                               bias=bias, scale=w).then_inc(S("xnt_ready"), 1)

            def q_act(layer):
                act.wait_ge(S("q_ps"), layer + 1)
                act.activation(QT[:, :], PM[:, 0:T], ACT.Identity,
                               bias=colat["bq"] if layer == 0 else 0.0).then_inc(S("q_ready"), 1)

            def unit_act(layer):
                (early, late, values), chunks = plan(layer)
                made, used = S(f"bank_made{layer}"), S(f"bank_used{layer}")

                def size(c):
                    return CK if c < CH else NQ

                def bank(ring):
                    r, n = ring.next()
                    act.wait_ge(made, n)
                    return PS[:, r, :]

                def prepare(ring, b, par, what):
                    for kind, g in what:
                        if kind == "ct" and g == 0:
                            act.wait_ge(S("ct_saved"), 16 * b + 16)
                        o = bank(ring)
                        if kind == "ct":
                            act.activation(CT[:, g * 500:(g + 1) * 500], o[:, 0:500], ACT.Copy).then_inc(used, 1)
                        elif kind == "xt":
                            act.activation(KTT[:, par, g * 375:(g + 1) * 375], o[:, 0:375], ACT.Identity,
                                           scale=colat["w1"], bias=colat["b1"]).then_inc(used, 1)
                        elif kind == "kt":
                            act.activation(KTT[:, par, g * 500:(g + 1) * 500], o[:, 0:500], ACT.Identity,
                                           bias=colat["bk"] if layer == 0 else 0.0).then_inc(used, 1)
                        else:
                            n = CH // len(values)
                            act.activation(VP[0:CK, par, n * g:n * g + n, :, 1:VW],
                                           o[0:CK, 0:n * D].rearrange("p (c j w) -> p c j w", c=n, w=2 * DH),
                                           ACT.Copy).then_inc(used, 1)
                        if (kind, g) in (("ct", 2), ("xt", 3)):
                            act.wait_ge(used, ring.base + ring.k)
                            act.nop().then_inc(S(f"{kind}_made"), 1)
                    if what == values and layer < 2:
                        act.wait_ge(used, ring.base + ring.k)
                        act.nop().then_inc(S(f"ct_used{layer}"), 1)

                def copy_out(ring, c, vp):
                    o = bank(ring)
                    act.activation(SU[0:size(c), vp, c, :], o[0:size(c), 0:UNIT], ACT.Copy).then_inc(used, 1)

                def exps(u, up, p):
                    act.wait_ge(S(f"shifted{layer}"), 3 * u + p + 1)
                    w = SU[0:CK, up, 4 * p:4 * p + 4, :]
                    ins = act.activation(w, w, ACT.Exp, scale=SCALES[layer])
                    if p == 2 and chunks > CH:
                        w = SU[0:NQ, up, CH, :]
                        ins = act.activation(w, w, ACT.Exp, scale=SCALES[layer])
                    ins.then_inc(S(f"exp_made{layer}"), 1)

                def slot(ring, i, s):
                    u, b, par = 4 * i + s, 2 * i + s // 2, (s // 2 + 1) % 2
                    last = isinstance(u, int) and u == UNITS - 1
                    prep = not (isinstance(b, int) and b == NB - 1)

                    def raw_out():
                        act.wait_ge(S(f"weighed{layer}"), u + WEIGHED)
                        act.activation(OU[:, :], (PO, PM)[(s - 1) % 2][0:VW, 0:UNIT], ACT.Copy)\
                           .then_inc(S(f"raw_out{layer}"), 1)

                    def turned(b):
                        act.wait_ge(S(f"zt_ps{layer}"), b + 1)
                        act.activation(ZT[:, 0:PAIR], TR[:, 0, 0:PAIR], ACT.Copy).then_inc(S(f"zt_ready{layer}"), 1)

                    def spread_out():
                        act.wait_ge(S("sums_spread3"), u)
                        act.activation(RB, TR[:, 0, 0:UNIT], ACT.Copy).then_inc(S("rb_out"), 1)

                    if isinstance(u, int) and u == UNITS:
                        if layer < 3:
                            raw_out()
                            turned(NB - 1)
                        else:
                            spread_out()
                        return
                    exps(u, s % 2, 0)
                    if layer == 3 and not last and not (isinstance(u, int) and u == 0):
                        act.wait_ge(S("sums_made3"), u)
                    for p in range(3):
                        for c in range(4 * p, 4 * p + 4 if p < 2 else chunks):
                            if c == 4 and layer == 3 and not (isinstance(u, int) and u == 0):
                                spread_out()
                            if c == 8 and layer < 3 and not (isinstance(u, int) and u == 0):
                                raw_out()
                            if not last:
                                copy_out(ring, c, (s + 1) % 2)
                        if p == 0:
                            if s % 2 and layer < 3 and not (isinstance(u, int) and u < 3):
                                turned(b - 1)
                            exps(u, s % 2, 1)
                        if p == 1:
                            if prep and s % 2 == 0:
                                prepare(ring, b + 1, par, early)
                            exps(u, s % 2, 2)
                    if prep:
                        prepare(ring, b + 1, par, late if s % 2 == 0 else values)

                ring = Ring(0, 0)
                prepare(ring, 0, 0, early + late)
                prepare(ring, 0, 0, values)
                for c in range(chunks):
                    copy_out(ring, c, 0)
                slot(ring, 0, 0)
                slot(ring, 0, 1)
                n0, turn = ring.k, per_turn(layer)
                assert n0 == ahead(layer)
                with act.Fori(0, NB // 2 - 1) as i:
                    ring = Ring(i * turn + n0, n0)
                    for s in range(2, 6):
                        slot(ring, i, s)
                ring = Ring((NB // 2 - 1) * turn + n0, n0)
                for s in range(2, 5):
                    slot(ring, NB // 2 - 1, s)

            def top_act():
                def keys_out(b):
                    act.wait_ge(S("k_ps2"), b + 1 + PRIME)
                    act.activation(KT[:, 0:NK], PS[:, 0:3, 0:500], ACT.Copy).then_inc(S("k_ready2"), 1)

                def scores_out(b, j):
                    act.wait_ge(S("s_ready2"), PAIRS * b + j + 1)
                    act.activation(SC[:, j % 2, :], PS[:, 0:3, 0:500], ACT.Copy).then_inc(S("scores_out"), 1)

                def values_in(b):
                    act.wait_ge(S("nat_in2"), 16 * (b + 1))
                    act.activation(VP[0:CK, 0, :, :, 1:VW], NAT[:, :, :].rearrange("p c (j w) -> p c j w", j=PAIRS),
                                   ACT.Copy).then_inc(S("nat_used2"), 1)

                def exps(b, j):
                    act.wait_ge(S("max_ready2"), b * PAIRS + j + 1)
                    act.wait_ge(S("p_ready2"), b * PAIRS + j + PRIME)
                    act.activation(E[:, :], SC[:, j % 2, :], ACT.Exp, bias=nb[:, j:j + 1],
                                   scale=SCALES[2]).then_inc(S("e_ready"), 1)

                def step(b, j):
                    last = isinstance(b, int) and b == NB - 1
                    if j + 1 < PAIRS:
                        exps(b, j + 1)
                    elif not last:
                        exps(b + 1, 0)
                    if j + 2 < PAIRS:
                        scores_out(b, j + 2)
                    elif not last:
                        scores_out(b + 1, j + 2 - PAIRS)
                    act.wait_ge(S("pv_ready2"), b * PAIRS + j - 1 + PV_PRIME)
                    for g in range(3):
                        k = 3 * j + g
                        act.wait_ge(S("tr_ready2"), b * TURNS + k + 1 + TR_PRIME)
                        act.activation(PT[0:CK, j % 2, 4 * g:4 * g + 4, :], TR[0:CK, k % 2, 0:4 * 128],
                                       ACT.Copy).then_inc(S("tr_used2"), 1)
                    if j == PAIRS - 3 and not last:
                        keys_out(b + 1)
                    if j == PAIRS - 1:
                        act.wait_ge(S("pv_ready2"), (b + 1) * PAIRS + PV_PRIME)
                        act.activation(OR[:, :], PO[:, 0:PAIRS * VW], ACT.Copy).then_inc(S("raw_out2"), 1)
                        if not last:
                            values_in(b + 1)

                keys_out(0)
                scores_out(0, 0)
                exps(0, 0)
                scores_out(0, 1)
                act.wait_ge(S("ones_made"), 1)
                values_in(0)
                step(0, 0)
                step(0, 1)
                with act.Fori(0, NB - 1) as b:
                    for j in range(2, PAIRS):
                        step(b, j)
                    step(b + 1, 0)
                    step(b + 1, 1)
                for j in range(2, PAIRS):
                    step(NB - 1, j)

            for i in range(len(RAWS)):
                act.wait_ge(S("tw_ps"), i + 1)
                act.activation(TW[:, i, :], PS[:, i % 4, 0:128], ACT.Copy).then_inc(S("tw_ready"), 1)
            act.wait_ge(S("w_l0"), 16 * 4)
            act.wait_ge(S("bvo_ps"), 1)
            act.activation(rbv, PO[0:1, 0:D], ACT.Copy).then_inc(S("bvo_made"), 1)
            ln_act(0)
            q_act(0)
            unit_act(0)
            ln_act(1)
            act.wait_ge(S("w_col"), 16 * 11)
            for t in range(NB):
                act.wait_ge(S("z_gates"), t + 1)
                act.wait_ge(S("c_ready"), t + 1)
                z_ = PS[:, t % 2, :]
                act.activation(gates[:, 0, :], z_[:, 0:NQ], ACT.Sigmoid, bias=colat["bf"]).then_inc(S("g_ready"), 1)
                act.activation(gates[:, 1, :], z_[:, NQ:2 * NQ], ACT.Sigmoid, bias=colat["bi"]).then_inc(S("g_ready"), 1)
                act.activation(gates[:, 2, :], z_[:, 2 * NQ:3 * NQ], ACT.Tanh, bias=colat["bc"]).then_inc(S("g_ready"), 1)
            act.wait_ge(S("h_ps"), 1)
            act.activation(XN[:, :, :], TR[0:NQ, :, :], ACT.Tanh).then_inc(S("h_ready"), 1)
            ln_act(2)
            q_act(1)
            unit_act(1)

            def moe_act(which):
                blocks = moe_blocks(which)
                done = len(moe_blocks(0)) if which else 0
                b1 = b1a if which == 0 else b1b
                func = ACT.Gelu if which == 0 else ACT.Gelu_apprx_tanh
                if which:
                    act.wait_ge(S("gh_ps"), 1)
                    for k in range(2):
                        act.activation(GH[:, k, :], PS[:, k, 0:T], ACT.Gelu, bias=gb1[:, k:k + 1])\
                           .then_inc(S("gh_ready"), 1)
                act.wait_ge(S("dl_ready"), which + 1)
                act.activation(ex[:, :, :], dl[:, :, :], ACT.Exp).then_inc(S("ex_ready"), 1)
                act.wait_ge(S("gt_ps"), which + 1)
                act.activation(GT[:, :], PO[0:NEXP, 0:T], ACT.Copy).then_inc(S("gt_ready"), 1)
                for i, (e, k) in enumerate(blocks):
                    act.wait_ge(S("up_ps"), done + i + 1)
                    if i >= 3:
                        act.wait_ge(S("hg_ready"), done + i - 2)
                    act.activation(H[:, i % 3, :], PS[:, i % 4, 0:T], func,
                                   bias=b1[:, e * blocks_per(which) + k:e * blocks_per(which) + k + 1])\
                       .then_inc(S("gelu_ready"), 1)
                act.wait_ge(S("down_ps"), done + len(blocks))
                act.activation(YT[:, :], PM[:, 0:T], ACT.Copy).then_inc(S("yt_ready"), 1)

            ln_act(3)
            moe_act(0)
            ln_act(4)
            q_act(2)
            top_act()
            ln_act(5)
            moe_act(1)
            for i in range(24):
                act.wait_ge(S("w3t_ps"), i + 1)
                act.activation(W3T[:, i * 128:(i + 1) * 128], PS[:, i % 4, 0:128], ACT.Copy)\
                   .then_inc(S("w3t_ready"), 1)
            for h in range(NH):
                act.wait_ge(S("gm_ps"), 2 * h + 1)
                act.activation(G3[:, h, :], PS[:, h % 2, 0:D], ACT.Copy).then_inc(S("gm_ready"), 1)
                act.wait_ge(S("gm_ps"), 2 * h + 2)
                act.activation(M3[:, h, :], PS[:, 2 + h % 2, 0:D], ACT.Copy).then_inc(S("gm_ready"), 1)
            ln_act(6)
            std_act(7)
            act.wait_ge(S("xnt_ps"), 8)
            act.activation(LT[:, :], PM[:, 0:T], ACT.Identity, bias=colat["b2"], scale=colat["w2"])\
               .then_inc(S("lat_t"), 1)
            act.wait_ge(S("lat_t"), 1)
            act.nop().then_inc(S("xnt_ready"), 1)
            act.wait_ge(S("cmv_ready"), 1)
            act.activation(crs[:, :], cmv[:, :, 1], ACT.Sqrt, bias=epst[0:CK, :]).then_inc(S("cstd_ready"), 1)
            for h in range(NH):
                act.wait_ge(S("q3_ps"), h + 1)
                act.activation(Q3[:, h, :], PS[:, h % 4, 0:T], ACT.Copy).then_inc(S("q3_ready"), 1)
            unit_act(3)
            act.wait_ge(S("lora_ps"), 1)
            act.activation(ldT, TR[0:100, 0, 0:4], ACT.Copy).then_inc(S("lora_ready"), 1)
            act.activation(luT, TR[0:4, 0, 4:54], ACT.Copy).then_inc(S("lora_ready"), 1)
            act.activation(uaT, TR[0:50, 0, 128:256], ACT.Copy).then_inc(S("lora_ready"), 1)
            act.wait_ge(S("lora_ps"), 2)
            act.activation(t1_, TR[0:4, 1, 0:128], ACT.Copy).then_inc(S("lora_ready"), 1)
            act.wait_ge(S("lora_ps"), 3)
            act.activation(t2_, TR[0:50, 1, 128:256], ACT.Copy).then_inc(S("lora_ready"), 1)
            act.wait_ge(S("lora_ps"), 4)
            act.activation(lwT, TR[:, 1, 256:384], ACT.Copy).then_inc(S("lora_ready"), 1)
            ln_act(8)

        @block.vector
        def _(dve):
            n = [0]
            chain = S("dve_step")

            def link(ins):
                n[0] += 1
                ins.then_inc(chain, 1)
                dve.wait_ge(chain, n[0])

            def ln_dve(k, src, dst):
                for b in range(NB):
                    ins = dve.bn_stats(st[:, b, :], src[:, b, :])
                link(ins)
                for b in range(NB):
                    ins = dve.bn_aggr(mv[:, b, :], st[:, b, :])
                ins.then_inc(S("var_ready"), 1)
                dve.wait_ge(S("std_ready"), k + 1)
                link(dve.reciprocal(rstd[:, :], std[:, :]))
                if k:
                    dve.wait_ge(S("xnt_ps"), k)
                for b in range(NB):
                    ins = dve.tensor_scalar(dst[:, b, :], src[:, b, :], mv[:, b, 0:1], rstd[:, b:b + 1],
                                            ALU.subtract, ALU.mult)
                ins.then_inc(S("xn_ready"), 1)

            def unit_dve(layer):
                (early, late, values), chunks = plan(layer)
                used = S(f"bank_used{layer}")
                out_made = S(f"out_made{layer}")

                def batch_in(cnt, i, b):
                    if layer == 0:
                        dve.wait_ge(S("nat_in0"), 16 * (b + 1))
                        for c in range(CH):
                            ins = dve.bn_stats(cstat[:, c, :], NAT[:, c, :])
                        stand(dve, chain, cnt.mark(ins))
                        for c in range(CH):
                            ins = dve.bn_aggr(cmvb[:, c, :], cstat[:, c, :])
                        dve.wait_ge(chain, cnt.mark(ins))
                        dve.tensor_copy(cmv[:, bass.ds(b * CH, CH), :], cmvb[:, :, :]).then_inc(S("nat_used0"), 1)
                    if layer == 3:
                        dve.wait_ge(S("nat_in3"), 16 * (b + 1))
                        for c in range(CH):
                            ins = dve.tensor_scalar(
                                NAT[:, c, :], NAT[:, c, :],
                                cmv[:, bass.ds(b * CH + c, 1), 0:1].rearrange("p a s -> p (a s)"),
                                crs[:, bass.ds(b * CH + c, 1)], ALU.subtract, ALU.mult)
                        ins.then_inc(S("cn_ready"), 1)

                def size(c):
                    return CK if c < CH else NQ

                def chunk_max(cnt, ring, c, vp, last):
                    _, n = ring.next()
                    if c in (0, 2):
                        return
                    dve.wait_ge(used, n)
                    k = size(c)
                    if c in (1, 3):
                        a = c // 2
                        last[a] = cnt.mark(dve.tensor_tensor(ACC[:, vp, a, :], SU[0:CK, vp, c - 1, :],
                                                             SU[0:CK, vp, c, :], ALU.max))
                        return
                    a = c % 2
                    dve.wait_ge(chain, last[a])
                    last[a] = cnt.mark(dve.tensor_tensor(ACC[0:k, vp, a, :], ACC[0:k, vp, a, :],
                                                         SU[0:k, vp, c, :], ALU.max))

                def join_max(vp, last):
                    dve.wait_ge(chain, last[0])
                    dve.wait_ge(chain, last[1])
                    dve.tensor_tensor(ACC[:, vp, 0, :], ACC[:, vp, 0, :], ACC[:, vp, 1, :], ALU.max)\
                       .then_inc(S(f"chunk_max{layer}"), 1)

                def diagonal(values, name):
                    dve.tensor_tensor(DG[:, :, :],
                                      ident[0:PAIR, 0:PAIR].rearrange("p (a n) -> p a n", a=1)
                                      .to_broadcast([PAIR, 4, PAIR]),
                                      values[:, :].rearrange("p (j a) -> p j a", a=1).to_broadcast([PAIR, 4, PAIR]),
                                      ALU.mult).then_inc(S(name), 1)

                def column_max(cnt, u):
                    dve.wait_ge(S(f"max_turned{layer}"), u + 1)
                    dve.wait_ge(chain, cnt.mark(dve.tensor_reduce(
                        rmx[:, :], TR[0:PAIR, 0, 0:4 * CK].rearrange("p (j k) -> p j k", j=4), X_AX, ALU.max)))
                    diagonal(rmx, f"diag_made{layer}")

                def shift(u, up, p):
                    if p == 0:
                        dve.wait_ge(S(f"max_spread{layer}"), u + 1)
                    w = SU[0:CK, up, 4 * p:4 * p + 4, :]
                    ins = dve.tensor_tensor(w, w, TR[0:CK, 1, 0:UNIT].rearrange("p (a n) -> p a n", a=1)
                                            .to_broadcast([CK, 4, UNIT]), ALU.subtract)
                    if p == 2 and chunks > CH:
                        w = SU[0:NQ, up, CH, :]
                        ins = dve.tensor_tensor(w, w, TR[0:NQ, 1, 0:UNIT], ALU.subtract)
                    ins.then_inc(S(f"shifted{layer}"), 1)

                def sums(cnt, u):
                    dve.wait_ge(S("sums_turned3"), u + 1 + PRIME)
                    dve.wait_ge(chain, cnt.mark(dve.reciprocal(rdu[:, :], TR[0:PAIR, 0, 0:4])))
                    diagonal(rdu, "sums_diag")

                def output(cnt, u, up):
                    if layer == 3:
                        o = (PO, PM)[up][:, 0:UNIT]
                        dve.wait_ge(S("rb_out"), u + 1)
                        dve.wait_ge(S("weighed3"), u + 1 + WEIGHED)
                        dve.tensor_tensor(O3[:, 8 * up:8 * up + 8, :],
                                          o.rearrange("p (h q) -> p h q", q=NQ),
                                          RB.rearrange("p (h q) -> p h q", q=NQ), ALU.mult)\
                           .then_inc(out_made, 1)
                        return
                    dve.wait_ge(S(f"sums_turned{layer}"), u + 1)
                    ov = TR[0:PAIR, 0, 0:4 * VW].rearrange("p (j w) -> p j w", w=VW)
                    dve.wait_ge(chain, cnt.mark(dve.reciprocal(
                        rdu[:, :].rearrange("p (j a) -> p j a", a=1), ov[:, :, 0:1])))
                    dve.wait_ge(chain, cnt.mark(dve.tensor_tensor(
                        rdv[:, :, :], rdu[:, :].rearrange("p (j a) -> p j a", a=1).to_broadcast([PAIR, 4, 2]),
                        pm[:, :].rearrange("p (a h) -> p a h", a=1).to_broadcast([PAIR, 4, 2]), ALU.mult)))
                    dve.tensor_tensor(ZU[:, 4 * up:4 * up + 4, :, :],
                                      ov[:, :, 1:VW].rearrange("p j (h d) -> p j h d", d=DH),
                                      rdv[:, :, :].rearrange("p j (h a) -> p j h a", a=1)
                                      .to_broadcast([PAIR, 4, 2, DH]), ALU.mult).then_inc(out_made, 1)

                def add(b):
                    dve.wait_ge(S(f"y_ready{layer}"), b + 1)
                    xb = X[:, bass.ds(b, 1), :].rearrange("p a d -> p (a d)")
                    dve.tensor_tensor(xb, TR[0:NQ, 0, 128:256], xb, ALU.add).then_inc(S(f"tail{layer}"), 1)

                def slot(cnt, ring, i, s):
                    u, b = 4 * i + s, 2 * i + s // 2
                    first, last = isinstance(u, int) and u == 0, isinstance(u, int) and u == UNITS - 1
                    drain = isinstance(u, int) and u == UNITS
                    complete = s % 2 == 1 and not (isinstance(u, int) and u < 3)
                    prep = not (isinstance(b, int) and b >= NB - 1)
                    running = {}

                    def maxima(c):
                        if not last:
                            chunk_max(cnt, ring, c, (s + 1) % 2, running)

                    if drain:
                        if layer == 3:
                            sums(cnt, u - 1)
                        output(cnt, u - 1, (s - 1) % 2)
                        add(NB - 1)
                        return
                    column_max(cnt, u)
                    shift(u, s % 2, 0)
                    shift(u, s % 2, 1)
                    if layer == 3 and not first:
                        sums(cnt, u - 1)
                    for c in range(4):
                        maxima(c)
                    shift(u, s % 2, 2)
                    if prep and s % 2 == 0 and layer == 3:
                        batch_in(cnt, i, b + 1)
                    maxima(4)
                    maxima(5)
                    if complete:
                        add(b - 1)
                    maxima(6)
                    maxima(7)
                    if prep and s % 2 == 0:
                        if layer == 0:
                            batch_in(cnt, i, b + 1)
                        ring.k += len(early)
                    for c in range(8, chunks):
                        maxima(c)
                    if not last:
                        join_max((s + 1) % 2, running)
                    if not first:
                        output(cnt, u - 1, (s - 1) % 2)
                    if prep:
                        ring.k += len(late if s % 2 == 0 else values)

                prep0 = len(early + late + values)
                cnt, ring = Count(chain, n[0]), Ring(prep0, 0)
                batch_in(cnt, 0, 0)
                running = {}
                for c in range(chunks):
                    chunk_max(cnt, ring, c, 0, running)
                join_max(0, running)
                slot(cnt, ring, 0, 0)
                slot(cnt, ring, 0, 1)
                base, n0, turn = n[0] + cnt.k, ahead(layer), per_turn(layer)
                assert prep0 + ring.k == n0
                marks = MARKS[layer]
                with dve.Fori(0, NB // 2 - 1) as i:
                    cnt, ring = Count(chain, i * marks + base), Ring(i * turn + n0, 0)
                    for s in range(2, 6):
                        slot(cnt, ring, i, s)
                    assert cnt.k == marks, (layer, cnt.k)
                last_turn = NB // 2 - 1
                cnt, ring = Count(chain, last_turn * marks + base), Ring(last_turn * turn + n0, 0)
                for s in range(2, 5):
                    slot(cnt, ring, last_turn, s)
                n[0] = last_turn * marks + base + cnt.k
                dve.wait_ge(S(f"tail{layer}"), NB + PRIME)
                dve.wait_ge(chain, n[0])

            def top_dve():
                marks = 13 * PAIRS + 2

                def tile(b, j, base, tail=None, part=None):
                    k = [0]
                    sc, a, c = SC[:, j % 2, :], m8[:, 0:TOPK], m8[:, TOPK + 1:TOPK + 1 + TOPK // 2]
                    large, small = W[:, 0:NK // 2], W[:, NK // 2:NK]

                    def mark(ins):
                        k[0] += 1
                        ins.then_inc(chain, 1)
                        return base + k[0]

                    def largest(of, into, r):
                        return mark(dve.max(into[:, 8 * r:8 * r + 8], of))

                    def remove(of, found, r, done):
                        stand(dve, chain, done)
                        return mark(dve.match_replace(out=of, in_to_replace=found[:, 8 * r:8 * r + 8],
                                                      in_values=of, imm_value=LOWEST))

                    def sums():
                        dve.wait_ge(S("raw_out2"), tail + 1)
                        mark(dve.reciprocal(rden[:, :].rearrange("p (j a) -> p j a", a=1), orv[:, :, 0:1]))

                    def spread():
                        mark(spread_sums())

                    between = {0: [sums, spread, lambda: output(tail)], 1: [None, None, lambda: add(tail)]}\
                        .get(part, [None] * 3)
                    dve.wait_ge(S("scores_out"), PAIRS * b + j + 1 + PRIME)
                    da = mark(dve.tensor_tensor(large, sc[:, 0:NK // 2], sc[:, NK // 2:NK], ALU.max))
                    dc = mark(dve.tensor_tensor(small, sc[:, 0:NK // 2], sc[:, NK // 2:NK], ALU.min))
                    stand(dve, chain, da)
                    da = largest(large, a, 0)
                    stand(dve, chain, dc)
                    dc = largest(small, c, 0)
                    dve.wait_ge(chain, da)
                    dve.tensor_scalar(nb[:, j:j + 1], a[:, 0:1], -SCALES[2], None, ALU.mult)\
                       .then_inc(S("max_ready2"), 1)
                    for r in range(TOPK // 8 - 1):
                        da = remove(large, a, r, da)
                        if r == 0:
                            dc = remove(small, c, r, dc)
                        if between[r]:
                            between[r]()
                        stand(dve, chain, da)
                        da = largest(large, a, r + 1)
                        if r == 0:
                            stand(dve, chain, dc)
                            dc = largest(small, c, 1)
                    dve.wait_ge(chain, da)
                    done = mark(dve.tensor_tensor(least[:, :], m8[:, TOPK - 1:TOPK // 2 - 2:-1],
                                                  m8[:, TOPK:TOPK + 1 + TOPK // 2], ALU.min))
                    dve.wait_ge(chain, done)
                    dve.tensor_reduce(limit[:, j % 2:j % 2 + 1], least[:, :], X_AX, ALU.max)\
                       .then_inc(S("cut_ready"), 1)
                    return k[0]

                orv = OR[:, :].rearrange("p (j w) -> p j w", w=VW)

                def spread_sums():
                    return dve.tensor_tensor(
                        rdm[:, :, :], rden[:, :].rearrange("p (j a) -> p j a", a=1).to_broadcast([128, PAIRS, 2]),
                        pmask[:, :].rearrange("p (a h) -> p a h", a=1).to_broadcast([128, PAIRS, 2]), ALU.mult)

                def output(b):
                    dve.tensor_tensor(
                        Z.rearrange("p (j h d) -> p j h d", h=2, d=DH),
                        orv[:, :, 1:VW].rearrange("p j (h d) -> p j h d", d=DH),
                        rdm[:, :, :].rearrange("p j (h a) -> p j h a", a=1).to_broadcast([128, PAIRS, 2, DH]),
                        ALU.mult).then_inc(S("z_ready2"), 1)

                def add(b):
                    dve.wait_ge(S("y_ready2"), b + 1)
                    xb = X[:, bass.ds(b, 1), :].rearrange("p a d -> p (a d)")
                    dve.tensor_tensor(xb, PM[0:NQ, 128:256], xb, ALU.add).then_inc(S("tail2"), 1)

                n[0] += tile(0, 0, n[0])
                n[0] += tile(0, 1, n[0])
                n[0] += tile(0, 2, n[0])
                base = n[0]
                with dve.Fori(0, NB - 1) as b:
                    k = 0
                    for j in range(3, PAIRS):
                        k += tile(b, j, b * marks + (base + k))
                    for j, part in enumerate([None, 0, 1]):
                        k += tile(b + 1, j, b * marks + (base + k), b, part)
                    assert k == marks
                n[0] += (NB - 1) * marks
                for j in range(3, PAIRS):
                    n[0] += tile(NB - 1, j, n[0])
                dve.wait_ge(S("raw_out2"), NB)
                link(dve.reciprocal(rden[:, :].rearrange("p (j a) -> p j a", a=1), orv[:, :, 0:1]))
                link(spread_sums())
                output(NB - 1)
                add(NB - 1)
                dve.wait_ge(S("tail2"), NB + PRIME)

            dve.wait_ge(S("const"), 1)
            dve.wait_ge(S("mask_in"), 16)
            dve.tensor_scalar(MM[0:NQ, :].rearrange("q (c p) -> q c p", c=CH),
                              MI[:, :].rearrange("q (p c) -> q c p", c=CH), 0.0, BELOW,
                              ALU.is_equal, ALU.mult).then_inc(S("mask_made"), 1)
            dve.wait_ge(S("mask_made"), 1)
            dve.wait_ge(S("x_in"), 16)
            ln_dve(0, X, XN)
            dve.wait_ge(S("q_ready"), 1)
            unit_dve(0)
            ln_dve(1, X, XN)
            dve.wait_ge(S("w_col"), 16 * 11)
            dve.tensor_scalar(cst[:, 0, :], ones[:, 0:NQ], colat["in_c"], None, ALU.mult).then_inc(S("c_ready"), 1)
            dve.wait_ge(S("c_ready"), 1)
            for t in range(NB):
                dve.wait_ge(S("g_ready"), 3 * t + 3)
                dve.tensor_tensor(gtmp[:, 0, :], gates[:, 0, :], cst[:, t % 2, :], ALU.mult)
                link(dve.tensor_tensor(gtmp[:, 1, :], gates[:, 1, :], gates[:, 2, :], ALU.mult))
                dve.tensor_tensor(cst[:, (t + 1) % 2, :], gtmp[:, 0, :], gtmp[:, 1, :], ALU.add)\
                   .then_inc(S("c_ready"), 1)
                dve.wait_ge(S("c_ready"), t + 2)
            dve.wait_ge(S("h_ready"), 1)
            link(dve.tensor_tensor(X[:, :, :], X[:, :, :], XN[:, :, :], ALU.add))
            ln_dve(2, X, XN)
            dve.wait_ge(S("q_ready"), 2)
            unit_dve(1)

            def moe_dve(which):
                blocks = moe_blocks(which)
                done = len(moe_blocks(0)) if which else 0
                dve.wait_ge(S("const_late"), 1)
                dve.wait_ge(S("lg_ps"), which + 1)
                link(dve.tensor_copy(lg[:, :, :], PO[0:NQ, 0:NB * NEXP]))
                for b in range(NB):
                    ins = dve.max(top[:, b, :], lg[:, b, :])
                link(ins)
                for b in range(NB):
                    ins = dve.max_index(tidx[:, b, :], top[:, b, :], lg[:, b, :])
                link(ins)
                link(dve.tensor_copy(tif[:, :, :], tidx[:, :, 0:2]))
                t0 = top[:, :, 0:1].to_broadcast([NQ, NB, NEXP])
                dve.tensor_tensor(dl[:, :, :], top[:, :, :] , t0, ALU.subtract).then_inc(S("dl_ready"), 1)
                dve.wait_ge(S("ex_ready"), which + 1)
                terms = ex[:, :, 0:2] if which == 0 else ex[:, :, :]
                link(dve.tensor_reduce(sm[:, :], terms, X_AX, ALU.add))
                link(dve.reciprocal(sm[:, :], sm[:, :]))
                link(dve.tensor_tensor(wt[:, :, :], ex[:, :, 0:2],
                                       sm[:, :].rearrange("p (b a) -> p b a", a=1).to_broadcast([NQ, NB, 2]), ALU.mult))
                for r, g_ in ((0, gt), (1, gt2)):
                    link(dve.tensor_tensor(g_[:, :, :], iota8[:, :].rearrange("p (a e) -> p a e", a=1).to_broadcast([NQ, NB, NEXP]),
                                           tif[:, :, r:r + 1].to_broadcast([NQ, NB, NEXP]), ALU.is_equal))
                    link(dve.tensor_tensor(g_[:, :, :], g_[:, :, :], wt[:, :, r:r + 1].to_broadcast([NQ, NB, NEXP]), ALU.mult))
                dve.tensor_tensor(gt[:, :, :], gt[:, :, :], gt2[:, :, :], ALU.add).then_inc(S("gate_ready"), 1)
                per = blocks_per(which)
                for i, (e, k) in enumerate(blocks):
                    dve.wait_ge(S("gelu_ready"), done + i + 1)
                    if i >= 3:
                        dve.wait_ge(S("down_ps"), done + i - 2)
                    if e < NEXP:
                        dve.wait_ge(S("gb_ps"), (NEXP if which else 0) + e + 1)
                        dve.tensor_tensor(HG[:, i % 3, :], H[:, i % 3, :], TR[:, e % 2, 0:T], ALU.mult)\
                           .then_inc(S("hg_ready"), 1)
                    else:
                        dve.tensor_copy(HG[:, i % 3, :], H[:, i % 3, :]).then_inc(S("hg_ready"), 1)
                dve.wait_ge(S("y_nat"), which + 1)
                link(dve.tensor_tensor(X[:, :, :], X[:, :, :], PS[0:NQ, 0:2, :].rearrange("p a (b d) -> p (a b) d", d=D),
                                       ALU.add))
                dve.nop().then_inc(S("moe_done"), 1)

            ln_dve(3, X, XN)
            moe_dve(0)
            ln_dve(4, X, XN)
            dve.wait_ge(S("q_ready"), 3)
            top_dve()
            ln_dve(5, X, XN)
            moe_dve(1)
            ln_dve(6, X, XN)
            dve.wait_ge(S("xn_ready"), 7)
            ln_dve(7, XN, XN2)
            dve.nop().then_inc(S("cmv_ready"), 1)
            dve.wait_ge(S("cstd_ready"), 1)
            link(dve.reciprocal(crs[:, :], crs[:, :]))
            dve.wait_ge(S("q3_ready"), NH)
            unit_dve(3)
            ln_dve(8, X, XN)
            dve.wait_ge(S("y_last"), 1)
            dve.tensor_tensor(X[:, :, :], X[:, :, :], PS[0:NQ, 0:2, :].rearrange("p a (b d) -> p (a b) d", d=D),
                              ALU.add).then_inc(S("x_final"), 1)


def kernel(**inputs):
    import numpy as _np
    import concourse.bacc as _bacc
    from concourse import mybir as _mybir
    from concourse.bass_utils import run_bass_kernel_spmd as _run

    nc = _bacc.Bacc("TRN2", target_bir_lowering=False, num_devices=1)
    arrays, args = {}, {}
    for name in inputs:
        a = _np.ascontiguousarray(inputs[name])
        if name == "L2_ffn_task_ids":
            continue
        arrays[f"in_{name}"] = a
        args[name] = nc.dram_tensor(f"in_{name}", a.shape, _mybir.dt.from_np(a.dtype), kind="ExternalInput").ap()
    scratch = nc.dram_tensor("ctx_transposed", (NB, D, NK), F32, kind="Internal").ap()
    out = nc.dram_tensor("out_0", (NB, NQ, D), F32, kind="ExternalOutput").ap()
    megakernel(nc, args, scratch, out)
    r = _run(nc, [arrays], core_ids=[0])
    return r.results[0]["out_0"]
```
